# Optimizing a Trainium2 kernel written in Bass

```python
import numpy as np
import jax
import jax.numpy as jnp

def _softmax(x, axis=-1):
    return jax.nn.softmax(x, axis=axis)

def _gelu(x):
    return jax.nn.gelu(x, approximate=True)

def _silu(x):
    return jax.nn.silu(x)

def _sigmoid(x):
    return jax.nn.sigmoid(x)

def _layernorm(x, axis=-1, eps=1e-05):
    m = jnp.mean(x, axis=axis, keepdims=True)
    v = jnp.var(x, axis=axis, keepdims=True)
    return (x - m) / jnp.sqrt(v + eps)

def _scatter_add(tgt, idx, src, axis=0):
    return tgt.at[idx].add(src)

def _segment_sum(src, seg, n):
    return jax.ops.segment_sum(src, seg, n)
kernel_name = 'mk_hybrid_d2_jaxref_r8_cf3d5a'

def setup_inputs(seed: int=0):
    np.random.seed(seed)
    _w = jnp.asarray

    def _L0_attn_a_setup():
        import math
        import jax, jax.numpy as jnp
        import numpy as np
        LN_EPS = 1e-05

        def _relative_sinusoidal(t, hd, dtype):
            pos = jnp.arange(-(t - 1), t, dtype=dtype)[:, None]
            div = jnp.exp(jnp.arange(0, hd, 2, dtype=dtype) * (-math.log(10000.0) / hd))
            pe = jnp.zeros((2 * t - 1, hd), dtype=dtype)
            pe = pe.at[:, 0::2].set(jnp.sin(pos * div))
            pe = pe.at[:, 1::2].set(jnp.cos(pos * div))
            return pe
        key = jax.random.key(seed)
        ks = jax.random.split(key, 4)
        b, t, dim, H = (2, 256, 128, 16)
        hd = dim // H
        s = 0.02
        return {'x': jax.random.normal(ks[0], (b, t, dim), jnp.float32), 'ln_g': jnp.ones((dim,), jnp.float32), 'ln_b': jnp.zeros((dim,), jnp.float32), 'w_qkv': jax.random.normal(ks[1], (dim, 3 * dim), jnp.float32) * s, 'b_qkv': jnp.zeros((3 * dim,), jnp.float32), 'w_rel': jax.random.normal(ks[2], (hd, H), jnp.float32) * s, 'w_out': jax.random.normal(ks[3], (dim, dim), jnp.float32) * s, 'b_out': jnp.zeros((dim,), jnp.float32)}
    _L0_attn_a_in = _L0_attn_a_setup()

    def _L0_attn_b_setup():
        import jax, jax.numpy as jnp
        import numpy as np
        DIM = 128
        HEADS = 16
        HEAD_DIM = DIM // HEADS
        DECAY = 0.95
        EPS = 1e-05

        def _decay_mask(S, dtype):
            idx = jnp.arange(S)
            diff = (idx[:, None] - idx[None, :]).astype(jnp.float32)
            mask = jnp.where(diff >= 0, jnp.exp(diff * np.log(DECAY)), 0.0)
            return mask.astype(dtype)
        key = jax.random.key(seed)
        ks = jax.random.split(key, 11)
        B, S, D = (2, 256, DIM)
        s = 1.0 / np.sqrt(D)
        inp = {'x': jax.random.normal(ks[0], (B, S, D), dtype=jnp.float32), 'Wq': jax.random.normal(ks[1], (D, D), dtype=jnp.float32) * s, 'bq': jnp.zeros((D,), jnp.float32), 'Wk': jax.random.normal(ks[2], (D, D), dtype=jnp.float32) * s, 'bk': jnp.zeros((D,), jnp.float32), 'Wv': jax.random.normal(ks[3], (D, D), dtype=jnp.float32) * s, 'bv': jnp.zeros((D,), jnp.float32), 'Wo': jax.random.normal(ks[4], (D, D), dtype=jnp.float32) * s, 'bo': jnp.zeros((D,), jnp.float32), 'gamma': jnp.ones((D,), jnp.float32), 'beta': jnp.zeros((D,), jnp.float32)}
        return inp
    _L0_attn_b_in = _L0_attn_b_setup()

    def _L0_ffn_setup():
        import jax, jax.numpy as jnp
        import numpy as np
        DIM = 128
        NUM_EXPERTS = 8
        HIDDEN = 512
        CAP_FACTOR = 2.0
        B, S = (4, 256)
        key = jax.random.key(seed)
        ks = jax.random.split(key, 6)
        scale_r = 1.0 / np.sqrt(DIM)
        scale_1 = 1.0 / np.sqrt(DIM)
        scale_2 = 1.0 / np.sqrt(HIDDEN)
        return {'x': jax.random.normal(ks[0], (B, S, DIM), dtype=jnp.float32), 'router_w': jax.random.uniform(ks[1], (NUM_EXPERTS, DIM), jnp.float32, -scale_r, scale_r), 'w1': jax.random.uniform(ks[2], (NUM_EXPERTS, DIM, HIDDEN), jnp.float32, -scale_1, scale_1), 'b1': jax.random.uniform(ks[3], (NUM_EXPERTS, HIDDEN), jnp.float32, -scale_1, scale_1), 'w2': jax.random.uniform(ks[4], (NUM_EXPERTS, HIDDEN, DIM), jnp.float32, -scale_2, scale_2), 'b2': jax.random.uniform(ks[5], (NUM_EXPERTS, DIM), jnp.float32, -scale_2, scale_2)}
    _L0_ffn_in = _L0_ffn_setup()

    def _L1_attn_a_setup():
        import jax, jax.numpy as jnp
        import numpy as np
        N_EMBD = 128
        N_HEAD = 16
        HEAD_DIM = N_EMBD // N_HEAD
        K_KEEP = 391
        RECENCY = 64
        key = jax.random.key(seed)
        k1, k2, k3 = jax.random.split(key, 3)
        B, T = (4, 128)
        x = jax.random.normal(k1, (B, T, N_EMBD), dtype=jnp.float32)
        W_attn = jax.random.normal(k2, (N_EMBD, 3 * N_EMBD), dtype=jnp.float32) * 0.02
        W_proj = jax.random.normal(k3, (N_EMBD, N_EMBD), dtype=jnp.float32) * 0.02
        return {'x': x, 'W_attn': W_attn, 'W_proj': W_proj}
    _L1_attn_a_in = _L1_attn_a_setup()

    def _L1_attn_b_setup():
        import jax, jax.numpy as jnp
        import numpy as np
        N_EMBD = 128
        N_HEAD = 16
        N_LAYER = 24
        LAYER_ID = 12
        B, T = (4, 512)
        Q = 64
        EPS = 1e-05 * 64

        def _static_params():
            C, H = (N_EMBD, N_HEAD)
            r01 = LAYER_ID / (N_LAYER - 1)
            r1a0 = 1.0 - LAYER_ID / N_LAYER
            ddd = np.arange(C, dtype=np.float64) / C
            maa_k = (1.0 - ddd ** r1a0).astype(np.float32).reshape(1, 1, C)
            maa_v = (1.0 - (ddd ** r1a0 + 0.3 * r01)).astype(np.float32).reshape(1, 1, C)
            maa_r = (1.0 - ddd ** (0.5 * r1a0)).astype(np.float32).reshape(1, 1, C)
            maa_g = maa_r.copy()
            h = np.arange(H, dtype=np.float64)
            decay = (-6.0 + 5.0 * (h / (H - 1)) ** (0.7 + 1.3 * r01)).astype(np.float32).reshape(H, 1)
            faaaa = (r01 * (1.0 - h / (H - 1))).astype(np.float32).reshape(H, 1)
            return (maa_k, maa_v, maa_r, maa_g, decay, faaaa)

        def _rwkv_forward(x, time_maa_k, time_maa_v, time_maa_r, time_maa_g, time_decay, time_faaaa, Wr, Wk, Wv, Wg, Wo, ln_w, ln_b):
            Bv, Tv, C = x.shape
            H = N_HEAD
            N = C // H
            nC = Tv // Q
            xx = jnp.pad(x, ((0, 0), (1, 0), (0, 0)))[:, :Tv] - x
            xk = x + xx * time_maa_k
            xv = x + xx * time_maa_v
            xr = x + xx * time_maa_r
            xg = x + xx * time_maa_g
            r = (xr @ Wr.T).reshape(Bv, Tv, H, N).transpose(0, 2, 1, 3)
            k = (xk @ Wk.T).reshape(Bv, Tv, H, N).transpose(0, 2, 3, 1)
            v = (xv @ Wv.T).reshape(Bv, Tv, H, N).transpose(0, 2, 1, 3)
            g = jax.nn.gelu(xg @ Wg.T, approximate=False)
            w = jnp.exp(-jnp.exp(time_decay))[:, 0]
            u = time_faaaa[:, 0]
            q = jnp.arange(Q)
            ws = (w ** Q).reshape(1, H, 1, 1)
            wk = (w[:, None] ** (Q - 1 - q)).reshape(1, H, 1, Q)
            wb = (w[:, None] ** q).reshape(1, H, Q, 1)
            i_idx = q[:, None]
            j_idx = q[None, :]
            e = jnp.maximum(i_idx - j_idx - 1, 0)
            Wmat = jnp.where(i_idx > j_idx, w[:, None, None] ** e, 0.0)
            Wmat = Wmat + jnp.eye(Q, dtype=x.dtype) * u[:, None, None]
            Wmat = Wmat.reshape(1, H, Q, Q)
            rr = r.reshape(Bv, H, nC, Q, N).transpose(2, 0, 1, 3, 4)
            kk = k.reshape(Bv, H, N, nC, Q).transpose(3, 0, 1, 2, 4)
            vv = v.reshape(Bv, H, nC, Q, N).transpose(2, 0, 1, 3, 4)

            def step(state, inp):
                rc, kc, vc = inp
                att = rc @ kc
                yc = att * Wmat @ vc + rc @ state * wb
                new_state = ws * state + kc * wk @ vc
                return (new_state, yc)
            state0 = jnp.zeros((Bv, H, N, N), dtype=x.dtype)
            _, ys = jax.lax.scan(step, state0, (rr, kk, vv))
            y = ys.transpose(1, 2, 0, 3, 4).reshape(Bv, H, Tv, N)
            y = y.transpose(0, 2, 1, 3)
            mean = y.mean(axis=-1, keepdims=True)
            var = y.var(axis=-1, keepdims=True)
            yn = (y - mean) / jnp.sqrt(var + EPS)
            yn = yn * ln_w.reshape(1, 1, H, N) + ln_b.reshape(1, 1, H, N)
            yn = yn.reshape(Bv, Tv, C)
            out = yn * g @ Wo.T
            return out
        key = jax.random.key(seed)
        ks = jax.random.split(key, 8)
        C = N_EMBD
        maa_k, maa_v, maa_r, maa_g, decay, faaaa = _static_params()
        std = 0.02
        return {'x': jax.random.normal(ks[0], (B, T, C), dtype=jnp.float32), 'time_maa_k': jnp.asarray(maa_k), 'time_maa_v': jnp.asarray(maa_v), 'time_maa_r': jnp.asarray(maa_r), 'time_maa_g': jnp.asarray(maa_g), 'time_decay': jnp.asarray(decay), 'time_faaaa': jnp.asarray(faaaa), 'Wr': jax.random.normal(ks[1], (C, C), dtype=jnp.float32) * std, 'Wk': jax.random.normal(ks[2], (C, C), dtype=jnp.float32) * std, 'Wv': jax.random.normal(ks[3], (C, C), dtype=jnp.float32) * std, 'Wg': jax.random.normal(ks[4], (C, C), dtype=jnp.float32) * std, 'Wo': jax.random.normal(ks[5], (C, C), dtype=jnp.float32) * std, 'ln_w': jnp.ones((C,), dtype=jnp.float32), 'ln_b': jnp.zeros((C,), dtype=jnp.float32)}
    _L1_attn_b_in = _L1_attn_b_setup()

    def _L1_ffn_setup():
        import jax, jax.numpy as jnp
        import numpy as np
        INT4_QMAX = 7.0

        def simulate_quantize_int4(w):
            scale = jnp.max(jnp.abs(w)) / INT4_QMAX
            q = jnp.clip(jnp.round(w / scale), -8.0, 7.0)
            return q * scale
        key = jax.random.key(seed)
        k_x, k_w, k_bias, k_a, k_b = jax.random.split(key, 5)
        d_in, features, rank = (128, 128, 16)
        x = jax.random.normal(k_x, (4, 1024, d_in), dtype=jnp.float32)
        kernel = jax.random.normal(k_w, (d_in, features), dtype=jnp.float32)
        bias = jax.random.normal(k_bias, (features,), dtype=jnp.float32)
        a = jax.random.normal(k_a, (d_in, rank), dtype=jnp.float32) * (1.0 / np.sqrt(d_in))
        b = jax.random.normal(k_b, (rank, features), dtype=jnp.float32) * 0.01
        return {'x': x, 'kernel': kernel, 'bias': bias, 'a': a, 'b': b}
    _L1_ffn_in = _L1_ffn_setup()
    _d = {'L0_attn_a_x': _L0_attn_a_in['x'], 'L0_attn_a_ln_g': _L0_attn_a_in['ln_g'], 'L0_attn_a_ln_b': _L0_attn_a_in['ln_b'], 'L0_attn_a_w_qkv': _L0_attn_a_in['w_qkv'], 'L0_attn_a_b_qkv': _L0_attn_a_in['b_qkv'], 'L0_attn_a_w_rel': _L0_attn_a_in['w_rel'], 'L0_attn_a_w_out': _L0_attn_a_in['w_out'], 'L0_attn_a_b_out': _L0_attn_a_in['b_out'], 'L0_attn_b_Wq': _L0_attn_b_in['Wq'], 'L0_attn_b_bq': _L0_attn_b_in['bq'], 'L0_attn_b_Wk': _L0_attn_b_in['Wk'], 'L0_attn_b_bk': _L0_attn_b_in['bk'], 'L0_attn_b_Wv': _L0_attn_b_in['Wv'], 'L0_attn_b_bv': _L0_attn_b_in['bv'], 'L0_attn_b_Wo': _L0_attn_b_in['Wo'], 'L0_attn_b_bo': _L0_attn_b_in['bo'], 'L0_attn_b_gamma': _L0_attn_b_in['gamma'], 'L0_attn_b_beta': _L0_attn_b_in['beta'], 'L0_ffn_router_w': _L0_ffn_in['router_w'], 'L0_ffn_w1': _L0_ffn_in['w1'], 'L0_ffn_b1': _L0_ffn_in['b1'], 'L0_ffn_w2': _L0_ffn_in['w2'], 'L0_ffn_b2': _L0_ffn_in['b2'], 'L1_attn_a_W_attn': _L1_attn_a_in['W_attn'], 'L1_attn_a_W_proj': _L1_attn_a_in['W_proj'], 'L1_attn_b_time_maa_k': _L1_attn_b_in['time_maa_k'], 'L1_attn_b_time_maa_v': _L1_attn_b_in['time_maa_v'], 'L1_attn_b_time_maa_r': _L1_attn_b_in['time_maa_r'], 'L1_attn_b_time_maa_g': _L1_attn_b_in['time_maa_g'], 'L1_attn_b_time_decay': _L1_attn_b_in['time_decay'], 'L1_attn_b_time_faaaa': _L1_attn_b_in['time_faaaa'], 'L1_attn_b_Wr': _L1_attn_b_in['Wr'], 'L1_attn_b_Wk': _L1_attn_b_in['Wk'], 'L1_attn_b_Wv': _L1_attn_b_in['Wv'], 'L1_attn_b_Wg': _L1_attn_b_in['Wg'], 'L1_attn_b_Wo': _L1_attn_b_in['Wo'], 'L1_attn_b_ln_w': _L1_attn_b_in['ln_w'], 'L1_attn_b_ln_b': _L1_attn_b_in['ln_b'], 'L1_ffn_kernel': _L1_ffn_in['kernel'], 'L1_ffn_bias': _L1_ffn_in['bias'], 'L1_ffn_a': _L1_ffn_in['a'], 'L1_ffn_b': _L1_ffn_in['b']}
    _x0 = _d['L0_attn_a_x']
    _d['L0_attn_a_x'] = jax.random.normal(jax.random.fold_in(jax.random.key(seed), 1), (4, 1024, 128), dtype=_x0.dtype)
    del _x0
    return _d

def reference(L0_attn_a_x, L0_attn_a_ln_g, L0_attn_a_ln_b, L0_attn_a_w_qkv, L0_attn_a_b_qkv, L0_attn_a_w_rel, L0_attn_a_w_out, L0_attn_a_b_out, L0_attn_b_Wq, L0_attn_b_bq, L0_attn_b_Wk, L0_attn_b_bk, L0_attn_b_Wv, L0_attn_b_bv, L0_attn_b_Wo, L0_attn_b_bo, L0_attn_b_gamma, L0_attn_b_beta, L0_ffn_router_w, L0_ffn_w1, L0_ffn_b1, L0_ffn_w2, L0_ffn_b2, L1_attn_a_W_attn, L1_attn_a_W_proj, L1_attn_b_time_maa_k, L1_attn_b_time_maa_v, L1_attn_b_time_maa_r, L1_attn_b_time_maa_g, L1_attn_b_time_decay, L1_attn_b_time_faaaa, L1_attn_b_Wr, L1_attn_b_Wk, L1_attn_b_Wv, L1_attn_b_Wg, L1_attn_b_Wo, L1_attn_b_ln_w, L1_attn_b_ln_b, L1_ffn_kernel, L1_ffn_bias, L1_ffn_a, L1_ffn_b):

    def _L0_attn_a_ref(x, ln_g, ln_b, w_qkv, b_qkv, w_rel, w_out, b_out):
        import math
        import jax, jax.numpy as jnp
        import numpy as np
        LN_EPS = 1e-05

        def _relative_sinusoidal(t, hd, dtype):
            pos = jnp.arange(-(t - 1), t, dtype=dtype)[:, None]
            div = jnp.exp(jnp.arange(0, hd, 2, dtype=dtype) * (-math.log(10000.0) / hd))
            pe = jnp.zeros((2 * t - 1, hd), dtype=dtype)
            pe = pe.at[:, 0::2].set(jnp.sin(pos * div))
            pe = pe.at[:, 1::2].set(jnp.cos(pos * div))
            return pe
        b, t, dim = x.shape
        hd, H = w_rel.shape
        scale = hd ** (-0.5)
        mu = jnp.mean(x, axis=-1, keepdims=True)
        var = jnp.mean(jnp.square(x - mu), axis=-1, keepdims=True)
        xn = (x - mu) * jax.lax.rsqrt(var + LN_EPS) * ln_g + ln_b
        qkv = (xn @ w_qkv + b_qkv).reshape(b, t, 3, H, hd)
        qkv = jnp.transpose(qkv, (2, 0, 3, 1, 4))
        q, k, v = (qkv[0], qkv[1], qkv[2])
        scores = jnp.einsum('bhqd,bhkd->bhqk', q, k) * scale
        rel_pe = _relative_sinusoidal(t, hd, scores.dtype)
        rel_bias = rel_pe @ w_rel
        idx = jnp.arange(t)[:, None] - jnp.arange(t)[None, :] + (t - 1)
        bias = jnp.transpose(rel_bias[idx], (2, 0, 1))[None]
        attn = jax.nn.softmax(scores + bias, axis=-1)
        out = jnp.einsum('bhqk,bhkd->bhqd', attn, v)
        out = jnp.transpose(out, (0, 2, 1, 3)).reshape(b, t, dim)
        return out @ w_out + b_out

    def _L0_attn_b_ref(x, Wq, bq, Wk, bk, Wv, bv, Wo, bo, gamma, beta):
        import jax, jax.numpy as jnp
        import numpy as np
        DIM = 128
        HEADS = 16
        HEAD_DIM = DIM // HEADS
        DECAY = 0.95
        EPS = 1e-05

        def _decay_mask(S, dtype):
            idx = jnp.arange(S)
            diff = (idx[:, None] - idx[None, :]).astype(jnp.float32)
            mask = jnp.where(diff >= 0, jnp.exp(diff * np.log(DECAY)), 0.0)
            return mask.astype(dtype)
        B, S, D = x.shape
        H, hd = (HEADS, HEAD_DIM)

        def split_heads(y):
            return y.reshape(B, S, H, hd).transpose(0, 2, 1, 3)
        q = split_heads(x @ Wq + bq)
        k = split_heads(x @ Wk + bk)
        v = split_heads(x @ Wv + bv)
        mask = _decay_mask(S, x.dtype)
        scores = jnp.einsum('bhid,bhjd->bhij', q, k) * mask
        out = jnp.einsum('bhij,bhjd->bhid', scores, v)
        out = out.transpose(0, 2, 1, 3).reshape(B, S, D)
        out = out @ Wo + bo
        y = out.transpose(0, 2, 1)
        yg = y.reshape(B, H, hd, S)
        mu = yg.mean(axis=(2, 3), keepdims=True)
        var = yg.var(axis=(2, 3), keepdims=True)
        yn = (yg - mu) / jnp.sqrt(var + EPS)
        yn = yn.reshape(B, D, S) * gamma[None, :, None] + beta[None, :, None]
        return yn.transpose(0, 2, 1)

    def _L0_ffn_ref(x, router_w, w1, b1, w2, b2):
        import jax, jax.numpy as jnp
        import numpy as np
        DIM = 128
        NUM_EXPERTS = 8
        HIDDEN = 512
        CAP_FACTOR = 2.0
        B, S = (4, 256)
        Bz, Sz, Dz = x.shape
        E = router_w.shape[0]
        capacity = max(1, int(Sz * CAP_FACTOR / E) + 1)
        scores = jax.nn.softmax(jnp.einsum('bsd,ed->bse', x, router_w), axis=-1)
        scores_t = jnp.swapaxes(scores, 1, 2)
        gate_vals, sel_idx = jax.lax.top_k(scores_t, capacity)
        b_idx = jnp.arange(Bz)[:, None, None]
        tokens = x[b_idx, sel_idx]
        h = jnp.einsum('becd,edh->bech', tokens, w1) + b1[None, :, None, :]
        h = jax.nn.gelu(h, approximate=False)
        y = jnp.einsum('bech,ehd->becd', h, w2) + b2[None, :, None, :]
        gated = y * gate_vals[..., None]
        out = jnp.zeros_like(x).at[b_idx, sel_idx].add(gated)
        return out

    def _L1_attn_a_ref(x, W_attn, W_proj):
        import jax, jax.numpy as jnp
        import numpy as np
        N_EMBD = 128
        N_HEAD = 16
        HEAD_DIM = N_EMBD // N_HEAD
        K_KEEP = 391
        RECENCY = 64
        B, T, C = x.shape
        qkv = x @ W_attn
        q, k, v = jnp.split(qkv, 3, axis=2)

        def heads(t):
            return t.reshape(B, T, N_HEAD, HEAD_DIM).transpose(0, 2, 1, 3)
        q, k, v = (heads(q), heads(k), heads(v))
        inv_sqrt_d = 1.0 / np.sqrt(HEAD_DIM)
        k_keep = min(K_KEEP, T)
        last = jnp.einsum('bhd,bhkd->bhk', q[:, :, -1, :], k) * inv_sqrt_d
        if RECENCY > 0 and T > RECENCY:
            big = jax.lax.stop_gradient(jnp.max(last)) + 1.0
            recent = jnp.arange(T) >= T - RECENCY
            last = jnp.where(recent[None, None, :], big, last)
        _, idx = jax.lax.top_k(last, k_keep)
        K_keep = jnp.take_along_axis(k, idx[..., None], axis=2)
        V_keep = jnp.take_along_axis(v, idx[..., None], axis=2)
        attn_scores = jnp.einsum('bhqd,bhkd->bhqk', q, K_keep) * inv_sqrt_d
        attn = jax.nn.softmax(attn_scores, axis=-1)
        out = jnp.einsum('bhqk,bhkd->bhqd', attn, V_keep)
        out = out.transpose(0, 2, 1, 3).reshape(B, T, C)
        return out @ W_proj

    def _L1_attn_b_ref(x, time_maa_k, time_maa_v, time_maa_r, time_maa_g, time_decay, time_faaaa, Wr, Wk, Wv, Wg, Wo, ln_w, ln_b):
        import jax, jax.numpy as jnp
        import numpy as np
        N_EMBD = 128
        N_HEAD = 16
        N_LAYER = 24
        LAYER_ID = 12
        B, T = (4, 512)
        Q = 64
        EPS = 1e-05 * 64

        def _static_params():
            C, H = (N_EMBD, N_HEAD)
            r01 = LAYER_ID / (N_LAYER - 1)
            r1a0 = 1.0 - LAYER_ID / N_LAYER
            ddd = np.arange(C, dtype=np.float64) / C
            maa_k = (1.0 - ddd ** r1a0).astype(np.float32).reshape(1, 1, C)
            maa_v = (1.0 - (ddd ** r1a0 + 0.3 * r01)).astype(np.float32).reshape(1, 1, C)
            maa_r = (1.0 - ddd ** (0.5 * r1a0)).astype(np.float32).reshape(1, 1, C)
            maa_g = maa_r.copy()
            h = np.arange(H, dtype=np.float64)
            decay = (-6.0 + 5.0 * (h / (H - 1)) ** (0.7 + 1.3 * r01)).astype(np.float32).reshape(H, 1)
            faaaa = (r01 * (1.0 - h / (H - 1))).astype(np.float32).reshape(H, 1)
            return (maa_k, maa_v, maa_r, maa_g, decay, faaaa)

        def _rwkv_forward(x, time_maa_k, time_maa_v, time_maa_r, time_maa_g, time_decay, time_faaaa, Wr, Wk, Wv, Wg, Wo, ln_w, ln_b):
            Bv, Tv, C = x.shape
            H = N_HEAD
            N = C // H
            nC = Tv // Q
            xx = jnp.pad(x, ((0, 0), (1, 0), (0, 0)))[:, :Tv] - x
            xk = x + xx * time_maa_k
            xv = x + xx * time_maa_v
            xr = x + xx * time_maa_r
            xg = x + xx * time_maa_g
            r = (xr @ Wr.T).reshape(Bv, Tv, H, N).transpose(0, 2, 1, 3)
            k = (xk @ Wk.T).reshape(Bv, Tv, H, N).transpose(0, 2, 3, 1)
            v = (xv @ Wv.T).reshape(Bv, Tv, H, N).transpose(0, 2, 1, 3)
            g = jax.nn.gelu(xg @ Wg.T, approximate=False)
            w = jnp.exp(-jnp.exp(time_decay))[:, 0]
            u = time_faaaa[:, 0]
            q = jnp.arange(Q)
            ws = (w ** Q).reshape(1, H, 1, 1)
            wk = (w[:, None] ** (Q - 1 - q)).reshape(1, H, 1, Q)
            wb = (w[:, None] ** q).reshape(1, H, Q, 1)
            i_idx = q[:, None]
            j_idx = q[None, :]
            e = jnp.maximum(i_idx - j_idx - 1, 0)
            Wmat = jnp.where(i_idx > j_idx, w[:, None, None] ** e, 0.0)
            Wmat = Wmat + jnp.eye(Q, dtype=x.dtype) * u[:, None, None]
            Wmat = Wmat.reshape(1, H, Q, Q)
            rr = r.reshape(Bv, H, nC, Q, N).transpose(2, 0, 1, 3, 4)
            kk = k.reshape(Bv, H, N, nC, Q).transpose(3, 0, 1, 2, 4)
            vv = v.reshape(Bv, H, nC, Q, N).transpose(2, 0, 1, 3, 4)

            def step(state, inp):
                rc, kc, vc = inp
                att = rc @ kc
                yc = att * Wmat @ vc + rc @ state * wb
                new_state = ws * state + kc * wk @ vc
                return (new_state, yc)
            state0 = jnp.zeros((Bv, H, N, N), dtype=x.dtype)
            _, ys = jax.lax.scan(step, state0, (rr, kk, vv))
            y = ys.transpose(1, 2, 0, 3, 4).reshape(Bv, H, Tv, N)
            y = y.transpose(0, 2, 1, 3)
            mean = y.mean(axis=-1, keepdims=True)
            var = y.var(axis=-1, keepdims=True)
            yn = (y - mean) / jnp.sqrt(var + EPS)
            yn = yn * ln_w.reshape(1, 1, H, N) + ln_b.reshape(1, 1, H, N)
            yn = yn.reshape(Bv, Tv, C)
            out = yn * g @ Wo.T
            return out
        return _rwkv_forward(x, time_maa_k, time_maa_v, time_maa_r, time_maa_g, time_decay, time_faaaa, Wr, Wk, Wv, Wg, Wo, ln_w, ln_b)

    def _L1_ffn_ref(x, kernel, bias, a, b):
        import jax, jax.numpy as jnp
        import numpy as np
        INT4_QMAX = 7.0

        def simulate_quantize_int4(w):
            scale = jnp.max(jnp.abs(w)) / INT4_QMAX
            q = jnp.clip(jnp.round(w / scale), -8.0, 7.0)
            return q * scale
        w = simulate_quantize_int4(kernel)
        y = jnp.einsum('bsd,df->bsf', x, w) + bias
        lora = jnp.einsum('bsr,rf->bsf', jnp.einsum('bsd,dr->bsr', x, a), b)
        return y + lora
    x = L0_attn_a_x
    x = x + _L0_attn_a_ref(_layernorm(x, axis=-1), L0_attn_a_ln_g, L0_attn_a_ln_b, L0_attn_a_w_qkv, L0_attn_a_b_qkv, L0_attn_a_w_rel, L0_attn_a_w_out, L0_attn_a_b_out)
    x = x + _L0_ffn_ref(_layernorm(x, axis=-1), L0_ffn_router_w, L0_ffn_w1, L0_ffn_b1, L0_ffn_w2, L0_ffn_b2)
    x = x + _L0_attn_b_ref(_layernorm(x, axis=-1), L0_attn_b_Wq, L0_attn_b_bq, L0_attn_b_Wk, L0_attn_b_bk, L0_attn_b_Wv, L0_attn_b_bv, L0_attn_b_Wo, L0_attn_b_bo, L0_attn_b_gamma, L0_attn_b_beta)
    x = x + _L0_ffn_ref(_layernorm(x, axis=-1), L0_ffn_router_w, L0_ffn_w1, L0_ffn_b1, L0_ffn_w2, L0_ffn_b2)
    x = x + _L1_attn_a_ref(_layernorm(x, axis=-1), L1_attn_a_W_attn, L1_attn_a_W_proj)
    x = x + _L1_ffn_ref(_layernorm(x, axis=-1), L1_ffn_kernel, L1_ffn_bias, L1_ffn_a, L1_ffn_b)
    x = x + _L1_attn_b_ref(_layernorm(x, axis=-1), L1_attn_b_time_maa_k, L1_attn_b_time_maa_v, L1_attn_b_time_maa_r, L1_attn_b_time_maa_g, L1_attn_b_time_decay, L1_attn_b_time_faaaa, L1_attn_b_Wr, L1_attn_b_Wk, L1_attn_b_Wv, L1_attn_b_Wg, L1_attn_b_Wo, L1_attn_b_ln_w, L1_attn_b_ln_b)
    x = x + _L1_ffn_ref(_layernorm(x, axis=-1), L1_ffn_kernel, L1_ffn_bias, L1_ffn_a, L1_ffn_b)
    return x

_drawn_inputs = setup_inputs


def setup_inputs(seed=0):
    import zlib

    import numpy as np

    out = dict(_drawn_inputs(seed))
    spreads = {'L0_attn_a_ln_g': (1.0, 0.6),
     'L0_attn_a_ln_b': (0.0, 0.8),
     'L0_attn_a_b_qkv': (0.0, 0.1),
     'L0_attn_a_b_out': (0.0, 0.1),
     'L0_attn_b_bq': (0.0, 0.1),
     'L0_attn_b_bk': (0.0, 0.1),
     'L0_attn_b_bv': (0.0, 0.1),
     'L0_attn_b_bo': (0.0, 0.8),
     'L0_attn_b_gamma': (1.0, 0.2),
     'L0_attn_b_beta': (0.0, 0.1),
     'L1_attn_b_ln_w': (1.0, 0.6),
     'L1_attn_b_ln_b': (0.0, 0.8)}
    factors = {'L0_attn_a_w_qkv': 8.0,
     'L0_attn_a_w_rel': 8.0,
     'L0_ffn_b1': 5.188,
     'L0_ffn_b2': 3.939,
     'L1_attn_a_W_attn': 8.0,
     'L1_attn_a_W_proj': 8.0,
     'L1_attn_b_time_maa_k': 8.0,
     'L1_attn_b_time_maa_v': 8.0,
     'L1_attn_b_time_maa_r': 8.0,
     'L1_attn_b_time_maa_g': 8.0,
     'L1_attn_b_time_decay': 64.0,
     'L1_attn_b_time_faaaa': 8.0,
     'L1_attn_b_Wr': 8.0,
     'L1_attn_b_Wk': 8.0,
     'L1_attn_b_Wv': 8.0,
     'L1_attn_b_Wg': 8.0,
     'L1_attn_b_Wo': 8.0,
     'L1_ffn_a': 8.0,
     'L1_ffn_b': 8.0}
    for name, (base, spread) in spreads.items():
        noise = np.random.default_rng([zlib.crc32(name.encode()), seed]).standard_normal(out[name].shape)
        drawn = base * np.exp(spread * noise) if base else spread * noise
        out[name] = jnp.asarray(drawn.astype(out[name].dtype))
    for name, factor in factors.items():
        out[name] = (out[name] * factor).astype(out[name].dtype)
    return out
```

```python
from contextlib import ExitStack

import numpy as np
import concourse.bass as bass
from concourse import mybir

P = 128
B, T, D = 4, 1024, 128
TILES = T // P
H, HD = 16, 8
HEADS = B * H
EXPERTS, HIDDEN = 8, 512
HK = HIDDEN // P
CAPACITY = int(T * 2.0 / EXPERTS) + 1
K_KEEP, RECENCY = 391, 64
LN_EPS = 1e-5
RWKV_EPS = 1e-5 * 64
DECAY = 0.95
QSCALE = HD ** -0.5
SPLITS = 6
PART_Q = [0, 0, 1, 1, 0, 2]
PART_K = [0, 1, 0, 1, 2, 0]
SHIFT_ROWS = 2
TAKEN = -3.0e38
MASKED = -1.0e20

ALU = mybir.AluOpType
ACT = mybir.ActivationFunctionType
AX = mybir.AxisListType
F32 = mybir.dt.float32
BF16 = mybir.dt.bfloat16
ds = bass.ds


class Chain:

    def __init__(self, eng, sem):
        self.eng, self.sem, self.base, self.n = eng, sem, 0, 0

    def start(self, base):
        self.base, self.n = base, 0

    def __call__(self, ins, alone=False):
        self.n += 1
        ins.then_inc(self.sem, 1)
        (wait_alone if alone else type(self.eng).wait_ge)(self.eng, self.sem, self.base + self.n)


def wait_alone(eng, sem, value):
    eng.wait_ge(sem, value)
    if not isinstance(value, int):
        eng.sem_inc(Passed.sem, 1)


class Passed:

    sem = None


class Stage:

    def __init__(self, nc, name):
        self.nc, self.name, self.stack, self.sems = nc, name, ExitStack(), []

    def sb(self, name, shape, dt=F32):
        return self.stack.enter_context(self.nc.sbuf_tensor(f"{self.name}_{name}", shape, dt))

    def ps(self, name, shape, dt=F32):
        return self.stack.enter_context(self.nc.psum_tensor(f"{self.name}_{name}", shape, dt))

    def sem(self, name):
        self.sems.append(self.nc.alloc_semaphore(f"{self.name}_{name}"))
        return self.sems[-1]

    def __enter__(self):
        return self

    def __exit__(self, *a):
        with self.nc.Block() as block:
            @block.gpsimd
            def _(pool):
                for sem in self.sems:
                    pool.sem_clear(sem)
        for sem in self.sems:
            self.nc.release_semaphore(sem)
        self.stack.close()


def batch(x, s):
    return x[:, ds(s * T, T)].rearrange("p (j d) -> p j d", d=D)


class Norm:

    def __init__(self, st, env, again=False, affine=None, pad=0):
        self.env, self.again, self.affine, self.pad = env, again, affine, pad
        self.stats = st.sb("ln_stats", [P, 2, TILES, 6])
        self.mv = st.sb("ln_mv", [P, 2, TILES, 2])
        self.ve = st.sb("ln_ve", [P, 2, TILES])
        self.rstd = st.sb("ln_rstd", [P, 2, TILES])
        self.mv2 = st.sb("ln_mv2", [P, 2, TILES, 2])
        self.ve2 = st.sb("ln_ve2", [P, 2, TILES])
        self.rstd2 = st.sb("ln_rstd2", [P, 2, TILES])
        self.y = st.sb("ln_y", [P, 2, TILES, D])
        self.xT = st.sb("ln_xT", [P, 2, T + pad])
        self.psT = st.ps("ln_psT", [P, T])
        self.dve = st.sem("ln_dve")
        self.pool = st.sem("ln_pool")
        self.var_ready = st.sem("ln_var_ready")
        self.rstd_ready = st.sem("ln_rstd_ready")
        self.y_ready = st.sem("ln_y_ready")
        self.y_free = st.sem("ln_y_free")
        self.t_ready = st.sem("ln_t_ready")
        self.xt_ready = st.sem("ln_xt_ready")
        self.xt_free = st.sem("ln_xt_free")
        self.per = 3 if again else 1

    def credits(self, vector):
        vector.sem_inc(self.y_free, 2)
        vector.sem_inc(self.xt_free, 2)

    def vector(self, v, s, u, saved=None):
        rounds = 2 if self.again else 1
        ch = Chain(v, self.dve)
        ch.start(s * self.per)
        v.wait_ge(self.y_free, s + 1)
        if saved is not None:
            v.wait_ge(saved, s + 1)
        xb = batch(self.env.X, s)
        y = self.y[:, u]
        for r in range(rounds):
            src, mv, rs = (xb, self.mv, self.rstd) if r == 0 else (y, self.mv2, self.rstd2)
            for j in range(TILES):
                ins = v.bn_stats(self.stats[:, u, j, :], src[:, j, :])
            ch(ins, alone=True)
            for j in range(TILES):
                ins = v.bn_aggr(mv[:, u, j, :], self.stats[:, u, j, :])
            ins.then_inc(self.var_ready, 1)
            v.wait_ge(self.rstd_ready, s * rounds + r + 1)
            v.wait_ge(self.var_ready, s * rounds + r + 1)
            for j in range(TILES):
                ins = v.tensor_scalar(y[:, j, :], src[:, j, :], mv[:, u, j, 0:1], rs[:, u, j:j + 1],
                                      ALU.subtract, ALU.mult)
            if r + 1 < rounds:
                ch(ins)
        ins.then_inc(self.y_ready, 1)

    def gpsimd(self, g, s, u):
        rounds = 2 if self.again else 1
        ch = Chain(g, self.pool)
        ch.start(s * rounds)
        for r in range(rounds):
            mv, ve, rs = (self.mv, self.ve, self.rstd) if r == 0 else (self.mv2, self.ve2, self.rstd2)
            wait_alone(g, self.var_ready, s * rounds + r + 1)
            ch(g.tensor_scalar(ve[:, u, :], mv[:, u, :, 1], LN_EPS, None, ALU.add))
            g.tensor_tensor(rs[:, u, :], ve[:, u, :], self.env.minus_half[:, 0:TILES],
                            ALU.pow).then_inc(self.rstd_ready, 1)

    def tensor(self, t, s, u, psT_free=None):
        t.wait_ge(self.y_ready, s + 1)
        if psT_free is None:
            t.wait_ge(self.xt_ready, s)
        else:
            t.wait_ge(psT_free, s)
        for j in range(TILES):
            ins = t.transpose(self.psT[:, j * P:(j + 1) * P], self.y[:, u, j, :], self.env.ident[:])
        ins.then_inc(self.t_ready, 1)

    def scalar(self, a, s, u):
        a.wait_ge(self.t_ready, s + 1)
        a.wait_ge(self.xt_free, s + 1)
        a.sem_inc(self.y_free, 1)
        out = self.xT[:, u, self.pad:self.pad + T]
        if self.affine is None:
            a.activation(out, self.psT[:], ACT.Copy).then_inc(self.xt_ready, 1)
        else:
            gain, offset = self.affine
            a.activation(out, self.psT[:], ACT.Identity, bias=offset, scale=gain).then_inc(self.xt_ready, 1)


def loop_batches(eng, body):
    with eng.Fori(0, B // 2) as i:
        for u in range(2):
            body(i * 2 + u, u)


def load(eng, sem, pairs):
    for dst, src in pairs:
        eng.dma_start(dst, src).then_inc(sem, 16)
    return 16 * len(pairs)


def column(v):
    return v.rearrange("(p o) -> p o", o=1)


def add_projected(nc, env, st, src, w, bias):
    a = st.sb("po_in", [P, 2, T])
    aT = st.sb("po_inT", [P, 2, T])
    psT = st.ps("po_psT", [P, T])
    psY = st.ps("po_psY", [P, T])
    in_ready, in_free = st.sem("po_in_ready"), st.sem("po_in_free")
    t_ready, t_done, y_ready, y_free = (st.sem(f"po_{n}") for n in ("t_ready", "t_done", "y_ready", "y_free"))
    bias_done, bias_own = st.sem("po_bias_done"), st.sem("po_own")
    with nc.Block() as block:
        @block.scalar
        def _(act):
            act.sem_inc(in_free, 2)

            def body(s, u):
                act.wait_ge(in_free, s + 1)
                act.activation(a[:, u, :].rearrange(src.form, **src.sizes), src(s), ACT.Copy).then_inc(in_ready, 1)
                act.wait_ge(t_ready, s + 1)
                act.sem_inc(in_free, 1)
                act.activation(aT[:, u, :], psT[:], ACT.Copy).then_inc(t_done, 1)
            loop_batches(act, body)

        @block.gpsimd
        def _(pool):
            if bias is not None:
                def body(s, u):
                    xb = batch(env.X, s)
                    pool.tensor_tensor(xb, xb, bias[:].unsqueeze(1).broadcast_to([P, TILES, D]),
                                       ALU.add).then_inc(bias_done, 1)
                loop_batches(pool, body)

        @block.tensor
        def _(pe):
            def body(s, u):
                pe.wait_ge(in_ready, s + 1)
                pe.wait_ge(t_done, s)
                for j in range(TILES):
                    ins = pe.transpose(psT[:, j * P:(j + 1) * P], a[:, u, j * P:(j + 1) * P], env.ident[:])
                ins.then_inc(t_ready, 1)
                pe.wait_ge(t_done, s + 1)
                pe.wait_ge(y_free, s)
                for j in range(TILES):
                    ins = pe.matmul(psY[:, j * P:(j + 1) * P], aT[:, u, j * P:(j + 1) * P], w[:],
                                    start=True, stop=True)
                ins.then_inc(y_ready, 1)
            loop_batches(pe, body)

        @block.vector
        def _(dve):
            def body(s, u):
                dve.wait_ge(y_ready, s + 1)
                if bias is not None:
                    dve.wait_ge(bias_done, s + 1)
                xb = batch(env.X, s)
                dve.tensor_tensor(xb, psY[:].rearrange("p (j d) -> p j d", d=D), xb, ALU.add).then_inc(y_free, 1)
            loop_batches(dve, body)


class Source:
    def __init__(self, f, form, **sizes):
        self.f, self.form, self.sizes = f, form, sizes

    def __call__(self, s):
        return self.f(s)


def qkv_stage(nc, env, st, QS, KS, VTOK, w_qkv, biases, again, affine, LASTD=None):
    nm = Norm(st, env, again=again, affine=affine)
    full = st.sb("full", [P, 2, T])
    rest = st.sb("rest", [P, 2, T])
    part = st.sb("part", [P, 2, 3, T], BF16)
    psQK = st.ps("psQK", [P, 2, T])
    psV = st.ps("psV", [P, T])
    own = st.sem("own")
    qk_ready, qk_taken = st.sem("qk_ready"), st.sem("qk_taken")
    high_ready, rest_ready, mid_ready, low_ready = (st.sem(n) for n in ("high_ready", "rest_ready", "mid_ready", "low_ready"))
    stored = [st.sem("stored_q"), st.sem("stored_k")]
    v_ready, v_taken = st.sem("v_ready"), st.sem("v_taken")
    if LASTD is not None:
        ql = st.sb("ql", [P, H])
        last_sb = st.sb("last_sb", [H, 2, T])
        ql_ready, last_ready, last_taken, last_stored = (st.sem(n) for n in ("ql_ready", "last_ready", "last_taken", "last_stored"))
        last_free = st.sem("last_free")
    with nc.Block() as block:
        @block.vector
        def _(dve):
            nm.credits(dve)

            def body(s, u):
                nm.vector(dve, s, u)
                for c in range(2):
                    dve.wait_ge(qk_ready, s * 2 + c + 1)
                    dve.wait_ge(low_ready, s * 2)
                    mul = QSCALE if c == 0 else 1.0
                    if biases is not None:
                        ins = dve.tensor_scalar(full[:, c, :], psQK[:, c, :], biases[c], mul, ALU.add, ALU.mult)
                    else:
                        ins = dve.tensor_scalar(full[:, c, :], psQK[:, c, :], mul, None, ALU.mult)
                    ins.then_inc(qk_taken, 1)
                if LASTD is not None:
                    dve.wait_ge(qk_taken, s * 2 + 2)
                    dve.wait_ge(last_ready, s)
                    dve.tensor_scalar(ql[:], env.blk[:], full[:, 0, T - 1:T], None, ALU.mult).then_inc(ql_ready, 1)
                for c in range(2):
                    dve.wait_ge(high_ready, s * 2 + c + 1)
                    dve.wait_ge(qk_taken, s * 2 + c + 1)
                    dve.tensor_tensor(rest[:, c, :], full[:, c, :], part[:, c, 0, :],
                                      ALU.subtract).then_inc(rest_ready, 1)
                for c in range(2):
                    dve.wait_ge(mid_ready, s * 2 + c + 1)
                    dve.wait_ge(rest_ready, s * 2 + c + 1)
                    dve.wait_ge(stored[c], s * 16 * SPLITS)
                    dve.tensor_tensor(part[:, c, 2, :], rest[:, c, :], part[:, c, 1, :],
                                      ALU.subtract).then_inc(low_ready, 1)
                dve.wait_ge(v_ready, s + 1)
                out = VTOK[:, ds(s * H, H), :, 0:HD].rearrange("p h j d -> p j h d")
                src = psV[:].rearrange("p (j h d) -> p j h d", j=TILES, h=H)
                if biases is not None:
                    for j in range(TILES):
                        ins = dve.tensor_tensor(out[:, j], src[:, j], biases[2].rearrange("p (h d) -> p h d", h=H), ALU.add)
                else:
                    ins = dve.tensor_copy(out, src)
                ins.then_inc(v_taken, 1)
            loop_batches(dve, body)

        @block.gpsimd
        def _(pool):
            pool.memset(VTOK[:, :, :, HD:HD + 1], 1.0).then_inc(own, 1)
            loop_batches(pool, lambda s, u: nm.gpsimd(pool, s, u))
            pool.wait_ge(own, 1)

        @block.tensor
        def _(pe):
            def body(s, u):
                nm.tensor(pe, s, u, psT_free=last_taken if LASTD is not None else None)
                pe.wait_ge(nm.xt_ready, s + 1)
                for c in range(2):
                    pe.wait_ge(qk_taken, s * 2)
                    for n in range(2):
                        ins = pe.matmul(psQK[:, c, n * 512:(n + 1) * 512], w_qkv[:, c * D:(c + 1) * D],
                                        nm.xT[:, u, n * 512:(n + 1) * 512], start=True, stop=True)
                    ins.then_inc(qk_ready, 1)
                pe.wait_ge(v_taken, s)
                for j in range(TILES):
                    ins = pe.matmul(psV[:, j * D:(j + 1) * D], nm.xT[:, u, j * P:(j + 1) * P],
                                    w_qkv[:, 2 * D:3 * D], start=True, stop=True)
                ins.then_inc(v_ready, 1)
                if LASTD is not None:
                    pe.wait_ge(ql_ready, s + 1)
                    for n in range(2):
                        ins = pe.matmul(nm.psT[0:H, n * 512:(n + 1) * 512], ql[:], full[:, 1, n * 512:(n + 1) * 512],
                                        start=True, stop=True)
                    ins.then_inc(last_ready, 1)
            loop_batches(pe, body)

        @block.scalar
        def _(act):
            if LASTD is not None:
                act.sem_inc(last_free, 2)

            def body(s, u):
                nm.scalar(act, s, u)
                for c in range(2):
                    act.wait_ge(qk_taken, s * 2 + c + 1)
                    act.wait_ge(stored[c], s * 16 * SPLITS)
                    act.activation(part[:, c, 0, :], full[:, c, :], ACT.Copy).then_inc(high_ready, 1)
                for c in range(2):
                    act.wait_ge(rest_ready, s * 2 + c + 1)
                    act.activation(part[:, c, 1, :], rest[:, c, :], ACT.Copy).then_inc(mid_ready, 1)
                act.wait_ge(v_ready, s + 1)
                act.sem_inc(nm.xt_free, 1)
                if LASTD is not None:
                    act.wait_ge(last_ready, s + 1)
                    act.wait_ge(last_free, s + 1)
                    act.activation(last_sb[:, u, :], nm.psT[0:H, :], ACT.Copy).then_inc(last_taken, 1)
            loop_batches(act, body)

        @block.sync
        def _(sp):
            def body(s, u):
                for c, (dst, parts) in enumerate(((QS, PART_Q), (KS, PART_K))):
                    wait_alone(sp, low_ready, s * 2 + c + 1)
                    for n, p in enumerate(parts):
                        out = dst[ds(s, 1), :, n, :, :].rearrange("b h d t -> (b h) d t")
                        sp.dma_start(out, part[:, c, p, :]).then_inc(stored[c], 16)
                if LASTD is not None:
                    wait_alone(sp, last_taken, s + 1)
                    sp.dma_start(LASTD[ds(s, 1), :, :].rearrange("b h t -> (b h) t"),
                                 last_sb[:, u, :]).then_inc(last_stored, 16)
                for sem in stored:
                    wait_alone(sp, sem, s * 16 * SPLITS + 16 * SPLITS)
                if LASTD is not None:
                    wait_alone(sp, last_stored, s * 16 + 16)
                    sp.sem_inc(last_free, 1)
            loop_batches(sp, body)


def attention(nc, env, st, QS, KS, VTOK, ATT, rows, setup_k, mask_rows=None):
    SLOTS = 4
    full = rows + SHIFT_ROWS
    qt = st.sb("qt", [P, SLOTS, T], BF16)
    kt = st.sb("kt", [P, SLOTS, T], BF16)
    e = st.sb("e", [P, 2 * TILES, 512])
    vh = st.sb("vh", [P, 2, TILES, 32])
    partial = st.sb("partial", [P, 2, TILES])
    m2 = st.sb("m2", [P, 2, 2 * TILES], BF16)
    mrow = st.sb("mrow", [2 * TILES, 2, P], BF16)
    ot = st.sb("ot", [P, 2, 512])
    rden = st.sb("rden", [P, 2, TILES])
    psA = st.ps("psA", [P, 2, T])
    psS = st.ps("psS", [P, 3, 512])
    psO = st.ps("psO", [P, 512])
    AHEAD = 2 * TILES + 1
    PER = TILES + 1
    TURN = 2
    k_rows = KS.shape[2] * KS.shape[3]
    q_rows = QS.shape[2] * QS.shape[3]
    loads = 2 + (mask_rows is not None)
    loaded = [st.sem(f"loaded{k}") for k in range(SLOTS)]
    shifted = [st.sem(f"shifted{k}") for k in range(SLOTS)]
    head_free = st.sem("head_free")
    a_ready, a_taken = st.sem("a_ready"), st.sem("a_taken")
    m2_ready, mrow_ready = st.sem("m2_ready"), st.sem("mrow_ready")
    s_ready, e_ready = st.sem("s_ready"), st.sem("e_ready")
    av_done, ot_ready, tok_ready, norm_done = (st.sem(n) for n in ("av_done", "ot_ready", "tok_ready", "norm_done"))
    vh_ready, own_d, own_p = st.sem("vh_ready"), st.sem("own_d"), st.sem("own_p")
    filled = st.sem("filled")
    qsrc = QS.rearrange("b h s d t -> (b h) (s d) t")
    ksrc = KS.rearrange("b h s d t -> (b h) (s d) t")
    TURNS = HEADS // SLOTS

    def at(i, u, delta):
        return (u + delta) % SLOTS, i + (u + delta) // SLOTS

    def turns(eng, body):
        body(0, True, False)
        with eng.Fori(1, TURNS - 1) as i:
            body(i, False, False)
        body(TURNS - 1, False, True)

    with nc.Block() as block:
        @block.sync
        def _(sp):
            sp.wait_ge(filled, 2)
            n_fixed = 0
            for k in range(SLOTS):
                if setup_k is not None:
                    sp.dma_start(kt[k_rows:rows, k, :], setup_k).then_inc(filled, 16)
                    n_fixed += 1
            sp.wait_ge(filled, 2 + 16 * n_fixed)

            def fetch(i, u, wait):
                n = i * SLOTS + u
                if wait:
                    wait_alone(sp, head_free, n - SLOTS + 1)
                sp.dma_start(qt[0:q_rows, u, :], qsrc[ds(n, 1)].rearrange("a r t -> (a r) t")).then_inc(loaded[u], 16)
                sp.dma_start(kt[0:k_rows, u, :], ksrc[ds(n, 1)].rearrange("a r t -> (a r) t")).then_inc(loaded[u], 16)
                if mask_rows is not None:
                    sp.dma_start(kt[rows - 1:rows, u, :], mask_rows[ds(n, 1), :]).then_inc(loaded[u], 16)

            fetch(0, 0, False)

            def body(i, first, last):
                for u in range(SLOTS):
                    if not (last and u == SLOTS - 1):
                        u1, i1 = at(i, u, 1)
                        fetch(i1, u1, not (first and u + 1 < SLOTS))
                    wait_alone(sp, mrow_ready, i * SLOTS + u + 1)
                    for r in range(SHIFT_ROWS):
                        sp.dma_start(qt[rows + r:rows + r + 1, u, :].rearrange("o (a t) -> o a t", a=TILES),
                                     mrow[r * TILES:(r + 1) * TILES, u % 2, :]).then_inc(shifted[u], 16)
            turns(sp, body)

        @block.gpsimd
        def _(pool):
            pool.memset(vh[:], 0.0).then_inc(own_p, 1)
            pool.wait_ge(own_p, 1)

            def fill(n, par, wait):
                if wait:
                    pool.wait_ge(av_done, n * 4 - 4)
                pool.tensor_copy(vh[:, par, :, 0:HD + 1],
                                 VTOK[:, ds(n, 1), :, :].rearrange("p n j d -> p (n j) d")).then_inc(vh_ready, 1)
            fill(0, 0, False)
            fill(1, 1, False)
            with pool.Fori(1, HEADS // 2) as i:
                for par in range(2):
                    fill(i * 2 + par, par, True)

        @block.tensor
        def _(pe):
            pe.wait_ge(filled, 2 + (16 * SLOTS if setup_k is not None else 0))

            def psA_free(use):
                if not (isinstance(use, int) and use < 2):
                    pe.wait_ge(a_taken, use - 1)

            def first_pass(i, u, j, use, slot):
                if j == 0:
                    pe.wait_ge(loaded[u], (i + 1) * 16 * loads)
                psA_free(use)
                for c in range(2):
                    ins = pe.matmul(psA[:, slot, c * 512:(c + 1) * 512], qt[0:rows, u, j * P:(j + 1) * P],
                                    kt[0:rows, u, c * 512:(c + 1) * 512], start=True, stop=True)
                ins.then_inc(a_ready, 1)

            def turn_max(n, par, use, slot):
                pe.wait_ge(m2_ready, n + 1)
                psA_free(use)
                pe.transpose(psA[0:2 * TILES, slot, 0:P // 2].bitcast(BF16), m2[:, par, :], env.identb[:]).then_inc(a_ready, 1)

            def second_pass(i, u, c):
                k = i * SLOTS + u
                if c == 0:
                    pe.wait_ge(shifted[u], (i + 1) * 16 * SHIFT_ROWS)
                turn = 16 * u + c
                if turn == 0:
                    if not isinstance(k, int) or k > 0:
                        pe.wait_ge(e_ready, k * 16)
                elif not isinstance(k, int) or k * 16 + c > 2:
                    pe.wait_ge(e_ready, k * 16 + c - 2)
                j, q = c // 2, c % 2
                ins = pe.matmul(psS[:, turn % 3, :], kt[0:full, u, j * P:(j + 1) * P],
                                qt[0:full, u, q * 512:(q + 1) * 512], start=True, stop=True)
                ins.then_inc(s_ready, 1)

            def sums(k, par, part):
                pe.wait_ge(e_ready, k * 16 + 4 * part + 4)
                if part == 0:
                    pe.wait_ge(vh_ready, k + 1)
                for j in range(part * 2, part * 2 + 2):
                    for q in range(2):
                        g = 2 * (j % 2) + q
                        ins = pe.matmul(psO[32 * g:32 * g + 32, :], vh[:, par, j, :], e[:, 2 * j + q, :],
                                        start=(j < 2), stop=(j >= 6))
                ins.then_inc(av_done, 1)

            def to_tokens(k, par):
                pe.wait_ge(ot_ready, k + 1)
                for j in range(TILES // 2):
                    ins = pe.matmul(psO[:, j * 32:j * 32 + 2 * (HD + 1)], ot[:, par, j * P:(j + 1) * P],
                                    env.sel[:], start=True, stop=True)
                ins.then_inc(tok_ready, 1)

            for j in range(TILES):
                first_pass(0, 0, j, j, j % 2)
            turn_max(0, 0, TILES, TILES % 2)
            for j in range(TILES):
                first_pass(0, 1, j, TILES + 1 + j, (TILES + 1 + j) % 2)

            def body(i, first, last):
                for u in range(SLOTS):
                    k = i * SLOTS + u
                    u2, i2 = at(i, u, 2)
                    use, slot = k * PER + AHEAD, (u * PER + AHEAD) % 2
                    if last and u == 2:
                        turn_max(k + 1, (u + 1) % 2, use, slot)
                    for c in range(16):
                        second_pass(i, u, c)
                        if c == 15:
                            pe.wait_ge(s_ready, k * 16 + 16)
                            pe.sem_inc(head_free, 1)
                        if c in (2, 4) and not (first and u == 0):
                            sums(k - 1, (u - 1) % 2, 2 + (c == 4))
                        if c == 7 and not (first and u == 0):
                            to_tokens(k - 1, (u - 1) % 2)
                        if c in (11, 13):
                            if c == 11 and not (first and u == 0):
                                pe.wait_ge(norm_done, k)
                            sums(k, u % 2, int(c == 13))
                        if c % 2 == 1 and not (last and u >= 2):
                            j = c // 2
                            first_pass(i2, u2, j, use + j + (j > TURN), (slot + j + (j > TURN)) % 2)
                            if j == TURN:
                                turn_max(k + 1, (u + 1) % 2, use + j + 1, (slot + j + 1) % 2)
            turns(pe, body)
            sums(HEADS - 1, 1, 2)
            sums(HEADS - 1, 1, 3)
            to_tokens(HEADS - 1, 1)

        @block.vector
        def _(dve):
            def maxima(par, j, use, slot):
                dve.wait_ge(a_ready, use + 1)
                dve.tensor_reduce(partial[:, par, j:j + 1], psA[:, slot, :], AX.X, ALU.max,
                                  negate=True).then_inc(a_taken, 1)

            def shift_parts(n, par, last_use):
                dve.wait_ge(a_taken, last_use + 1)
                dve.tensor_copy(m2[:, par, 0:TILES], partial[:, par, :]).then_inc(own_d, 1)
                dve.wait_ge(own_d, n + 1)
                dve.tensor_tensor(m2[:, par, TILES:2 * TILES], partial[:, par, :], m2[:, par, 0:TILES],
                                  ALU.subtract).then_inc(m2_ready, 1)

            def shift_row(i, u, wait, use, slot):
                dve.wait_ge(a_ready, use + 1)
                if wait:
                    u0, i0 = at(i, u, -2)
                    dve.wait_ge(shifted[u0], (i0 + 1) * 16 * SHIFT_ROWS)
                dve.tensor_copy(mrow[:, u % 2, :], psA[0:2 * TILES, slot, 0:P // 2].bitcast(BF16)).then_inc(a_taken, 1)
                dve.wait_ge(a_taken, use + 1)
                dve.sem_inc(mrow_ready, 1)

            recip_done = env.recip_sem[st.name]

            def normalise(k, par):
                tok = psO[:, 0:32 * (TILES // 2)].rearrange("p (j x) -> p j x", x=32)[:, :, 0:2 * (HD + 1)].rearrange(
                    "p j (q d) -> p j q d", q=2)
                rd = rden[:, par, :].rearrange("p (j q) -> p j q", q=2)
                dve.wait_ge(tok_ready, k + 1)
                dve.reciprocal(rd, tok[:, :, :, HD]).then_inc(recip_done, 1)
                dve.wait_ge(recip_done, k + 1)
                out = ATT[:, ds(k, 1), :, :].rearrange("p n (q j) d -> p (n j) q d", q=2)
                for q in range(2):
                    ins = dve.tensor_tensor(out[:, :, q], tok[:, :, q, 0:HD],
                                            rd[:, :, q].unsqueeze(2).broadcast_to([P, TILES // 2, HD]), ALU.mult)
                ins.then_inc(norm_done, 1)

            for x in (qt, kt):
                dve.memset(x[0:96], 0.0)
                dve.memset(x[96:P], 1.0).then_inc(filled, 1)
            for j in range(TILES):
                maxima(0, j, j, j % 2)
            shift_parts(0, 0, TILES - 1)
            shift_row(0, 0, False, TILES, TILES % 2)
            for j in range(TILES):
                maxima(1, j, TILES + 1 + j, (TILES + 1 + j) % 2)
            shift_parts(1, 1, 2 * TILES)

            def body(i, first, last):
                for u in range(SLOTS):
                    k = i * SLOTS + u
                    use, slot = k * PER + AHEAD, (u * PER + AHEAD) % 2
                    u1, i1 = at(i, u, 1)
                    if last and u == 2:
                        shift_row(i1, u1, True, use, slot)
                    for j in range(TILES):
                        if not (last and u >= 2):
                            maxima(u % 2, j, use + j + (j > TURN), (slot + j + (j > TURN)) % 2)
                            if j == TURN:
                                shift_row(i1, u1, not (first and u == 0), use + j + 1, (slot + j + 1) % 2)
                        if j == TURN and not (first and u == 0):
                            normalise(k - 1, (u - 1) % 2)
                    if not (last and u >= 2):
                        shift_parts(k + 2, u % 2, use + TILES)
            turns(dve, body)
            normalise(HEADS - 1, 1)

        @block.scalar
        def _(act):
            def exps(k, u, c):
                act.wait_ge(s_ready, k * 16 + c + 1)
                if c % 4 == 0 and not (isinstance(k, int) and k == 0):
                    act.wait_ge(av_done, k * 4 - 3 + c // 4)
                act.activation(e[:, c, :], psS[:, (16 * u + c) % 3, :], ACT.Exp).then_inc(e_ready, 1)

            def take_sums(k, par, wait):
                act.wait_ge(av_done, k * 4 + 4)
                if wait:
                    act.wait_ge(tok_ready, k - 1)
                act.activation(ot[:, par, :], psO[:], ACT.Copy).then_inc(ot_ready, 1)

            def body(i, first, last):
                for u in range(SLOTS):
                    k = i * SLOTS + u
                    for c in range(16):
                        exps(k, u, c)
                        if c == 4 and not (first and u == 0):
                            take_sums(k - 1, (u - 1) % 2, not (first and u < 3))
            turns(act, body)
            take_sums(HEADS - 1, 1, True)





def constants():
    c = {}
    c["ident"] = np.eye(P, dtype=np.float32)
    p = np.arange(P)
    c["blk"] = (p[:, None] // HD == np.arange(H)[None, :]).astype(np.float32)
    c["blk2"] = (p[:, None] // HD == p[None, :] // HD).astype(np.float32)
    col = np.arange(2 * (HD + 1))[None, :]
    c["sel"] = ((p[:, None] % 32 == col % (HD + 1)) & (p[:, None] // 32 % 2 == col // (HD + 1))).astype(np.float32)
    div = np.exp(np.arange(0, HD, 2, dtype=np.float32) * np.float32(-np.log(10000.0) / HD)).astype(np.float32)
    ang = np.arange(T, dtype=np.float64)[None, :] * div.astype(np.float64)[:, None]
    table = np.stack([np.sin(ang), np.cos(ang)], 1).reshape(HD, T).astype(np.float32)
    c["table"] = table
    feat = np.stack([np.cos(ang), np.sin(ang)], 1).reshape(HD, T).astype(np.float32)
    c["features"] = feat
    m1, m2 = np.zeros((HD, HD), np.float32), np.zeros((HD, HD), np.float32)
    for m in range(HD // 2):
        m1[2 * m, 2 * m] = m1[2 * m + 1, 2 * m] = 1
        m2[2 * m + 1, 2 * m + 1] = -1
        m2[2 * m, 2 * m + 1] = 1
    c["m12"] = np.stack([m1, m2], 1)
    i, j = np.arange(P)[None, :], np.arange(P)[:, None]
    c["decay_mask"] = np.where(i >= j, np.exp((i - j) * np.log(DECAY)), 0).astype(np.float32)
    c["decay_cols"] = np.stack([DECAY ** (np.arange(P) + 1.0), DECAY ** (P - 1.0 - np.arange(P))], 1).astype(np.float32)
    c["row_base"] = (np.arange(B * EXPERTS) // EXPERTS * T).astype(np.float32)[:, None]
    c["lag"] = np.maximum(i - j - 1, 0).astype(np.float32)
    c["later"] = (i > j).astype(np.float32)
    c["steps"] = np.stack([np.arange(P), P - 1 - np.arange(P)], 1).astype(np.float32)
    return c


def relative_features(nc, env, st, w_rel, QS, key_features):
    wr = st.sb("wr", [HD, 2, H])
    lhs = st.sb("lhs", [HD, H, HD])
    tmp = st.sb("tmp", [HD, H, HD])
    table = st.sb("table", [HD, T])
    m12 = st.sb("m12", [HD, 2, HD])
    full = st.sb("full", [P, T])
    rest = st.sb("rest", [P, T])
    part = st.sb("part", [P, 3, T], BF16)
    ps = st.ps("ps", [P, T])
    kf = st.sb("kf", [HD, 2, T])
    kpart = st.sb("kpart", [HD, 3, T], BF16)
    got, own, made, stored = (st.sem(n) for n in ("got", "own", "made", "stored"))
    with nc.Block() as block:
        @block.sync
        def _(sp):
            sp.dma_start(kf[:, 0, :], env.dram["features"]).then_inc(got, 16)
            sp.dma_start(wr[:, 0, :], w_rel).then_inc(got, 16)
            for m in range(HD):
                sp.dma_start(wr[m:m + 1, 1, :], w_rel[m ^ 1:(m ^ 1) + 1, :]).then_inc(got, 16)
            sp.dma_start(table[:], env.dram["table"]).then_inc(got, 16)
            sp.dma_start(m12[:], env.dram["m12"]).then_inc(got, 16)
            sp.wait_ge(own, 8)
            for b in range(B):
                for n, p in enumerate(PART_Q):
                    sp.dma_start(QS[b, :, SPLITS + n, :, :], part[:, p, :]).then_inc(stored, 16)
            sp.wait_ge(own, 12)
            for n, p in enumerate(PART_K):
                sp.dma_start(key_features[n * HD:(n + 1) * HD, :], kpart[:, p, :]).then_inc(stored, 16)
            sp.wait_ge(stored, 16 * (B + 1) * SPLITS)

        @block.vector
        def _(dve):
            ch = Chain(dve, own)
            dve.wait_ge(got, 16 * (HD + 4))
            a = lambda k: wr[:, k, :].unsqueeze(2).broadcast_to([HD, H, HD])
            m = lambda k: m12[:, k, :].unsqueeze(1).broadcast_to([HD, H, HD])
            ch(dve.tensor_tensor(lhs[:], a(0), m(0), ALU.mult))
            ch(dve.tensor_tensor(tmp[:], a(1), m(1), ALU.mult))
            ch(dve.tensor_tensor(lhs[:], lhs[:], tmp[:], ALU.add))
            dve.wait_ge(made, 1)
            ch(dve.tensor_copy(full[:], ps[:]))
            ch(dve.tensor_copy(part[:, 0, :], full[:]))
            ch(dve.tensor_tensor(rest[:], full[:], part[:, 0, :], ALU.subtract))
            ch(dve.tensor_copy(part[:, 1, :], rest[:]))
            ch(dve.tensor_tensor(part[:, 2, :], rest[:], part[:, 1, :], ALU.subtract))
            ch(dve.tensor_copy(kpart[:, 0, :], kf[:, 0, :]))
            ch(dve.tensor_tensor(kf[:, 1, :], kf[:, 0, :], kpart[:, 0, :], ALU.subtract))
            ch(dve.tensor_copy(kpart[:, 1, :], kf[:, 1, :]))
            ch(dve.tensor_tensor(kpart[:, 2, :], kf[:, 1, :], kpart[:, 1, :], ALU.subtract))

        @block.tensor
        def _(pe):
            pe.wait_ge(own, 3)
            for n in range(2):
                ins = pe.matmul(ps[:, n * 512:(n + 1) * 512], lhs[:].rearrange("p h f -> p (h f)"),
                                table[:, n * 512:(n + 1) * 512], start=True, stop=True)
            ins.then_inc(made, 1)


class Env:
    pass


def build(nc, i, out, stages=99, first=1):
    env = Env()
    env.dram = i
    env.recip_sem = {}
    with ExitStack() as ctx:
        main = ctx.enter_context(Stage(nc, "main"))
        env.X = main.sb("X", [P, B * T])
        env.ident = main.sb("ident", [P, P])
        env.identb = main.sb("identb", [P, P], BF16)
        env.blk = main.sb("blk", [P, H])
        env.blk2 = main.sb("blk2", [P, P])
        env.sel = main.sb("sel", [P, 2 * (HD + 1)])
        env.minus_half = main.sb("minus_half", [P, 32])
        x_in = i["L0_attn_a_x"].rearrange("b (j p) d -> p (b j) d", p=P)
        x_out = out.rearrange("b (j p) d -> p (b j) d", p=P)
        Passed.sem = main.sem("passed")
        got, own = main.sem("got"), main.sem("own")
        env.gathered = [nc.alloc_semaphore("gathered0"), nc.alloc_semaphore("gathered1")]
        env.scattered = nc.alloc_semaphore("scattered")
        env.experts_run = 0
        with nc.Block() as block:
            @block.sync
            def _(sp):
                n = load(sp, got, [(env.ident[:], i["ident"]), (env.blk[:], i["blk"]), (env.blk2[:], i["blk2"]),
                                   (env.sel[:], i["sel"])]
                         + [(env.X[:, b * T:(b + 1) * T].rearrange("p (j d) -> p j d", d=D),
                             x_in[:, b * TILES:(b + 1) * TILES, :]) for b in range(B)])
                sp.wait_ge(got, n)

            @block.vector
            def _(dve):
                dve.memset(env.minus_half[:], -0.5).then_inc(own, 1)
                dve.wait_ge(got, 8 * 16)
                dve.tensor_copy(env.identb[:], env.ident[:]).then_inc(own, 1)
                dve.wait_ge(own, 2)

        if first <= 1 <= stages:
            softmax_block_a(nc, env, i)
        if first <= 2 <= stages:
            experts(nc, env, i, "f1")
        if first <= 3 <= stages:
            retention_block(nc, env, i)
        if first <= 4 <= stages:
            experts(nc, env, i, "f2")
        if first <= 5 <= stages:
            masked_softmax_block(nc, env, i)
        if stages >= 6:
            linear_weights(nc, env, i, main)
        if first <= 6 <= stages:
            linear_block(nc, env, "l1")
        if first <= 7 <= stages:
            rwkv_block(nc, env, i)
        if first <= 8 <= stages:
            linear_block(nc, env, "l2")

        done = main.sem("done")
        with nc.Block() as block:
            @block.sync
            def _(sp):
                for b in range(B):
                    sp.dma_start(x_out[:, b * TILES:(b + 1) * TILES, :],
                                 env.X[:, b * T:(b + 1) * T].rearrange("p (j d) -> p j d", d=D)).then_inc(done, 16)
                sp.wait_ge(done, 16 * B)


def experts(nc, env, i, name):
    ROWS = B * EXPERTS
    ROUNDS = (CAPACITY + 7) // 8
    FULL = CAPACITY // P
    REST = CAPACITY - FULL * P
    assert FULL == 2 and REST == 1
    MT = FULL * B
    normed = nc.dram_tensor(f"{name}_normed", [B * T, D], F32, kind="Internal").ap()
    total = nc.dram_tensor(f"{name}_total", [B * T, D], F32, kind="Internal").ap()
    rest_d = nc.dram_tensor(f"{name}_rest", [ROWS, 2], F32, kind="Internal").ap()
    tokens = lambda d, s: d.rearrange("(b j p) d -> b p j d", b=B, p=P)[s]
    with Stage(nc, name) as sw:
        logits = sw.sb("logits", [P, TILES, B, EXPERTS])
        idxT = sw.sb("idxT", [P, EXPERTS, MT], mybir.dt.uint32)
        gateT = sw.sb("gateT", [P, EXPERTS, MT])
        rest_f = sw.sb("rest_f", [B, EXPERTS, 2])
        rest_i = sw.sb("rest_i", [B, EXPERTS], mybir.dt.uint32)
        saved_total = sw.sem("saved_total")
        with Stage(nc, name + "r") as st:
            nm = Norm(st, env)
            rw = st.sb("rw", [P, EXPERTS])
            psR = st.ps("psR", [P, TILES, EXPERTS])
            got, r_ready, r_taken = st.sem("got"), st.sem("r_ready"), st.sem("r_taken")
            y_saved, y_stored = st.sem("y_saved"), st.sem("y_stored")
            with nc.Block() as block:
                @block.sync
                def _(sp):
                    sp.dma_start(rw[:], i["router_wT"]).then_inc(got, 16)
                    for b in range(B):
                        sp.dma_start(tokens(total, b), batch(env.X, b)).then_inc(saved_total, 16)

                    def body(s, u):
                        wait_alone(sp, nm.y_ready, s + 1)
                        sp.dma_start(normed.rearrange("(b j p) d -> b p j d", b=B, p=P)[ds(s, 1)].rearrange(
                            "o p j d -> (o p) j d"), nm.y[:, u]).then_inc(y_stored, 16)
                        sp.wait_ge(y_stored, s * 16 + 16)
                        sp.sem_inc(y_saved, 1)
                    loop_batches(sp, body)
                    sp.wait_ge(saved_total, 16 * B)

                @block.vector
                def _(dve):
                    nm.credits(dve)
                    dve.sem_inc(y_saved, 2)

                    def body(s, u):
                        nm.vector(dve, s, u, saved=y_saved)
                        dve.wait_ge(r_ready, s + 1)
                        dve.tensor_copy(logits[:, :, ds(s, 1), :].rearrange("p j b e -> p j (b e)"),
                                        psR[:]).then_inc(r_taken, 1)
                    loop_batches(dve, body)

                @block.gpsimd
                def _(pool):
                    loop_batches(pool, lambda s, u: nm.gpsimd(pool, s, u))

                @block.tensor
                def _(pe):
                    pe.wait_ge(got, 16)

                    def body(s, u):
                        nm.tensor(pe, s, u)
                        pe.wait_ge(nm.xt_ready, s + 1)
                        pe.wait_ge(r_taken, s)
                        for j in range(TILES):
                            ins = pe.matmul(psR[:, j, :], nm.xT[:, u, j * P:(j + 1) * P], rw[:], start=True, stop=True)
                        ins.then_inc(r_ready, 1)
                    loop_batches(pe, body)

                @block.scalar
                def _(act):
                    def body(s, u):
                        nm.scalar(act, s, u)
                        act.wait_ge(r_ready, s + 1)
                        act.sem_inc(nm.xt_free, 1)
                    loop_batches(act, body)

        with Stage(nc, name + "k") as st:
            small = st.sb("small", [P, TILES * B])
            work = st.sb("work", [ROWS, T])
            best = st.sb("best", [ROWS, ROUNDS * 8])
            where = st.sb("where", [ROWS, ROUNDS * 8], mybir.dt.uint32)
            where_f = st.sb("where_f", [ROWS, ROUNDS * 8])
            rest = st.sb("rest", [ROWS, 2])
            row_base = st.sb("row_base", [ROWS, 1])
            top8 = st.sb("top8", [ROWS, 8])
            idx8 = st.sb("idx8", [ROWS, 8], mybir.dt.uint32)
            psW = st.ps("psW", [ROWS, T])
            psI = st.ps("psI", [P, 2, FULL, ROWS])
            got, own, ex_ready, in_ready, w_ready, t_ready, moved = (
                st.sem(n) for n in ("got", "own", "ex_ready", "in_ready", "w_ready", "t_ready", "moved"))
            rounds_own = st.sem("rounds_own")
            lg = logits[:].rearrange("p j b e -> p (j b) e")
            spread = small[:].unsqueeze(2).broadcast_to([P, TILES * B, EXPERTS])
            with nc.Block() as block:
                @block.vector
                def _(dve):
                    ch = Chain(dve, own)
                    ch(dve.tensor_reduce(small[:], lg, AX.X, ALU.max))
                    dve.tensor_tensor(lg, lg, spread, ALU.subtract).then_inc(in_ready, 1)
                    dve.wait_ge(ex_ready, 1)
                    ch(dve.tensor_reduce(small[:], lg, AX.X, ALU.add))
                    ch(dve.reciprocal(small[:], small[:]))
                    dve.tensor_tensor(lg, lg, spread, ALU.mult).then_inc(in_ready, 1)
                    dve.wait_ge(w_ready, 1)
                    dve.tensor_copy(work[:], psW[:]).then_inc(rounds_own, 1)
                    dve.wait_ge(rounds_own, 1)
                    with dve.Fori(0, ROUNDS) as r:
                        b8, w8 = best[:, ds(r * 8, 8)], where[:, ds(r * 8, 8)]
                        dve.max(top8[:], work[:]).then_inc(rounds_own, 1)
                        dve.wait_ge(rounds_own, r * 3 + 2)
                        dve.tensor_copy(b8, top8[:]).then_inc(rounds_own, 1)
                        dve.max_index(idx8[:], top8[:], work[:])
                        dve.match_replace(work[:], top8[:], work[:], TAKEN).then_inc(rounds_own, 1)
                        dve.wait_ge(rounds_own, r * 3 + 4)
                        dve.tensor_copy(w8, idx8[:])
                    ch(dve.memset(rest[:], 0.0))
                    ch(dve.tensor_copy(where_f[:], where[:]))
                    dve.wait_ge(got, 16)
                    ch(dve.tensor_scalar(where_f[:], where_f[:], row_base[:, 0:1], None, ALU.add))
                    dve.tensor_copy(rest[:, 0:1], where_f[:, CAPACITY - 1:CAPACITY])
                    dve.tensor_copy(rest[:, 1:2], best[:, CAPACITY - 1:CAPACITY]).then_inc(in_ready, 1)
                    dve.wait_ge(t_ready, 1)
                    form = lambda k: psI[:, k].rearrange("p f (b e) -> p e f b", b=B)
                    for f in range(FULL):
                        dve.tensor_copy(idxT[:, :, f * B:(f + 1) * B], form(0)[:, :, f])
                        ins = dve.tensor_copy(gateT[:, :, f * B:(f + 1) * B], form(1)[:, :, f])
                    ch(ins)
                    dve.wait_ge(moved, 32)
                    ch(dve.tensor_copy(rest_i[:], rest_f[:, :, 0]))

                @block.scalar
                def _(act):
                    act.wait_ge(in_ready, 1)
                    act.activation(lg, lg, ACT.Exp).then_inc(ex_ready, 1)

                @block.tensor
                def _(pe):
                    pe.wait_ge(in_ready, 2)
                    for j in range(TILES):
                        ins = pe.transpose(psW[:, j * P:(j + 1) * P], logits[:, j].rearrange("p b e -> p (b e)"),
                                           env.ident[:])
                    ins.then_inc(w_ready, 1)
                    pe.wait_ge(in_ready, 3)
                    for k, src in enumerate((where_f, best)):
                        for f in range(FULL):
                            ins = pe.transpose(psI[:, k, f, :], src[:, f * P:(f + 1) * P], env.ident[0:ROWS, 0:ROWS])
                    ins.then_inc(t_ready, 1)

                @block.sync
                def _(sp):
                    sp.dma_start(row_base[:], i["row_base"]).then_inc(got, 16)
                    sp.wait_ge(in_ready, 3)
                    sp.dma_start(rest_d, rest[:]).then_inc(moved, 16)
                    sp.wait_ge(moved, 16)
                    sp.dma_start(rest_f[:], rest_d.rearrange("(b e) k -> b e k", b=B)).then_inc(moved, 16)
                    sp.wait_ge(moved, 32)

        with Stage(nc, name + "e") as st:
            w1 = st.sb("w1", [P, 2, HIDDEN])
            w2 = st.sb("w2", [P, 2, HK, D])
            b1 = st.sb("b1", [P, 2, HK])
            b2 = st.sb("b2", [P, 2, D])
            ie = st.sb("ie", [P, 2, MT], mybir.dt.uint32)
            ir = st.sb("ir", [B, 2, 1], mybir.dt.uint32)
            g = st.sb("g", [P, 2, MT * D])
            gr = st.sb("gr", [B, 2, D])
            WIDE = MT * P + B
            xg = st.sb("xg", [P, 2, WIDE])
            hT = st.sb("hT", [P, 2, HK, WIDE])
            yg = st.sb("yg", [P, 2, MT * D])
            yr = st.sb("yr", [B, 2, D])
            psG = st.ps("psG", [P, MT * P])
            psH = st.ps("psH", [P, 2, 512])
            psY = st.ps("psY", [P, MT * D])
            psL = st.ps("psL", [P, 512])
            psLY = st.ps("psLY", [B, D])
            lx, lh, ly = psL[:, 256:256 + B], psL[:, 384:384 + HK * B], psLY[:]
            w_got = [st.sem("w_got0"), st.sem("w_got1")]
            gathered, scattered = env.gathered, env.scattered
            got0, scattered0 = env.experts_run * 16 * (MT + 1) * EXPERTS // 2, env.experts_run * 16 * (MT + 1) * EXPERTS
            env.experts_run += 1
            names = ("idx_own", "g_taken", "xt_ready", "xg_ready", "h_ready", "h_taken", "lh_ready", "hidden_ready",
                     "y_ready", "y_taken", "own", "yg_ready")
            (idx_own, g_taken, xt_ready, xg_ready, h_ready, h_taken, lh_ready, hidden_ready, y_ready, y_taken,
             own, yg_ready) = (st.sem(n) for n in names)
            yg_free = st.sem("yg_free")
            TURNS = EXPERTS // 2
            CH = MT * P // 512 * HK

            def turns(eng, body):
                body(0, True, False)
                with eng.Fori(1, TURNS - 1) as t:
                    body(t, False, False)
                body(TURNS - 1, False, True)

            with nc.Block() as block:
                @block.sync
                def _(sp):
                    def body(t, first, last):
                        for u in range(2):
                            e = t * 2 + u
                            if not first:
                                wait_alone(sp, y_taken, e - 1)
                            sp.dma_start(w1[:, u, :], i["L0_ffn_w1"][ds(e, 1)].rearrange("o p h -> (o p) h")).then_inc(w_got[u], 16)
                            sp.dma_start(w2[:, u], i["L0_ffn_w2"].rearrange("e (k p) d -> e p k d", p=P)[ds(e, 1)].rearrange(
                                "o p k d -> (o p) k d")).then_inc(w_got[u], 16)
                            sp.dma_start(b1[:, u, :], i["b1_cols"][ds(e, 1)].rearrange(
                                "o p k -> (o p) k")).then_inc(w_got[u], 16)
                            sp.dma_start(b2[:, u, :], i["L0_ffn_b2"][ds(e, 1), :].rearrange(
                                "o d -> (o d)").partition_broadcast(P)).then_inc(w_got[u], 16)
                    turns(sp, body)

                @block.gpsimd
                def _(pool):
                    def gather(t, u, first):
                        e = t * 2 + u
                        if not first:
                            pool.wait_ge(g_taken, e - 1)
                        pool.tensor_copy(ie[:, u, :], idxT[:, ds(e, 1), :].rearrange("p o m -> p (o m)")).then_inc(idx_own, 1)
                        pool.tensor_copy(ir[:, u, :], rest_i[:, ds(e, 1)]).then_inc(idx_own, 1)
                        wait_alone(pool, idx_own, e * 2 + 2)
                        for m in range(MT):
                            pool.indirect_dma_start(g[:, u, m * D:(m + 1) * D], None, normed,
                                                    bass.IndirectOffsetOnAxis(ap=ie[:, u, m:m + 1], axis=0)).then_inc(gathered[u], 16)
                        pool.indirect_dma_start(gr[:, u, :], None, normed,
                                                bass.IndirectOffsetOnAxis(ap=ir[:, u, :], axis=0)).then_inc(gathered[u], 16)

                    gather(0, 0, True)
                    done = 16 * (MT + 1)

                    def body(t, first, last):
                        for u in range(2):
                            e = t * 2 + u
                            if not (first and u == 0):
                                wait_alone(pool, scattered, e * done + scattered0)
                            if not (last and u == 1):
                                gather(t + u, 1 - u, first and u == 0)
                            wait_alone(pool, yg_ready, e + 1)
                            for m in range(MT):
                                pool.indirect_dma_start(total, bass.IndirectOffsetOnAxis(ap=ie[:, u, m:m + 1], axis=0),
                                                        yg[:, u, m * D:(m + 1) * D], None, compute_op=ALU.add).then_inc(scattered, 16)
                            pool.indirect_dma_start(total, bass.IndirectOffsetOnAxis(ap=ir[:, u, :], axis=0),
                                                    yr[:, u, :], None, compute_op=ALU.add).then_inc(scattered, 16)
                    turns(pool, body)
                    pool.wait_ge(scattered, done * EXPERTS + scattered0)

                @block.tensor
                def _(pe):
                    def transposes(t, u, first):
                        e = t * 2 + u
                        pe.wait_ge(gathered[u], (t + 1) * 16 * (MT + 1) + got0)
                        if not first:
                            pe.wait_ge(xg_ready, e)
                        for m in range(MT):
                            pe.transpose(psG[:, m * P:(m + 1) * P], g[:, u, m * D:(m + 1) * D], env.ident[:])
                        pe.transpose(lx, gr[:, u, :], env.ident[0:B, 0:B]).then_inc(xt_ready, 1)

                    def hidden(t, u):
                        e = t * 2 + u
                        pe.wait_ge(xg_ready, e + 1)
                        pe.wait_ge(w_got[u], (t + 1) * 64)
                        for k in range(HK):
                            ins = pe.matmul(lh[:, k * B:(k + 1) * B], w1[:, u, k * P:(k + 1) * P],
                                            xg[:, u, MT * P:WIDE], start=True, stop=True)
                        ins.then_inc(lh_ready, 1)
                        for n in range(CH):
                            if not (isinstance(e, int) and e == 0 and n < 2):
                                pe.wait_ge(h_taken, e * CH + n - 1)
                            k, c = n % HK, n // HK
                            pe.matmul(psH[:, n % 2, :], w1[:, u, k * P:(k + 1) * P], xg[:, u, c * 512:(c + 1) * 512],
                                      start=True, stop=True).then_inc(h_ready, 1)

                    def outputs(t, u):
                        e = t * 2 + u
                        pe.wait_ge(hidden_ready, e + 1)
                        pe.wait_ge(y_taken, e)
                        for m in range(MT + 1):
                            o, lo, hi = (ly, MT * P, WIDE) if m == MT else (psY[:, m * D:(m + 1) * D], m * P, (m + 1) * P)
                            for k in range(HK):
                                ins = pe.matmul(o, hT[:, u, k, lo:hi], w2[:, u, k, :], start=(k == 0), stop=(k == HK - 1))
                        ins.then_inc(y_ready, 1)

                    transposes(0, 0, True)

                    def body(t, first, last):
                        for u in range(2):
                            hidden(t, u)
                            if not (last and u == 1):
                                pe.wait_ge(hidden_ready, t * 2 + u + 1)
                                transposes(t + u, 1 - u, False)
                            outputs(t, u)
                    turns(pe, body)

                @block.scalar
                def _(act):
                    def take(t, u):
                        e = t * 2 + u
                        act.wait_ge(xt_ready, e + 1)
                        act.activation(xg[:, u, 0:MT * P], psG[:], ACT.Copy)
                        act.activation(xg[:, u, MT * P:WIDE], lx, ACT.Copy).then_inc(xg_ready, 1)
                        act.sem_inc(g_taken, 1)

                    take(0, 0)

                    def body(t, first, last):
                        for u in range(2):
                            e = t * 2 + u
                            act.wait_ge(w_got[u], (t + 1) * 64)
                            if not first:
                                act.wait_ge(y_ready, e - 1)
                            act.wait_ge(lh_ready, e + 1)
                            for k in range(HK):
                                act.activation(hT[:, u, k, MT * P:WIDE], lh[:, k * B:(k + 1) * B], ACT.Gelu, bias=b1[:, u, k:k + 1])
                            for n in range(CH):
                                k, c = n % HK, n // HK
                                act.wait_ge(h_ready, e * CH + n + 1)
                                ins = act.activation(hT[:, u, k, c * 512:(c + 1) * 512], psH[:, n % 2, :], ACT.Gelu,
                                                     bias=b1[:, u, k:k + 1])
                                ins.then_inc(h_taken, 1)
                            act.wait_ge(h_taken, e * CH + CH)
                            act.sem_inc(hidden_ready, 1)
                            if not (last and u == 1):
                                take(t + u, 1 - u)
                    turns(act, body)

                @block.vector
                def _(dve):
                    def body(t, first, last):
                        for u in range(2):
                            e = t * 2 + u
                            out = yg[:, u, :].rearrange("p (m d) -> p m d", d=D)
                            if not first:
                                dve.wait_ge(scattered, (e - 1) * 16 * (MT + 1) + scattered0)
                            dve.wait_ge(y_ready, e + 1)
                            dve.tensor_tensor(out, psY[:].rearrange("p (m d) -> p m d", d=D),
                                              b2[:, u, :].unsqueeze(1).broadcast_to([P, MT, D]), ALU.add)
                            dve.tensor_tensor(yr[:, u, :], ly, b2[0:B, u, :], ALU.add).then_inc(own, 1)
                            dve.wait_ge(own, e + 1)
                            dve.tensor_tensor(out, out, gateT[:, ds(e, 1), :].rearrange("p o m -> p (o m)").unsqueeze(2)
                                              .broadcast_to([P, MT, D]), ALU.mult)
                            dve.tensor_tensor(yr[:, u, :], yr[:, u, :], rest_f[:, ds(e, 1), 1].broadcast_to([B, D]),
                                              ALU.mult).then_inc(yg_ready, 1)
                            dve.sem_inc(y_taken, 1)
                    turns(dve, body)

            back = st.sem("back")
            with nc.Block() as block:
                @block.sync
                def _(sp):
                    for b in range(B):
                        sp.dma_start(batch(env.X, b), tokens(total, b)).then_inc(back, 16)
                    sp.wait_ge(back, 16 * B)


def retention_inputs(nc, env, st, weights, jobs, mixes=None, pad=0):
    nm = Norm(st, env, pad=pad)
    n_src = 1 if mixes is None else mixes.shape[1]
    psP = st.ps("psP", [P, 2, T])
    p_ready, p_taken = st.sem("p_ready"), st.sem("p_taken")
    src_ready, own = st.sem("src_ready"), st.sem("own")
    if mixes is not None:
        diff = st.sb("diff", [P, T])
        src = st.sb("src", [P, n_src, T])
    J = len(jobs)
    with nc.Block() as block:
        @block.vector
        def _(dve):
            nm.credits(dve)
            ch = Chain(dve, own)
            if mixes is not None:
                dve.memset(nm.xT[:, :, 0:pad], 0.0).then_inc(src_ready, 1)

            def body(s, u):
                nm.vector(dve, s, u)
                if mixes is not None:
                    dve.wait_ge(nm.xt_ready, s + 1)
                    x = nm.xT[:, u, pad:pad + T]
                    ch.start(s)
                    ch(dve.tensor_tensor(diff[:], nm.xT[:, u, 0:T], x, ALU.subtract))
                    dve.wait_ge(p_ready, s * J)
                    for m in range(n_src):
                        ins = dve.scalar_tensor_tensor(src[:, m, :], diff[:], mixes[:, m:m + 1], x, ALU.mult, ALU.add)
                    ins.then_inc(src_ready, 1)
                    dve.wait_ge(src_ready, s + 2)
                    dve.sem_inc(nm.xt_free, 1)
            loop_batches(dve, body)

        @block.gpsimd
        def _(pool):
            loop_batches(pool, lambda s, u: nm.gpsimd(pool, s, u))

        @block.tensor
        def _(pe):
            pe.sem_inc(p_taken, 2)

            def body(s, u):
                nm.tensor(pe, s, u)
                if mixes is None:
                    pe.wait_ge(nm.xt_ready, s + 1)
                else:
                    pe.wait_ge(src_ready, s + 2)
                for n, (m, w, form, bias, func, dst) in enumerate(jobs):
                    x = nm.xT[:, u, :] if mixes is None else src[:, m, :]
                    pe.wait_ge(p_taken, s * J + n + 1)
                    o = psP[:, (u * J + n) % 2, :]
                    if form == "channels":
                        for k in range(2):
                            ins = pe.matmul(o[:, k * 512:(k + 1) * 512], w, x[:, k * 512:(k + 1) * 512], start=True, stop=True)
                    else:
                        for k in range(TILES):
                            ins = pe.matmul(o[:, k * P:(k + 1) * P], x[:, k * P:(k + 1) * P], w, start=True, stop=True)
                    ins.then_inc(p_ready, 1)
            loop_batches(pe, body)

        @block.scalar
        def _(act):
            def body(s, u):
                nm.scalar(act, s, u)
                for n, (m, w, form, bias, func, dst) in enumerate(jobs):
                    wait_alone(act, p_ready, s * J + n + 1)
                    o = psP[:, (u * J + n) % 2, :].rearrange("p (j d) -> p j d", d=D)
                    if bias is not None:
                        act.activation(dst(s), o, ACT.Identity, bias=bias).then_inc(p_taken, 1)
                    else:
                        act.activation(dst(s), o, func).then_inc(p_taken, 1)
                if mixes is None:
                    act.sem_inc(nm.xt_free, 1)
            loop_batches(act, body)


def retention(nc, env, st, QK, KT, V, OUT, mask, key_decay, out_decay, state_decay):
    qk = st.sb("qk", [P, 2, 2, P])
    qx = st.sb("qx", [P, 2, H, P])
    kd = st.sb("kd", [P, 2, D])
    sm = st.sb("sm", [P, 2, H, P])
    state = st.sb("state", [P, B, D])
    inter = st.sb("inter", [P, 2, D])
    upd = st.sb("upd", [P, 2, D])
    psS = st.ps("psS", [P, 2, 4, P])
    psO = st.ps("psO", [P, 2, 512])
    psC = st.ps("psC", [P, 2, 512])
    psU = st.ps("psU", [P, 2, 512])
    names = ("qk_ready", "kd_ready", "qx_ready", "s_ready", "s_masked", "o_ready", "inter_ready", "u_ready", "state_ready",
             "out_done", "own", "inter_taken")
    (qk_ready, kd_ready, qx_ready, s_ready, s_masked, o_ready, inter_ready, u_ready, state_ready, out_done, own,
     inter_taken) = (st.sem(n) for n in names)
    qk_free, kd_free, sm_free, o_free = (st.sem(n) for n in ("qk_free", "kd_free", "sm_free", "o_free"))
    heads_of_mask = mask.shape[1]

    def chunks(eng, body):
        with eng.Fori(0, TILES) as c:
            for b in range(B):
                body(c * B + b, c + b * TILES, b)

    with nc.Block() as block:
        @block.scalar
        def _(act):
            act.sem_inc(qk_free, 2)

            def body(m, n, b):
                act.wait_ge(qk_free, m + 1)
                act.activation(qk[:, b % 2], QK[:, ds(n, 1)].rearrange("p o a t -> p (o a) t"), ACT.Copy).then_inc(qk_ready, 1)
            chunks(act, body)

        @block.gpsimd
        def _(pool):
            pool.sem_inc(kd_free, 2)

            def body(m, n, b):
                u = b % 2
                pool.wait_ge(qk_ready, m + 1)
                pool.wait_ge(kd_free, m + 1)
                pool.tensor_tensor(qx[:, u], qk[:, u, 0, :].unsqueeze(1).broadcast_to([P, H, P]),
                                   env.blk[:].unsqueeze(2).broadcast_to([P, H, P]), ALU.mult).then_inc(qx_ready, 1)
                pool.tensor_tensor(kd[:, u, :], KT[:, ds(n, 1), :].rearrange("p o d -> p (o d)"), key_decay,
                                   ALU.mult).then_inc(kd_ready, 1)
            chunks(pool, body)

        @block.tensor
        def _(pe):
            pe.wait_ge(own, 1)

            def body(m, n, b):
                u = b % 2
                pe.wait_ge(qx_ready, m + 1)
                for g in range(4):
                    pe.wait_ge(s_masked, m * 4 + g + 1)
                    pe.matmul(psS[:, g % 2].rearrange("p h t -> p (h t)"), qk[:, u, 1, :],
                              qx[:, u, 4 * g:4 * g + 4, :].rearrange("p h t -> p (h t)"),
                              start=True, stop=True).then_inc(s_ready, 1)
                pe.wait_ge(state_ready, m + 1)
                pe.wait_ge(o_free, m + 1)
                pe.matmul(psC[:, u, 0:D], qk[:, u, 0, :], state[:, b, :], start=True, stop=True).then_inc(inter_ready, 1)
                pe.wait_ge(kd_ready, m + 1)
                v = V[:, ds(n, 1), :].rearrange("p o d -> p (o d)")
                pe.matmul(psU[:, u, 0:D], kd[:, u, :], v, start=True, stop=True).then_inc(u_ready, 1)
                pe.wait_ge(s_masked, m * 4 + 6)
                for h in range(H):
                    ins = pe.matmul(psO[:, u, h * HD:(h + 1) * HD], sm[:, u, h, :],
                                    V[:, ds(n, 1), h * HD:(h + 1) * HD].rearrange("p o d -> p (o d)"), start=True, stop=True)
                ins.then_inc(o_ready, 1)
            chunks(pe, body)

        @block.vector
        def _(dve):
            dve.sem_inc(s_masked, 2)
            dve.sem_inc(o_free, 2)
            dve.memset(state[:], 0.0).then_inc(own, 1)
            dve.wait_ge(own, 1)
            dve.sem_inc(state_ready, B)

            def body(m, n, b):
                u = b % 2
                for g in range(4):
                    dve.wait_ge(s_ready, m * 4 + g + 1)
                    mk = mask[:, 4 * g:4 * g + 4, :] if heads_of_mask > 1 else mask.broadcast_to([P, 4, P])
                    dve.tensor_tensor(sm[:, u, 4 * g:4 * g + 4, :], psS[:, g % 2], mk, ALU.mult).then_inc(s_masked, 1)
                dve.wait_ge(inter_ready, m + 1)
                dve.tensor_tensor(inter[:, u, :], psC[:, u, 0:D], out_decay, ALU.mult).then_inc(inter_taken, 1)
                dve.wait_ge(u_ready, m + 1)
                dve.sem_inc(qk_free, 1)
                dve.sem_inc(kd_free, 1)
                dve.tensor_tensor(upd[:, u, :], psU[:, u, 0:D], env.blk2[:], ALU.mult).then_inc(inter_taken, 1)
                dve.wait_ge(inter_taken, m * 2 + 2)
                dve.scalar_tensor_tensor(state[:, b, :], state[:, b, :], state_decay, upd[:, u, :], ALU.mult,
                                         ALU.add).then_inc(state_ready, 1)
                dve.wait_ge(o_ready, m + 1)
                dve.tensor_tensor(OUT[:, ds(n, 1), :].rearrange("p o d -> p (o d)"), psO[:, u, 0:D], inter[:, u, :],
                                  ALU.add).then_inc(o_free, 1)
            chunks(dve, body)


def retention_block(nc, env, i):
    W = {}
    with Stage(nc, "b") as sw:
        for n in ("Wq", "Wk", "Wv", "Wo"):
            W[n] = sw.sb(n, [P, D])
        cols = sw.sb("cols", [P, 7])
        bk, bv = sw.sb("bk", [P, D]), sw.sb("bv", [P, D])
        mask = sw.sb("mask", [P, 1, P])
        tok_decay = sw.sb("tok_decay", [P, 2])
        dmat = sw.sb("dmat", [P, 2, D])
        QK = sw.sb("QK", [P, B * TILES, 2, P])
        KT = sw.sb("KT", [P, B * TILES, D])
        V = sw.sb("V", [P, B * TILES, D])
        got, own = sw.sem("got"), sw.sem("own")
        with nc.Block() as block:
            @block.sync
            def _(sp):
                n = load(sp, got, [(W[k][:], i[f"L0_attn_b_{k}"]) for k in W]
                         + [(cols[:, k:k + 1], column(i[f"L0_attn_b_{v}"])) for k, v in enumerate(("bq", "bk", "bo", "gamma", "beta"))]
                         + [(bk[:], i["L0_attn_b_bk"].partition_broadcast(P)), (bv[:], i["L0_attn_b_bv"].partition_broadcast(P)),
                            (mask[:, 0, :], i["decay_mask"]), (tok_decay[:], i["decay_cols"])])
                sp.wait_ge(got, n)

            @block.vector
            def _(dve):
                dve.memset(dmat[:], 1.0).then_inc(own, 1)
                dve.memset(cols[:, 6:7], DECAY ** P).then_inc(own, 1)
                dve.wait_ge(own, 2)
                dve.wait_ge(got, 13 * 16)
                for k in range(2):
                    ins = dve.tensor_scalar(dmat[:, k, :], dmat[:, k, :], tok_decay[:, k:k + 1], None, ALU.mult)
                ins.then_inc(own, 1)
        tiles = lambda x, s: x[:, ds(s * TILES, TILES)]
        with Stage(nc, "bi") as st:
            retention_inputs(nc, env, st, None, [
                (0, W["Wq"][:], "channels", cols[:, 0:1], None, lambda s: tiles(QK, s)[:, :, 0, :]),
                (0, W["Wk"][:], "channels", cols[:, 1:2], None, lambda s: tiles(QK, s)[:, :, 1, :]),
                (0, W["Wk"][:], "tokens", None, ACT.Copy, lambda s: tiles(KT, s)),
                (0, W["Wv"][:], "tokens", None, ACT.Copy, lambda s: tiles(V, s)),
            ])
            bias_done = st.sem("bias_done")
            with nc.Block() as block:
                @block.vector
                def _(dve):
                    for x, bias in ((KT, bk), (V, bv)):
                        dve.tensor_tensor(x[:], x[:], bias[:].unsqueeze(1).broadcast_to([P, B * TILES, D]),
                                          ALU.add).then_inc(bias_done, 1)
                    dve.wait_ge(bias_done, 2)
        OUT = sw.sb("OUT", [P, B * TILES, D])
        with Stage(nc, "br") as st:
            retention(nc, env, st, QK, KT, V, OUT, mask[:], dmat[:, 1, :], dmat[:, 0, :], cols[:, 6:7])
        with Stage(nc, "bo") as st:
            group_norm_out(nc, env, st, OUT, W["Wo"], cols)


def group_norm_out(nc, env, st, OUT, wo, cols):
    a = st.sb("a", [P, 2, T])
    aT = st.sb("aT", [P, 2, T])
    yT = st.sb("yT", [P, 2, T])
    stats = st.sb("stats", [P, 2, 2, 6])
    mv = st.sb("mv", [P, 2, 2])
    avg = st.sb("avg", [P, P])
    work = st.sb("work", [P, 2, 8])
    psT = st.ps("psT", [P, T])
    psY = st.ps("psY", [P, T])
    psM = st.ps("psM", [P, 2, 512])
    names = ("a_ready", "t1_ready", "aT_ready", "y_ready", "yT_ready", "stats_ready", "mean_ready", "dev_ready",
             "var_ready", "ve_ready", "rstd_ready", "affine_ready", "z_ready", "t2_ready", "added", "own")
    (a_ready, t1_ready, aT_ready, y_ready, yT_ready, stats_ready, mean_ready, dev_ready, var_ready, ve_ready,
     rstd_ready, affine_ready, z_ready, t2_ready, added, own) = (st.sem(n) for n in names)
    made = st.sem("made")
    with nc.Block() as block:
        @block.scalar
        def _(act):
            def body(s, u):
                act.wait_ge(t2_ready, s)
                act.activation(a[:, u, :], OUT[:, ds(s * TILES, TILES), :].rearrange("p j d -> p (j d)"), ACT.Copy).then_inc(a_ready, 1)
                act.wait_ge(t1_ready, s + 1)
                act.activation(aT[:, u, :], psT[:], ACT.Copy).then_inc(aT_ready, 1)
                act.wait_ge(y_ready, s + 1)
                act.activation(yT[:, u, :], psY[:], ACT.Identity, bias=cols[:, 2:3]).then_inc(yT_ready, 1)
                act.wait_ge(affine_ready, s + 1)
                act.activation(yT[:, u, :], yT[:, u, :], ACT.Identity, bias=work[:, u, 5:6], scale=work[:, u, 4:5]).then_inc(z_ready, 1)
            loop_batches(act, body)

        @block.tensor
        def _(pe):
            pe.wait_ge(made, 1)

            def body(s, u):
                pe.wait_ge(a_ready, s + 1)
                pe.wait_ge(added, s)
                for j in range(TILES):
                    ins = pe.transpose(psT[:, j * P:(j + 1) * P], a[:, u, j * P:(j + 1) * P], env.ident[:])
                ins.then_inc(t1_ready, 1)
                pe.wait_ge(aT_ready, s + 1)
                pe.wait_ge(yT_ready, s)
                for k in range(2):
                    ins = pe.matmul(psY[:, k * 512:(k + 1) * 512], wo[:], aT[:, u, k * 512:(k + 1) * 512], start=True, stop=True)
                ins.then_inc(y_ready, 1)
                pe.wait_ge(stats_ready, s + 1)
                pe.matmul(psM[:, 0, 0:1], avg[:], mv[:, u, 0:1], start=True, stop=True).then_inc(mean_ready, 1)
                pe.wait_ge(dev_ready, s + 1)
                pe.matmul(psM[:, 1, 0:1], avg[:], work[:, u, 2:3], start=True, stop=True).then_inc(var_ready, 1)
                pe.wait_ge(z_ready, s + 1)
                for j in range(TILES):
                    ins = pe.transpose(psT[:, j * P:(j + 1) * P], yT[:, u, j * P:(j + 1) * P], env.ident[:])
                ins.then_inc(t2_ready, 1)
            loop_batches(pe, body)

        @block.gpsimd
        def _(pool):
            def body(s, u):
                pool.wait_ge(ve_ready, s + 1)
                pool.tensor_tensor(work[:, u, 6:7], work[:, u, 3:4], env.minus_half[:, 0:1], ALU.pow).then_inc(rstd_ready, 1)
            loop_batches(pool, body)

        @block.vector
        def _(dve):
            dve.tensor_scalar(avg[:], env.blk2[:], 1.0 / HD, None, ALU.mult).then_inc(made, 1)
            ch = Chain(dve, own)

            def body(s, u):
                w = lambda k: work[:, u, k:k + 1]
                ch.start(s * 7)
                dve.wait_ge(yT_ready, s + 1)
                for k in range(2):
                    ins = dve.bn_stats(stats[:, u, k, :], yT[:, u, k * 512:(k + 1) * 512])
                ch(ins, alone=True)
                dve.bn_aggr(mv[:, u, :], stats[:, u].rearrange("p k n -> p (k n)")).then_inc(stats_ready, 1)
                dve.wait_ge(mean_ready, s + 1)
                ch(dve.tensor_copy(w(0), psM[:, 0, 0:1]))
                ch(dve.tensor_tensor(w(1), mv[:, u, 0:1], w(0), ALU.subtract))
                ch(dve.tensor_tensor(w(1), w(1), w(1), ALU.mult))
                dve.tensor_tensor(w(2), w(1), mv[:, u, 1:2], ALU.add).then_inc(dev_ready, 1)
                dve.wait_ge(var_ready, s + 1)
                dve.tensor_scalar(w(3), psM[:, 1, 0:1], LN_EPS, None, ALU.add).then_inc(ve_ready, 1)
                dve.wait_ge(rstd_ready, s + 1)
                ch(dve.tensor_tensor(w(4), w(6), cols[:, 3:4], ALU.mult))
                ch(dve.tensor_tensor(w(7), w(0), w(4), ALU.mult))
                ch(dve.tensor_tensor(w(5), cols[:, 4:5], w(7), ALU.subtract))
                dve.sem_inc(affine_ready, 1)
                dve.wait_ge(t2_ready, s + 1)
                xb = batch(env.X, s)
                dve.tensor_tensor(xb, psT[:].rearrange("p (j d) -> p j d", d=D), xb, ALU.add).then_inc(added, 1)
            loop_batches(dve, body)


def masked_softmax_block(nc, env, i):
    QS = nc.dram_tensor("c_q_parts", [B, H, SPLITS, HD, T], BF16, kind="Internal").ap()
    KS = nc.dram_tensor("c_k_parts", [B, H, SPLITS, HD, T], BF16, kind="Internal").ap()
    LASTD = nc.dram_tensor("c_last", [B, H, T], F32, kind="Internal").ap()
    MASKD = nc.dram_tensor("c_mask", [HEADS, T], BF16, kind="Internal").ap()
    RANKED = T - RECENCY
    TAKE = K_KEEP - RECENCY
    ROUNDS, LEFT = TAKE // 8, TAKE % 8
    assert LEFT > 0
    with Stage(nc, "c") as sw:
        w = sw.sb("w", [P, 3 * D])
        wo = sw.sb("wo", [P, D])
        got = sw.sem("got")
        with nc.Block() as block:
            @block.sync
            def _(sp):
                n = load(sp, got, [(w[:], i["L1_attn_a_W_attn"]), (wo[:], i["L1_attn_a_W_proj"])])
                sp.wait_ge(got, n)
        VTOK = sw.sb("vtok", [P, HEADS, TILES, HD + 1])
        ATT = sw.sb("att", [P, HEADS, TILES, HD])
        with Stage(nc, "cq") as st:
            qkv_stage(nc, env, st, QS, KS, VTOK, w, None, False, None, LASTD)
        with Stage(nc, "ck") as st:
            work = st.sb("work", [HEADS, T])
            top8 = st.sb("top8", [HEADS, 8])
            keep = st.sb("keep", [HEADS, T], BF16)
            loaded, own, stored = st.sem("loaded"), st.sem("own"), st.sem("stored")
            with nc.Block() as block:
                @block.sync
                def _(sp):
                    sp.dma_start(work[:], LASTD.rearrange("b h t -> (b h) t")).then_inc(loaded, 16)
                    sp.wait_ge(own, 2 * ROUNDS + 5)
                    sp.dma_start(MASKD, keep[:]).then_inc(stored, 16)
                    sp.wait_ge(stored, 16)

                @block.vector
                def _(dve):
                    dve.memset(keep[:], 0.0).then_inc(own, 1)
                    dve.wait_ge(loaded, 16)
                    r_work = work[:, 0:RANKED]
                    with dve.Fori(0, ROUNDS) as r:
                        dve.max(top8[:], r_work).then_inc(own, 1)
                        wait_alone(dve, own, r * 2 + 2)
                        dve.match_replace(r_work, top8[:], r_work, TAKEN).then_inc(own, 1)
                        dve.wait_ge(own, r * 2 + 3)
                    ch = Chain(dve, own)
                    ch.start(2 * ROUNDS + 1)
                    ch(dve.max(top8[:], r_work))
                    ch(dve.memset(top8[:, LEFT:8], TAKEN))
                    ch(dve.match_replace(r_work, top8[:], r_work, TAKEN))
                    ch(dve.tensor_scalar(keep[:, 0:RANKED], r_work, TAKEN, MASKED, ALU.is_gt, ALU.mult))
        with Stage(nc, "ca") as st:
            env.recip_sem["ca"] = st.sem("recip")
            attention(nc, env, st, QS, KS, VTOK, ATT, 96 + 1, None, MASKD)
        with Stage(nc, "co") as st:
            add_projected(nc, env, st, Source(
                lambda s: ATT[:, ds(s * H, H), :, :].rearrange("p h j d -> p j h d"),
                "p (j h d) -> p j h d", j=TILES, h=H), wo, None)


def linear_weights(nc, env, i, main):
    env.lin_w = main.sb("lin_w", [P, D])
    env.lin_b = main.sb("lin_b", [P, D])
    with Stage(nc, "lw") as st:
        k = st.sb("k", [P, D])
        a, b = st.sb("a", [16, D]), st.sb("b", [16, D])
        mx = st.sb("mx", [P, 4])
        ps = st.ps("ps", [P, D])
        got, own, pown, ab_ready, mx_ready, q_ready = (st.sem(n) for n in ("got", "own", "pown", "ab_ready", "mx_ready", "q_ready"))
        with nc.Block() as block:
            @block.sync
            def _(sp):
                n = load(sp, got, [(k[:], i["L1_ffn_kernel"]), (a[:], i["lora_aT"]), (b[:], i["L1_ffn_b"]),
                                   (env.lin_b[:], i["L1_ffn_bias"].partition_broadcast(P))])
                sp.wait_ge(got, n)

            @block.tensor
            def _(pe):
                pe.wait_ge(got, 64)
                pe.matmul(ps[:], a[:], b[:], start=True, stop=True).then_inc(ab_ready, 1)

            @block.gpsimd
            def _(pool):
                pool.wait_ge(mx_ready, 1)
                ch = Chain(pool, pown)
                ch(pool.partition_all_reduce(mx[:, 1:2], mx[:, 0:1], P, bass.bass_isa.ReduceOp.max))
                pool.tensor_scalar(mx[:, 2:3], mx[:, 1:2], 1.0 / 7.0, None, ALU.mult).then_inc(q_ready, 1)

            @block.vector
            def _(dve):
                ch = Chain(dve, own)
                dve.wait_ge(got, 64)
                dve.tensor_reduce(mx[:, 0:1], k[:], AX.X, ALU.max, apply_absolute_value=True).then_inc(mx_ready, 1)
                dve.wait_ge(q_ready, 1)
                ch(dve.reciprocal(mx[:, 3:4], mx[:, 2:3]))
                ch(dve.tensor_scalar(k[:], k[:], mx[:, 3:4], None, ALU.mult))
                ch(dve.tensor_scalar(k[:], k[:], 12582912.0, None, ALU.add))
                ch(dve.tensor_scalar(k[:], k[:], 12582912.0, None, ALU.subtract))
                ch(dve.tensor_scalar(k[:], k[:], -8.0, 7.0, ALU.max, ALU.min))
                ch(dve.tensor_scalar(k[:], k[:], mx[:, 2:3], None, ALU.mult))
                dve.wait_ge(ab_ready, 1)
                ch(dve.tensor_tensor(env.lin_w[:], ps[:], k[:], ALU.add))


def linear_block(nc, env, name):
    with Stage(nc, name) as st:
        nm = Norm(st, env)
        psY = st.ps("psY", [P, T])
        y_ready, added, bias_done = st.sem("y_ready"), st.sem("added"), st.sem("bias_done")
        with nc.Block() as block:
            @block.vector
            def _(dve):
                nm.credits(dve)

                def body(s, u):
                    nm.vector(dve, s, u)
                    dve.wait_ge(y_ready, s + 1)
                    dve.wait_ge(bias_done, s + 1)
                    xb = batch(env.X, s)
                    dve.tensor_tensor(xb, psY[:].rearrange("p (j d) -> p j d", d=D), xb, ALU.add).then_inc(added, 1)
                loop_batches(dve, body)

            @block.gpsimd
            def _(pool):
                def body(s, u):
                    nm.gpsimd(pool, s, u)
                    pool.wait_ge(nm.y_ready, s + 1)
                    xb = batch(env.X, s)
                    pool.tensor_tensor(xb, xb, env.lin_b[:].unsqueeze(1).broadcast_to([P, TILES, D]), ALU.add).then_inc(bias_done, 1)
                loop_batches(pool, body)

            @block.tensor
            def _(pe):
                def body(s, u):
                    nm.tensor(pe, s, u)
                    pe.wait_ge(nm.xt_ready, s + 1)
                    pe.wait_ge(added, s)
                    for j in range(TILES):
                        ins = pe.matmul(psY[:, j * D:(j + 1) * D], nm.xT[:, u, j * P:(j + 1) * P], env.lin_w[:], start=True, stop=True)
                    ins.then_inc(y_ready, 1)
                loop_batches(pe, body)

            @block.scalar
            def _(act):
                def body(s, u):
                    nm.scalar(act, s, u)
                    act.wait_ge(y_ready, s + 1)
                    act.sem_inc(nm.xt_free, 1)
                loop_batches(act, body)


def rwkv_block(nc, env, i):
    with Stage(nc, "r") as sw:
        W = {n: sw.sb(n, [P, D]) for n in ("WrT", "WkT", "WvT", "WgT", "WoT")}
        maa = sw.sb("maa", [P, 4])
        hd = sw.sb("hd", [P, 2, H])
        hc = sw.sb("hc", [P, 2])
        lag, later, steps = sw.sb("lag", [P, P]), sw.sb("later", [P, P]), sw.sb("steps", [P, 2])
        mask = sw.sb("mask", [P, H, P])
        dmat = sw.sb("dmat", [P, 2, H, HD])
        ln_w, ln_b = sw.sb("ln_w", [P, D]), sw.sb("ln_b", [P, D])
        QK = sw.sb("QK", [P, B * TILES, 2, P])
        KT = sw.sb("KT", [P, B * TILES, D])
        V = sw.sb("V", [P, B * TILES, D])
        G = sw.sb("G", [P, B * TILES, D])
        got, own, aown, e_ready, m_ready = (sw.sem(n) for n in ("got", "own", "aown", "e_ready", "m_ready"))
        bonus = sw.sb("bonus", [P, P])
        with nc.Block() as block:
            @block.sync
            def _(sp):
                n = load(sp, got, [(W[k][:], i[k]) for k in W]
                         + [(maa[:, n:n + 1], i[f"L1_attn_b_time_maa_{k}"].rearrange("a b c -> c (a b)"))
                            for n, k in enumerate(("r", "k", "v", "g"))]
                         + [(hd[:, 0, :], i["L1_attn_b_time_decay"].rearrange("h o -> (h o)").partition_broadcast(P)),
                            (hd[:, 1, :], i["L1_attn_b_time_faaaa"].rearrange("h o -> (h o)").partition_broadcast(P)),
                            (lag[:], i["lag"]), (later[:], i["later"]), (steps[:], i["steps"]),
                            (ln_w[:], i["L1_attn_b_ln_w"].partition_broadcast(P)),
                            (ln_b[:], i["L1_attn_b_ln_b"].partition_broadcast(P))])
                for h in range(H):
                    sp.dma_start(hc[h * HD:(h + 1) * HD, 0:1], i["L1_attn_b_time_decay"][h:h + 1, :].rearrange(
                        "a b -> (a b)").partition_broadcast(HD)).then_inc(got, 16)
                sp.wait_ge(got, n + 16 * H)

            ALL = 16 * (5 + 4 + 7 + H)

            @block.scalar
            def _(act):
                act.wait_ge(got, ALL)
                act.activation(hd[:, 0, :], hd[:, 0, :], ACT.Exp)
                act.activation(hc[:, 0:1], hc[:, 0:1], ACT.Exp).then_inc(e_ready, 1)
                act.wait_ge(m_ready, 1)
                act.activation(hc[:, 1:2], hc[:, 0:1], ACT.Exp, scale=float(P)).then_inc(aown, 1)
                for h in range(H):
                    act.activation(mask[:, h, :], lag[:], ACT.Exp, scale=hd[:, 0, h:h + 1]).then_inc(aown, 1)
                for k in range(2):
                    act.activation(dmat[:, k, :, 0], hd[:, 0, :], ACT.Exp, scale=steps[:, k:k + 1]).then_inc(aown, 1)
                act.wait_ge(aown, H + 3)
                for k in range(2):
                    for d in range(1, HD):
                        act.activation(dmat[:, k, :, d], dmat[:, k, :, 0], ACT.Copy).then_inc(aown, 1)

            @block.vector
            def _(dve):
                ch = Chain(dve, own)
                dve.wait_ge(e_ready, 1)
                ch(dve.tensor_scalar(hd[:, 0, :], hd[:, 0, :], 1.0e30, -1.0, ALU.min, ALU.mult))
                dve.tensor_scalar(hc[:, 0:1], hc[:, 0:1], 1.0e30, -1.0, ALU.min, ALU.mult).then_inc(m_ready, 1)
                dve.wait_ge(aown, H + 3)
                ch(dve.tensor_tensor(mask[:], mask[:], later[:].unsqueeze(1).broadcast_to([P, H, P]), ALU.mult))
                for h in range(H):
                    dve.scalar_tensor_tensor(mask[:, h, :], env.ident[:], hd[:, 1, h:h + 1], mask[:, h, :], ALU.mult,
                                             ALU.add).then_inc(own, 1)
                dve.wait_ge(own, H + 2)
        tiles = lambda x, s: x[:, ds(s * TILES, TILES)]
        with Stage(nc, "ri") as st:
            retention_inputs(nc, env, st, None, [
                (0, W["WrT"][:], "channels", None, ACT.Copy, lambda s: tiles(QK, s)[:, :, 0, :]),
                (1, W["WkT"][:], "channels", None, ACT.Copy, lambda s: tiles(QK, s)[:, :, 1, :]),
                (1, W["WkT"][:], "tokens", None, ACT.Copy, lambda s: tiles(KT, s)),
                (2, W["WvT"][:], "tokens", None, ACT.Copy, lambda s: tiles(V, s)),
                (3, W["WgT"][:], "tokens", None, ACT.Gelu, lambda s: tiles(G, s)),
            ], mixes=maa[:], pad=1)
        OUT = sw.sb("OUT", [P, B * TILES, D])
        with Stage(nc, "rr") as st:
            retention(nc, env, st, QK, KT, V, OUT, mask[:], dmat[:, 1].rearrange("p h d -> p (h d)"),
                      dmat[:, 0].rearrange("p h d -> p (h d)"), hc[:, 1:2])
        with Stage(nc, "rn") as st:
            head_norm_gate(nc, env, st, OUT, G, ln_w, ln_b)
        with Stage(nc, "ro") as st:
            add_projected(nc, env, st, Source(lambda s: OUT[:, ds(s * TILES, TILES), :], "p (j d) -> p j d", d=D), W["WoT"], None)


def head_norm_gate(nc, env, st, OUT, G, ln_w, ln_b):
    N = TILES * H
    y = st.sb("y", [P, 2, N, HD])
    sq = st.sb("sq", [P, 2, N, HD])
    s1, s2, half = st.sb("s1", [P, 2, N]), st.sb("s2", [P, 2, N]), st.sb("half", [P, N])
    own, sq_ready, ve_ready, rstd_ready, n_ready, p_own, done = (
        st.sem(n) for n in ("own", "sq_ready", "ve_ready", "rstd_ready", "n_ready", "p_own", "done"))
    y_ready, y_free, made = st.sem("y_ready"), st.sem("y_free"), st.sem("made")
    with nc.Block() as block:
        @block.vector
        def _(dve):
            dve.memset(half[:], -0.5).then_inc(made, 1)
            dve.sem_inc(y_free, 2)
            ch = Chain(dve, own)

            def body(s, u):
                ch.start(s * 3)
                o = OUT[:, ds(s * TILES, TILES), :].rearrange("p j (h d) -> p (j h) d", d=HD)
                dve.wait_ge(y_free, s + 1)
                ch(dve.tensor_reduce(s1[:, u, :], o, AX.X, ALU.add))
                ch(dve.tensor_scalar(s1[:, u, :], s1[:, u, :], 1.0 / HD, None, ALU.mult))
                dve.tensor_tensor(y[:, u], o, s1[:, u, :].unsqueeze(2).broadcast_to([P, N, HD]), ALU.subtract).then_inc(y_ready, 1)
                dve.wait_ge(sq_ready, s + 1)
                ch(dve.tensor_reduce(s2[:, u, :], sq[:, u], AX.X, ALU.add))
                dve.tensor_scalar(s2[:, u, :], s2[:, u, :], 1.0 / HD, RWKV_EPS, ALU.mult, ALU.add).then_inc(ve_ready, 1)
                dve.wait_ge(rstd_ready, s + 1)
                dve.tensor_tensor(y[:, u], y[:, u], s1[:, u, :].unsqueeze(2).broadcast_to([P, N, HD]), ALU.mult).then_inc(n_ready, 1)
            loop_batches(dve, body)

        @block.scalar
        def _(act):
            def body(s, u):
                act.wait_ge(y_ready, s + 1)
                act.activation(sq[:, u], y[:, u], ACT.Square).then_inc(sq_ready, 1)
            loop_batches(act, body)

        @block.gpsimd
        def _(pool):
            ch = Chain(pool, p_own)
            pool.wait_ge(made, 1)

            def body(s, u):
                ch.start(s * 3)
                pool.wait_ge(ve_ready, s + 1)
                pool.tensor_tensor(s1[:, u, :], s2[:, u, :], half[:], ALU.pow).then_inc(rstd_ready, 1)
                pool.wait_ge(n_ready, s + 1)
                v = y[:, u].rearrange("p (j h) d -> p j (h d)", h=H)
                ch(pool.tensor_tensor(v, v, ln_w[:].unsqueeze(1).broadcast_to([P, TILES, D]), ALU.mult))
                ch(pool.tensor_tensor(v, v, ln_b[:].unsqueeze(1).broadcast_to([P, TILES, D]), ALU.add))
                ch(pool.tensor_tensor(OUT[:, ds(s * TILES, TILES), :], v, G[:, ds(s * TILES, TILES), :], ALU.mult))
                pool.sem_inc(y_free, 1)
            loop_batches(pool, body)


def softmax_block_a(nc, env, i):
    QS = nc.dram_tensor("a_q_parts", [B, H, 2 * SPLITS, HD, T], BF16, kind="Internal").ap()
    KS = nc.dram_tensor("a_k_parts", [B, H, SPLITS, HD, T], BF16, kind="Internal").ap()
    KF = nc.dram_tensor("a_key_features", [SPLITS * HD, T], BF16, kind="Internal").ap()
    with Stage(nc, "aw") as sw:
        w = sw.sb("w", [P, 3 * D])
        wo = sw.sb("wo", [P, D])
        cols = sw.sb("cols", [P, 4])
        bv = sw.sb("bv", [P, D])
        bo = sw.sb("bo", [P, D])
        got = sw.sem("got")
        with nc.Block() as block:
            @block.sync
            def _(sp):
                bq = i["L0_attn_a_b_qkv"]
                n = load(sp, got, [(w[:], i["L0_attn_a_w_qkv"]), (wo[:], i["L0_attn_a_w_out"]),
                                   (cols[:, 0:1], column(bq[0:D])), (cols[:, 1:2], column(bq[D:2 * D])),
                                   (cols[:, 2:3], column(i["L0_attn_a_ln_g"])), (cols[:, 3:4], column(i["L0_attn_a_ln_b"])),
                                   (bv[:], bq[2 * D:3 * D].partition_broadcast(P)),
                                   (bo[:], i["L0_attn_a_b_out"].partition_broadcast(P))])
                sp.wait_ge(got, n)
        with Stage(nc, "ar") as st:
            relative_features(nc, env, st, i["L0_attn_a_w_rel"], QS, KF)
        VTOK = sw.sb("vtok", [P, HEADS, TILES, HD + 1])
        ATT = sw.sb("att", [P, HEADS, TILES, HD])
        with Stage(nc, "aq") as st:
            qkv_stage(nc, env, st, QS[:, :, 0:SPLITS], KS, VTOK, w, (cols[:, 0:1], cols[:, 1:2], bv[:]), True,
                      (cols[:, 2:3], cols[:, 3:4]))
        with Stage(nc, "aa") as st:
            env.recip_sem["aa"] = st.sem("recip")
            attention(nc, env, st, QS, KS, VTOK, ATT, 2 * SPLITS * HD, KF)
        with Stage(nc, "ao") as st:
            add_projected(nc, env, st, Source(
                lambda s: ATT[:, ds(s * H, H), :, :].rearrange("p h j d -> p j h d"),
                "p (j h d) -> p j h d", j=TILES, h=H), wo, bo)


def laid_out(inputs):
    out = {name: np.asarray(a) for name, a in inputs.items()}
    out["b1_cols"] = out.pop("L0_ffn_b1").reshape(EXPERTS, HK, P).transpose(0, 2, 1)
    out["router_wT"] = out.pop("L0_ffn_router_w").T
    out["lora_aT"] = out.pop("L1_ffn_a").T
    for n in ("Wr", "Wk", "Wv", "Wg", "Wo"):
        out[f"{n}T"] = out.pop(f"L1_attn_b_{n}").T
    return out




def kernel(**inputs):
    import numpy as _np
    import concourse.bacc as _bacc
    from concourse import mybir as _mybir
    from concourse.bass_utils import run_bass_kernel_spmd as _run

    nc = _bacc.Bacc("TRN2", target_bir_lowering=False, num_devices=1)
    arrays, args = {}, {}
    for name, a in {**laid_out(inputs), **constants()}.items():
        a = _np.ascontiguousarray(a)
        arrays[f"in_{name}"] = a
        args[name] = nc.dram_tensor(f"in_{name}", a.shape, _mybir.dt.from_np(a.dtype), kind="ExternalInput").ap()
    out = nc.dram_tensor("out_0", (B, T, D), _mybir.dt.float32, kind="ExternalOutput").ap()
    build(nc, args, out)
    r = _run(nc, [arrays], core_ids=[0])
    return r.results[0]["out_0"]
```

```python
from contextlib import ExitStack

import numpy as np
import concourse.bass as bass
from concourse import mybir

P = 128
B, T, D = 4, 1024, 128
TILES = T // P
H, HD = 16, 8
HEADS = B * H
EXPERTS, HIDDEN = 8, 512
HK = HIDDEN // P
CAPACITY = int(T * 2.0 / EXPERTS) + 1
K_KEEP, RECENCY = 391, 64
LN_EPS = 1e-5
RWKV_EPS = 1e-5 * 64
DECAY = 0.95
QSCALE = HD ** -0.5
SPLITS = 6
PART_Q = [0, 0, 1, 1, 0, 2]
PART_K = [0, 1, 0, 1, 2, 0]
SHIFT_ROWS = 2
TAKEN = -3.0e38
MASKED = -1.0e20

ALU = mybir.AluOpType
ACT = mybir.ActivationFunctionType
AX = mybir.AxisListType
F32 = mybir.dt.float32
BF16 = mybir.dt.bfloat16
ds = bass.ds


class Chain:

    def __init__(self, eng, sem):
        self.eng, self.sem, self.base, self.n = eng, sem, 0, 0

    def start(self, base):
        self.base, self.n = base, 0

    def __call__(self, ins, alone=False):
        self.n += 1
        ins.then_inc(self.sem, 1)
        (wait_alone if alone else type(self.eng).wait_ge)(self.eng, self.sem, self.base + self.n)


def wait_alone(eng, sem, value):
    eng.wait_ge(sem, value)
    if not isinstance(value, int):
        eng.sem_inc(Passed.sem, 1)


class Passed:

    sem = None


class Stage:

    def __init__(self, nc, name):
        self.nc, self.name, self.stack, self.sems = nc, name, ExitStack(), []

    def sb(self, name, shape, dt=F32):
        return self.stack.enter_context(self.nc.sbuf_tensor(f"{self.name}_{name}", shape, dt))

    def ps(self, name, shape, dt=F32):
        return self.stack.enter_context(self.nc.psum_tensor(f"{self.name}_{name}", shape, dt))

    def sem(self, name):
        self.sems.append(self.nc.alloc_semaphore(f"{self.name}_{name}"))
        return self.sems[-1]

    def __enter__(self):
        return self

    def __exit__(self, *a):
        with self.nc.Block() as block:
            @block.gpsimd
            def _(pool):
                for sem in self.sems:
                    pool.sem_clear(sem)
        for sem in self.sems:
            self.nc.release_semaphore(sem)
        self.stack.close()


def batch(x, s):
    return x[:, ds(s * T, T)].rearrange("p (j d) -> p j d", d=D)


class Norm:

    def __init__(self, st, env, again=False, affine=None, pad=0):
        self.env, self.again, self.affine, self.pad = env, again, affine, pad
        self.stats = st.sb("ln_stats", [P, 2, TILES, 6])
        self.mv = st.sb("ln_mv", [P, 2, TILES, 2])
        self.ve = st.sb("ln_ve", [P, 2, TILES])
        self.rstd = st.sb("ln_rstd", [P, 2, TILES])
        self.mv2 = st.sb("ln_mv2", [P, 2, TILES, 2])
        self.ve2 = st.sb("ln_ve2", [P, 2, TILES])
        self.rstd2 = st.sb("ln_rstd2", [P, 2, TILES])
        self.y = st.sb("ln_y", [P, 2, TILES, D])
        self.xT = st.sb("ln_xT", [P, 2, T + pad])
        self.psT = st.ps("ln_psT", [P, T])
        self.dve = st.sem("ln_dve")
        self.pool = st.sem("ln_pool")
        self.var_ready = st.sem("ln_var_ready")
        self.rstd_ready = st.sem("ln_rstd_ready")
        self.y_ready = st.sem("ln_y_ready")
        self.y_free = st.sem("ln_y_free")
        self.t_ready = st.sem("ln_t_ready")
        self.xt_ready = st.sem("ln_xt_ready")
        self.xt_free = st.sem("ln_xt_free")
        self.per = 3 if again else 1

    def credits(self, vector):
        vector.sem_inc(self.y_free, 2)
        vector.sem_inc(self.xt_free, 2)

    def vector(self, v, s, u, saved=None):
        rounds = 2 if self.again else 1
        ch = Chain(v, self.dve)
        ch.start(s * self.per)
        v.wait_ge(self.y_free, s + 1)
        if saved is not None:
            v.wait_ge(saved, s + 1)
        xb = batch(self.env.X, s)
        y = self.y[:, u]
        for r in range(rounds):
            src, mv, rs = (xb, self.mv, self.rstd) if r == 0 else (y, self.mv2, self.rstd2)
            for j in range(TILES):
                ins = v.bn_stats(self.stats[:, u, j, :], src[:, j, :])
            ch(ins, alone=True)
            for j in range(TILES):
                ins = v.bn_aggr(mv[:, u, j, :], self.stats[:, u, j, :])
            ins.then_inc(self.var_ready, 1)
            v.wait_ge(self.rstd_ready, s * rounds + r + 1)
            v.wait_ge(self.var_ready, s * rounds + r + 1)
            for j in range(TILES):
                ins = v.tensor_scalar(y[:, j, :], src[:, j, :], mv[:, u, j, 0:1], rs[:, u, j:j + 1],
                                      ALU.subtract, ALU.mult)
            if r + 1 < rounds:
                ch(ins)
        ins.then_inc(self.y_ready, 1)

    def gpsimd(self, g, s, u):
        rounds = 2 if self.again else 1
        ch = Chain(g, self.pool)
        ch.start(s * rounds)
        for r in range(rounds):
            mv, ve, rs = (self.mv, self.ve, self.rstd) if r == 0 else (self.mv2, self.ve2, self.rstd2)
            wait_alone(g, self.var_ready, s * rounds + r + 1)
            ch(g.tensor_scalar(ve[:, u, :], mv[:, u, :, 1], LN_EPS, None, ALU.add))
            g.tensor_tensor(rs[:, u, :], ve[:, u, :], self.env.minus_half[:, 0:TILES],
                            ALU.pow).then_inc(self.rstd_ready, 1)

    def tensor(self, t, s, u, psT_free=None):
        t.wait_ge(self.y_ready, s + 1)
        if psT_free is None:
            t.wait_ge(self.xt_ready, s)
        else:
            t.wait_ge(psT_free, s)
        for j in range(TILES):
            ins = t.transpose(self.psT[:, j * P:(j + 1) * P], self.y[:, u, j, :], self.env.ident[:])
        ins.then_inc(self.t_ready, 1)

    def scalar(self, a, s, u):
        a.wait_ge(self.t_ready, s + 1)
        a.wait_ge(self.xt_free, s + 1)
        a.sem_inc(self.y_free, 1)
        out = self.xT[:, u, self.pad:self.pad + T]
        if self.affine is None:
            a.activation(out, self.psT[:], ACT.Copy).then_inc(self.xt_ready, 1)
        else:
            gain, offset = self.affine
            a.activation(out, self.psT[:], ACT.Identity, bias=offset, scale=gain).then_inc(self.xt_ready, 1)


def loop_batches(eng, body):
    with eng.Fori(0, B // 2) as i:
        for u in range(2):
            body(i * 2 + u, u)


def loop_ahead(eng, ahead, body):
    ahead(0, 0)
    with eng.Fori(0, B // 2 - 1) as i:
        for u in range(2):
            ahead(i * 2 + u + 1, 1 - u)
            body(i * 2 + u, u)
    ahead(B - 1, 1)
    body(B - 2, 0)
    body(B - 1, 1)


def loop_after(eng, ahead, body):
    with eng.Fori(0, B // 2) as i:
        for u in range(2):
            ahead(i * 2 + u, u)
            body(i * 2 + u, u)


def load(eng, sem, pairs):
    for dst, src in pairs:
        eng.dma_start(dst, src).then_inc(sem, 16)
    return 16 * len(pairs)


def column(v):
    return v.rearrange("(p o) -> p o", o=1)


def add_projected(nc, env, st, src, w, bias):
    a = st.sb("po_in", [P, 2, T])
    aT = st.sb("po_inT", [P, 2, T])
    psT = st.ps("po_psT", [P, T])
    psY = st.ps("po_psY", [P, T])
    in_ready, in_free = st.sem("po_in_ready"), st.sem("po_in_free")
    t_ready, t_done, y_ready, y_free = (st.sem(f"po_{n}") for n in ("t_ready", "t_done", "y_ready", "y_free"))
    bias_done, bias_own = st.sem("po_bias_done"), st.sem("po_own")
    with nc.Block() as block:
        @block.scalar
        def _(act):
            act.sem_inc(in_free, 2)

            def body(s, u):
                act.wait_ge(in_free, s + 1)
                act.activation(a[:, u, :].rearrange(src.form, **src.sizes), src(s), ACT.Copy).then_inc(in_ready, 1)
                act.wait_ge(t_ready, s + 1)
                act.sem_inc(in_free, 1)
                act.activation(aT[:, u, :], psT[:], ACT.Copy).then_inc(t_done, 1)
            loop_batches(act, body)

        @block.gpsimd
        def _(pool):
            if bias is not None:
                def body(s, u):
                    xb = batch(env.X, s)
                    pool.tensor_tensor(xb, xb, bias[:].unsqueeze(1).broadcast_to([P, TILES, D]),
                                       ALU.add).then_inc(bias_done, 1)
                loop_batches(pool, body)

        @block.tensor
        def _(pe):
            def body(s, u):
                pe.wait_ge(in_ready, s + 1)
                pe.wait_ge(t_done, s)
                for j in range(TILES):
                    ins = pe.transpose(psT[:, j * P:(j + 1) * P], a[:, u, j * P:(j + 1) * P], env.ident[:])
                ins.then_inc(t_ready, 1)
                pe.wait_ge(t_done, s + 1)
                pe.wait_ge(y_free, s)
                for j in range(TILES):
                    ins = pe.matmul(psY[:, j * P:(j + 1) * P], aT[:, u, j * P:(j + 1) * P], w[:],
                                    start=True, stop=True)
                ins.then_inc(y_ready, 1)
            loop_batches(pe, body)

        @block.vector
        def _(dve):
            def body(s, u):
                dve.wait_ge(y_ready, s + 1)
                if bias is not None:
                    dve.wait_ge(bias_done, s + 1)
                xb = batch(env.X, s)
                dve.tensor_tensor(xb, psY[:].rearrange("p (j d) -> p j d", d=D), xb, ALU.add).then_inc(y_free, 1)
            loop_batches(dve, body)


class Source:
    def __init__(self, f, form, **sizes):
        self.f, self.form, self.sizes = f, form, sizes

    def __call__(self, s):
        return self.f(s)


def qkv_stage(nc, env, st, QS, KS, VTOK, w_qkv, biases, again, affine, LASTD=None):
    nm = Norm(st, env, again=again, affine=affine)
    full = st.sb("full", [P, 2, T])
    rest = st.sb("rest", [P, 2, T])
    part = st.sb("part", [P, 2, 3, T], BF16)
    psQK = st.ps("psQK", [P, 2, T])
    psV = st.ps("psV", [P, T])
    own = st.sem("own")
    qk_ready, qk_taken = st.sem("qk_ready"), st.sem("qk_taken")
    high_ready, rest_ready, mid_ready, low_ready = (st.sem(n) for n in ("high_ready", "rest_ready", "mid_ready", "low_ready"))
    stored = [st.sem("stored_q"), st.sem("stored_k")]
    v_ready, v_taken = st.sem("v_ready"), st.sem("v_taken")
    if LASTD is not None:
        ql = st.sb("ql", [P, H])
        last_sb = st.sb("last_sb", [H, 2, T])
        ql_ready, last_ready, last_taken, last_stored = (st.sem(n) for n in ("ql_ready", "last_ready", "last_taken", "last_stored"))
        last_free = st.sem("last_free")
    with nc.Block() as block:
        @block.vector
        def _(dve):
            nm.credits(dve)

            def body(s, u):
                for c in range(2):
                    dve.wait_ge(qk_ready, s * 2 + c + 1)
                    dve.wait_ge(low_ready, s * 2)
                    mul = QSCALE if c == 0 else 1.0
                    if biases is not None:
                        ins = dve.tensor_scalar(full[:, c, :], psQK[:, c, :], biases[c], mul, ALU.add, ALU.mult)
                    else:
                        ins = dve.tensor_scalar(full[:, c, :], psQK[:, c, :], mul, None, ALU.mult)
                    ins.then_inc(qk_taken, 1)
                if LASTD is not None:
                    dve.wait_ge(qk_taken, s * 2 + 2)
                    dve.wait_ge(last_ready, s)
                    dve.tensor_scalar(ql[:], env.blk[:], full[:, 0, T - 1:T], None, ALU.mult).then_inc(ql_ready, 1)
                for c in range(2):
                    dve.wait_ge(high_ready, s * 2 + c + 1)
                    dve.wait_ge(qk_taken, s * 2 + c + 1)
                    dve.tensor_tensor(rest[:, c, :], full[:, c, :], part[:, c, 0, :],
                                      ALU.subtract).then_inc(rest_ready, 1)
                for c in range(2):
                    dve.wait_ge(mid_ready, s * 2 + c + 1)
                    dve.wait_ge(rest_ready, s * 2 + c + 1)
                    dve.wait_ge(stored[c], s * 16 * SPLITS)
                    dve.tensor_tensor(part[:, c, 2, :], rest[:, c, :], part[:, c, 1, :],
                                      ALU.subtract).then_inc(low_ready, 1)
                dve.wait_ge(v_ready, s + 1)
                out = VTOK[:, ds(s * H, H), :, 0:HD].rearrange("p h j d -> p j h d")
                src = psV[:].rearrange("p (j h d) -> p j h d", j=TILES, h=H)
                if biases is not None:
                    for j in range(TILES):
                        ins = dve.tensor_tensor(out[:, j], src[:, j], biases[2].rearrange("p (h d) -> p h d", h=H), ALU.add)
                else:
                    ins = dve.tensor_copy(out, src)
                ins.then_inc(v_taken, 1)
            loop_ahead(dve, lambda s, u: nm.vector(dve, s, u), body)

        @block.gpsimd
        def _(pool):
            pool.memset(VTOK[:, :, :, HD:HD + 1], 1.0).then_inc(own, 1)
            loop_batches(pool, lambda s, u: nm.gpsimd(pool, s, u))
            pool.wait_ge(own, 1)

        @block.tensor
        def _(pe):
            def body(s, u):
                pe.wait_ge(nm.xt_ready, s + 1)
                for c in range(2):
                    pe.wait_ge(qk_taken, s * 2)
                    for n in range(2):
                        ins = pe.matmul(psQK[:, c, n * 512:(n + 1) * 512], w_qkv[:, c * D:(c + 1) * D],
                                        nm.xT[:, u, n * 512:(n + 1) * 512], start=True, stop=True)
                    ins.then_inc(qk_ready, 1)
                pe.wait_ge(v_taken, s)
                for j in range(TILES):
                    ins = pe.matmul(psV[:, j * D:(j + 1) * D], nm.xT[:, u, j * P:(j + 1) * P],
                                    w_qkv[:, 2 * D:3 * D], start=True, stop=True)
                ins.then_inc(v_ready, 1)
                if LASTD is not None:
                    pe.wait_ge(ql_ready, s + 1)
                    for n in range(2):
                        ins = pe.matmul(nm.psT[0:H, n * 512:(n + 1) * 512], ql[:], full[:, 1, n * 512:(n + 1) * 512],
                                        start=True, stop=True)
                    ins.then_inc(last_ready, 1)
            if LASTD is None:
                loop_ahead(pe, lambda s, u: nm.tensor(pe, s, u), body)
            else:
                loop_after(pe, lambda s, u: nm.tensor(pe, s, u, psT_free=last_taken), body)

        @block.scalar
        def _(act):
            if LASTD is not None:
                act.sem_inc(last_free, 2)

            def body(s, u):
                for c in range(2):
                    act.wait_ge(qk_taken, s * 2 + c + 1)
                    act.wait_ge(stored[c], s * 16 * SPLITS)
                    act.activation(part[:, c, 0, :], full[:, c, :], ACT.Copy).then_inc(high_ready, 1)
                for c in range(2):
                    act.wait_ge(rest_ready, s * 2 + c + 1)
                    act.activation(part[:, c, 1, :], rest[:, c, :], ACT.Copy).then_inc(mid_ready, 1)
                act.wait_ge(v_ready, s + 1)
                act.sem_inc(nm.xt_free, 1)
                if LASTD is not None:
                    act.wait_ge(last_ready, s + 1)
                    act.wait_ge(last_free, s + 1)
                    act.activation(last_sb[:, u, :], nm.psT[0:H, :], ACT.Copy).then_inc(last_taken, 1)
            (loop_ahead if LASTD is None else loop_after)(act, lambda s, u: nm.scalar(act, s, u), body)

        @block.sync
        def _(sp):
            def body(s, u):
                for c, (dst, parts) in enumerate(((QS, PART_Q), (KS, PART_K))):
                    wait_alone(sp, low_ready, s * 2 + c + 1)
                    for n, p in enumerate(parts):
                        out = dst[ds(s, 1), :, n, :, :].rearrange("b h d t -> (b h) d t")
                        sp.dma_start(out, part[:, c, p, :]).then_inc(stored[c], 16)
                if LASTD is not None:
                    wait_alone(sp, last_taken, s + 1)
                    sp.dma_start(LASTD[ds(s, 1), :, :].rearrange("b h t -> (b h) t"),
                                 last_sb[:, u, :]).then_inc(last_stored, 16)
                for sem in stored:
                    wait_alone(sp, sem, s * 16 * SPLITS + 16 * SPLITS)
                if LASTD is not None:
                    wait_alone(sp, last_stored, s * 16 + 16)
                    sp.sem_inc(last_free, 1)
            loop_batches(sp, body)


def attention(nc, env, st, QS, KS, VTOK, ATT, rows, setup_k, mask_rows=None):
    SLOTS = 4
    full = rows + SHIFT_ROWS
    qt = st.sb("qt", [P, SLOTS, T], BF16)
    kt = st.sb("kt", [P, SLOTS, T], BF16)
    e = st.sb("e", [P, 2 * TILES, 512])
    vh = st.sb("vh", [P, 2, TILES, 32])
    partial = st.sb("partial", [P, 2, TILES])
    m2 = st.sb("m2", [P, 2, 2 * TILES], BF16)
    mrow = st.sb("mrow", [2 * TILES, 2, P], BF16)
    ot = st.sb("ot", [P, 2, 512])
    rden = st.sb("rden", [P, 2, TILES])
    psA = st.ps("psA", [P, 2, T])
    psS = st.ps("psS", [P, 3, 512])
    psO = st.ps("psO", [P, 512])
    AHEAD = 2 * TILES + 1
    PER = TILES + 1
    TURN = 2
    k_rows = KS.shape[2] * KS.shape[3]
    q_rows = QS.shape[2] * QS.shape[3]
    loads = 2 + (mask_rows is not None)
    loaded = [st.sem(f"loaded{k}") for k in range(SLOTS)]
    shifted = [st.sem(f"shifted{k}") for k in range(SLOTS)]
    head_free = st.sem("head_free")
    a_ready, a_taken = st.sem("a_ready"), st.sem("a_taken")
    m2_ready, mrow_ready = st.sem("m2_ready"), st.sem("mrow_ready")
    s_ready, e_ready = st.sem("s_ready"), st.sem("e_ready")
    av_done, ot_ready, tok_ready, norm_done = (st.sem(n) for n in ("av_done", "ot_ready", "tok_ready", "norm_done"))
    vh_ready, own_d, own_p = st.sem("vh_ready"), st.sem("own_d"), st.sem("own_p")
    filled = [st.sem(f"filled{k}") for k in range(SLOTS)]
    qsrc = QS.rearrange("b h s d t -> (b h) (s d) t")
    ksrc = KS.rearrange("b h s d t -> (b h) (s d) t")
    TURNS = HEADS // SLOTS

    def at(i, u, delta):
        return (u + delta) % SLOTS, i + (u + delta) // SLOTS

    def fill_slot(eng, k):
        ch = Chain(eng, filled[k])
        for x in (qt, kt):
            ch(eng.memset(x[0:96, k], 0.0))
            ch(eng.memset(x[96:P, k], 1.0))

    def turns(eng, body):
        body(0, True, False)
        with eng.Fori(1, TURNS - 1) as i:
            body(i, False, False)
        body(TURNS - 1, False, True)

    with nc.Block() as block:
        @block.sync
        def _(sp):
            def fetch(i, u, wait, fill=False):
                n = i * SLOTS + u
                if fill:
                    sp.wait_ge(filled[u], 4)
                    if setup_k is not None:
                        sp.dma_start(kt[k_rows:rows, u, :], setup_k).then_inc(filled[u], 16)
                        sp.wait_ge(filled[u], 4 + 16)
                if wait:
                    wait_alone(sp, head_free, n - SLOTS + 1)
                sp.dma_start(qt[0:q_rows, u, :], qsrc[ds(n, 1)].rearrange("a r t -> (a r) t")).then_inc(loaded[u], 16)
                sp.dma_start(kt[0:k_rows, u, :], ksrc[ds(n, 1)].rearrange("a r t -> (a r) t")).then_inc(loaded[u], 16)
                if mask_rows is not None:
                    sp.dma_start(kt[rows - 1:rows, u, :], mask_rows[ds(n, 1), :]).then_inc(loaded[u], 16)

            fetch(0, 0, False, True)

            def body(i, first, last):
                for u in range(SLOTS):
                    if not (last and u == SLOTS - 1):
                        u1, i1 = at(i, u, 1)
                        in_front = first and u + 1 < SLOTS
                        fetch(i1, u1, not in_front, in_front)
                    wait_alone(sp, mrow_ready, i * SLOTS + u + 1)
                    for r in range(SHIFT_ROWS):
                        sp.dma_start(qt[rows + r:rows + r + 1, u, :].rearrange("o (a t) -> o a t", a=TILES),
                                     mrow[r * TILES:(r + 1) * TILES, u % 2, :]).then_inc(shifted[u], 16)
            turns(sp, body)

        @block.gpsimd
        def _(pool):
            pool.memset(vh[:], 0.0).then_inc(own_p, 1)
            pool.wait_ge(own_p, 1)

            def fill(n, par, wait):
                if wait:
                    pool.wait_ge(av_done, n * 4 - 4)
                pool.tensor_copy(vh[:, par, :, 0:HD + 1],
                                 VTOK[:, ds(n, 1), :, :].rearrange("p n j d -> p (n j) d")).then_inc(vh_ready, 1)
            fill_slot(pool, 1)
            fill(0, 0, False)
            fill(1, 1, False)
            fill_slot(pool, 2)
            fill_slot(pool, 3)
            with pool.Fori(1, HEADS // 2) as i:
                for par in range(2):
                    fill(i * 2 + par, par, True)

        @block.tensor
        def _(pe):
            def psA_free(use):
                if not (isinstance(use, int) and use < 2):
                    pe.wait_ge(a_taken, use - 1)

            def first_pass(i, u, j, use, slot):
                if j == 0:
                    pe.wait_ge(loaded[u], (i + 1) * 16 * loads)
                psA_free(use)
                for c in range(2):
                    ins = pe.matmul(psA[:, slot, c * 512:(c + 1) * 512], qt[0:rows, u, j * P:(j + 1) * P],
                                    kt[0:rows, u, c * 512:(c + 1) * 512], start=True, stop=True)
                ins.then_inc(a_ready, 1)

            def turn_max(n, par, use, slot):
                pe.wait_ge(m2_ready, n + 1)
                psA_free(use)
                pe.transpose(psA[0:2 * TILES, slot, 0:P // 2].bitcast(BF16), m2[:, par, :], env.identb[:]).then_inc(a_ready, 1)

            def second_pass(i, u, c):
                k = i * SLOTS + u
                if c == 0:
                    pe.wait_ge(shifted[u], (i + 1) * 16 * SHIFT_ROWS)
                turn = 16 * u + c
                if turn == 0:
                    if not isinstance(k, int) or k > 0:
                        pe.wait_ge(e_ready, k * 16)
                elif not isinstance(k, int) or k * 16 + c > 2:
                    pe.wait_ge(e_ready, k * 16 + c - 2)
                j, q = c // 2, c % 2
                ins = pe.matmul(psS[:, turn % 3, :], kt[0:full, u, j * P:(j + 1) * P],
                                qt[0:full, u, q * 512:(q + 1) * 512], start=True, stop=True)
                ins.then_inc(s_ready, 1)

            def sums(k, par, part):
                pe.wait_ge(e_ready, k * 16 + 4 * part + 4)
                if part == 0:
                    pe.wait_ge(vh_ready, k + 1)
                for j in range(part * 2, part * 2 + 2):
                    for q in range(2):
                        g = 2 * (j % 2) + q
                        ins = pe.matmul(psO[32 * g:32 * g + 32, :], vh[:, par, j, :], e[:, 2 * j + q, :],
                                        start=(j < 2), stop=(j >= 6))
                ins.then_inc(av_done, 1)

            def to_tokens(k, par):
                pe.wait_ge(ot_ready, k + 1)
                for j in range(TILES // 2):
                    ins = pe.matmul(psO[:, j * 32:j * 32 + 2 * (HD + 1)], ot[:, par, j * P:(j + 1) * P],
                                    env.sel[:], start=True, stop=True)
                ins.then_inc(tok_ready, 1)

            for j in range(TILES):
                first_pass(0, 0, j, j, j % 2)
            turn_max(0, 0, TILES, TILES % 2)
            for j in range(TILES):
                first_pass(0, 1, j, TILES + 1 + j, (TILES + 1 + j) % 2)

            def body(i, first, last):
                for u in range(SLOTS):
                    k = i * SLOTS + u
                    u2, i2 = at(i, u, 2)
                    use, slot = k * PER + AHEAD, (u * PER + AHEAD) % 2
                    if last and u == 2:
                        turn_max(k + 1, (u + 1) % 2, use, slot)
                    for c in range(16):
                        second_pass(i, u, c)
                        if c == 15:
                            pe.wait_ge(s_ready, k * 16 + 16)
                            pe.sem_inc(head_free, 1)
                        if c in (2, 4) and not (first and u == 0):
                            sums(k - 1, (u - 1) % 2, 2 + (c == 4))
                        if c == 7 and not (first and u == 0):
                            to_tokens(k - 1, (u - 1) % 2)
                        if c in (10, 13):
                            if c == 10 and not (first and u == 0):
                                pe.wait_ge(norm_done, k)
                            sums(k, u % 2, int(c == 13))
                        if c % 2 == 1 and not (last and u >= 2):
                            j = c // 2
                            first_pass(i2, u2, j, use + j + (j > TURN), (slot + j + (j > TURN)) % 2)
                            if j == TURN:
                                turn_max(k + 1, (u + 1) % 2, use + j + 1, (slot + j + 1) % 2)
            turns(pe, body)
            sums(HEADS - 1, 1, 2)
            sums(HEADS - 1, 1, 3)
            to_tokens(HEADS - 1, 1)

        @block.vector
        def _(dve):
            def maxima(par, j, use, slot):
                dve.wait_ge(a_ready, use + 1)
                dve.tensor_reduce(partial[:, par, j:j + 1], psA[:, slot, :], AX.X, ALU.max,
                                  negate=True).then_inc(a_taken, 1)

            def shift_parts(n, par, last_use):
                dve.wait_ge(a_taken, last_use + 1)
                dve.tensor_copy(m2[:, par, 0:TILES], partial[:, par, :]).then_inc(own_d, 1)
                dve.wait_ge(own_d, n + 1)
                dve.tensor_tensor(m2[:, par, TILES:2 * TILES], partial[:, par, :], m2[:, par, 0:TILES],
                                  ALU.subtract).then_inc(m2_ready, 1)

            def shift_row(i, u, wait, use, slot):
                dve.wait_ge(a_ready, use + 1)
                if wait:
                    u0, i0 = at(i, u, -2)
                    dve.wait_ge(shifted[u0], (i0 + 1) * 16 * SHIFT_ROWS)
                dve.tensor_copy(mrow[:, u % 2, :], psA[0:2 * TILES, slot, 0:P // 2].bitcast(BF16)).then_inc(a_taken, 1)
                dve.wait_ge(a_taken, use + 1)
                dve.sem_inc(mrow_ready, 1)

            recip_done = env.recip_sem[st.name]

            def normalise(k, par):
                tok = psO[:, 0:32 * (TILES // 2)].rearrange("p (j x) -> p j x", x=32)[:, :, 0:2 * (HD + 1)].rearrange(
                    "p j (q d) -> p j q d", q=2)
                rd = rden[:, par, :].rearrange("p (j q) -> p j q", q=2)
                dve.wait_ge(tok_ready, k + 1)
                dve.reciprocal(rd, tok[:, :, :, HD]).then_inc(recip_done, 1)
                dve.wait_ge(recip_done, k + 1)
                out = ATT[:, ds(k, 1), :, :].rearrange("p n (q j) d -> p (n j) q d", q=2)
                for q in range(2):
                    ins = dve.tensor_tensor(out[:, :, q], tok[:, :, q, 0:HD],
                                            rd[:, :, q].unsqueeze(2).broadcast_to([P, TILES // 2, HD]), ALU.mult)
                ins.then_inc(norm_done, 1)

            fill_slot(dve, 0)
            for j in range(TILES):
                maxima(0, j, j, j % 2)
            shift_parts(0, 0, TILES - 1)
            shift_row(0, 0, False, TILES, TILES % 2)
            for j in range(TILES):
                maxima(1, j, TILES + 1 + j, (TILES + 1 + j) % 2)
            shift_parts(1, 1, 2 * TILES)

            def body(i, first, last):
                for u in range(SLOTS):
                    k = i * SLOTS + u
                    use, slot = k * PER + AHEAD, (u * PER + AHEAD) % 2
                    u1, i1 = at(i, u, 1)
                    if last and u == 2:
                        shift_row(i1, u1, True, use, slot)
                    for j in range(TILES):
                        if not (last and u >= 2):
                            maxima(u % 2, j, use + j + (j > TURN), (slot + j + (j > TURN)) % 2)
                            if j == TURN:
                                shift_row(i1, u1, not (first and u == 0), use + j + 1, (slot + j + 1) % 2)
                        if j == TURN and not (first and u == 0):
                            normalise(k - 1, (u - 1) % 2)
                    if not (last and u >= 2):
                        shift_parts(k + 2, u % 2, use + TILES)
            turns(dve, body)
            normalise(HEADS - 1, 1)

        @block.scalar
        def _(act):
            def exps(k, u, c):
                act.wait_ge(s_ready, k * 16 + c + 1)
                if c % 4 == 0 and not (isinstance(k, int) and k == 0):
                    act.wait_ge(av_done, k * 4 - 3 + c // 4)
                act.activation(e[:, c, :], psS[:, (16 * u + c) % 3, :], ACT.Exp).then_inc(e_ready, 1)

            def take_sums(k, par, wait):
                act.wait_ge(av_done, k * 4 + 4)
                if wait:
                    act.wait_ge(tok_ready, k - 1)
                act.activation(ot[:, par, :], psO[:], ACT.Copy).then_inc(ot_ready, 1)

            def body(i, first, last):
                for u in range(SLOTS):
                    k = i * SLOTS + u
                    for c in range(16):
                        exps(k, u, c)
                        if c == 4 and not (first and u == 0):
                            take_sums(k - 1, (u - 1) % 2, not (first and u < 3))
            turns(act, body)
            take_sums(HEADS - 1, 1, True)





def constants():
    c = {}
    c["ident"] = np.eye(P, dtype=np.float32)
    c["flip"] = c["ident"][::-1].copy()
    p = np.arange(P)
    c["blk"] = (p[:, None] // HD == np.arange(H)[None, :]).astype(np.float32)
    c["own_columns"] = (p[None, :] % 32 // HD == np.arange(32 // HD)[:, None]).astype(np.float32)
    c["blk2"] = (p[:, None] // HD == p[None, :] // HD).astype(np.float32)
    col = np.arange(2 * (HD + 1))[None, :]
    c["sel"] = ((p[:, None] % 32 == col % (HD + 1)) & (p[:, None] // 32 % 2 == col // (HD + 1))).astype(np.float32)
    div = np.exp(np.arange(0, HD, 2, dtype=np.float32) * np.float32(-np.log(10000.0) / HD)).astype(np.float32)
    ang = np.arange(T, dtype=np.float64)[None, :] * div.astype(np.float64)[:, None]
    table = np.stack([np.sin(ang), np.cos(ang)], 1).reshape(HD, T).astype(np.float32)
    c["table"] = table
    feat = np.stack([np.cos(ang), np.sin(ang)], 1).reshape(HD, T).astype(np.float32)
    c["features"] = feat
    m1, m2 = np.zeros((HD, HD), np.float32), np.zeros((HD, HD), np.float32)
    for m in range(HD // 2):
        m1[2 * m, 2 * m] = m1[2 * m + 1, 2 * m] = 1
        m2[2 * m + 1, 2 * m + 1] = -1
        m2[2 * m, 2 * m + 1] = 1
    c["m12"] = np.stack([m1, m2], 1)
    i, j = np.arange(P)[None, :], np.arange(P)[:, None]
    c["decay_mask"] = np.where(i >= j, np.exp((i - j) * np.log(DECAY)), 0).astype(np.float32)
    c["decay_cols"] = np.stack([DECAY ** (np.arange(P) + 1.0), DECAY ** (P - 1.0 - np.arange(P))], 1).astype(np.float32)
    row = np.arange(2 * B * EXPERTS)
    c["row_base"] = (row % (B * EXPERTS) // EXPERTS * T + row // (B * EXPERTS) * (T // 2)).astype(np.float32)[:, None]
    c["lag"] = np.maximum(i - j - 1, 0).astype(np.float32)
    c["later"] = (i > j).astype(np.float32)
    c["steps"] = np.stack([np.arange(P), P - 1 - np.arange(P)], 1).astype(np.float32)
    return c


def relative_features(nc, env, st, w_rel, QS, key_features):
    wr = st.sb("wr", [HD, 2, H])
    lhs = st.sb("lhs", [HD, H, HD])
    tmp = st.sb("tmp", [HD, H, HD])
    table = st.sb("table", [HD, T])
    m12 = st.sb("m12", [HD, 2, HD])
    full = st.sb("full", [P, T])
    rest = st.sb("rest", [P, T])
    part = st.sb("part", [P, 3, T], BF16)
    kf = st.sb("kf", [HD, 2, T])
    kpart = st.sb("kpart", [HD, 3, T], BF16)
    got, own, made, stored = (st.sem(n) for n in ("got", "own", "made", "stored"))
    with Stage(nc, "rp") as inner:
        ps = inner.ps("ps", [P, T])
        with nc.Block() as block:
            @block.sync
            def _(sp):
                sp.dma_start(kf[:, 0, :], env.dram["features"]).then_inc(got, 16)
                sp.dma_start(wr[:, 0, :], w_rel).then_inc(got, 16)
                for m in range(HD):
                    sp.dma_start(wr[m:m + 1, 1, :], w_rel[m ^ 1:(m ^ 1) + 1, :]).then_inc(got, 16)
                sp.dma_start(table[:], env.dram["table"]).then_inc(got, 16)
                sp.dma_start(m12[:], env.dram["m12"]).then_inc(got, 16)
                sp.wait_ge(own, 8)
                for b in range(B):
                    for n, p in enumerate(PART_Q):
                        sp.dma_start(QS[b, :, SPLITS + n, :, :], part[:, p, :]).then_inc(stored, 16)
                sp.wait_ge(own, 12)
                for n, p in enumerate(PART_K):
                    sp.dma_start(key_features[n * HD:(n + 1) * HD, :], kpart[:, p, :]).then_inc(stored, 16)

            @block.vector
            def _(dve):
                ch = Chain(dve, own)
                dve.wait_ge(got, 16 * (HD + 4))
                a = lambda k: wr[:, k, :].unsqueeze(2).broadcast_to([HD, H, HD])
                m = lambda k: m12[:, k, :].unsqueeze(1).broadcast_to([HD, H, HD])
                ch(dve.tensor_tensor(lhs[:], a(0), m(0), ALU.mult))
                ch(dve.tensor_tensor(tmp[:], a(1), m(1), ALU.mult))
                ch(dve.tensor_tensor(lhs[:], lhs[:], tmp[:], ALU.add))
                dve.wait_ge(made, 1)
                ch(dve.tensor_copy(full[:], ps[:]))
                ch(dve.tensor_copy(part[:, 0, :], full[:]))
                ch(dve.tensor_tensor(rest[:], full[:], part[:, 0, :], ALU.subtract))
                ch(dve.tensor_copy(part[:, 1, :], rest[:]))
                ch(dve.tensor_tensor(part[:, 2, :], rest[:], part[:, 1, :], ALU.subtract))
                ch(dve.tensor_copy(kpart[:, 0, :], kf[:, 0, :]))
                ch(dve.tensor_tensor(kf[:, 1, :], kf[:, 0, :], kpart[:, 0, :], ALU.subtract))
                ch(dve.tensor_copy(kpart[:, 1, :], kf[:, 1, :]))
                ch(dve.tensor_tensor(kpart[:, 2, :], kf[:, 1, :], kpart[:, 1, :], ALU.subtract))

            @block.tensor
            def _(pe):
                pe.wait_ge(own, 3)
                for n in range(2):
                    ins = pe.matmul(ps[:, n * 512:(n + 1) * 512], lhs[:].rearrange("p h f -> p (h f)"),
                                    table[:, n * 512:(n + 1) * 512], start=True, stop=True)
                ins.then_inc(made, 1)
    return stored, 16 * (B + 1) * SPLITS


class Env:
    pass


def build(nc, i, out, stages=99, first=1):
    env = Env()
    env.dram = i
    env.recip_sem = {}
    with ExitStack() as ctx:
        main = ctx.enter_context(Stage(nc, "main"))
        env.X = main.sb("X", [P, B * T])
        env.ident = main.sb("ident", [P, P])
        env.identb = main.sb("identb", [P, P], BF16)
        env.blk = main.sb("blk", [P, H])
        env.blk2 = main.sb("blk2", [P, P])
        env.own_columns = main.sb("own_columns", [P, 32 // HD, P])
        env.sel = main.sb("sel", [P, 2 * (HD + 1)])
        env.minus_half = main.sb("minus_half", [P, 32])
        x_in = i["L0_attn_a_x"].rearrange("b (j p) d -> p (b j) d", p=P)
        x_out = out.rearrange("b (j p) d -> p (b j) d", p=P)
        Passed.sem = main.sem("passed")
        got, own = main.sem("got"), main.sem("own")
        env.gathered = [nc.alloc_semaphore("gathered0"), nc.alloc_semaphore("gathered1")]
        env.scattered = nc.alloc_semaphore("scattered")
        env.experts_run = 0
        with nc.Block() as block:
            @block.sync
            def _(sp):
                n = load(sp, got, [(env.ident[:], i["ident"]), (env.blk[:], i["blk"]), (env.blk2[:], i["blk2"]), 
                                   (env.own_columns[:], i["own_columns"].partition_broadcast(P)),
                                   (env.sel[:], i["sel"])]
                         + [(env.X[:, b * T:(b + 1) * T].rearrange("p (j d) -> p j d", d=D),
                             x_in[:, b * TILES:(b + 1) * TILES, :]) for b in range(B)])
                sp.wait_ge(got, n)

            @block.vector
            def _(dve):
                dve.memset(env.minus_half[:], -0.5).then_inc(own, 1)
                dve.wait_ge(got, (5 + B) * 16)
                dve.tensor_copy(env.identb[:], env.ident[:]).then_inc(own, 1)
                dve.wait_ge(own, 2)

        if first <= 1 <= stages:
            softmax_block_a(nc, env, i)
        if first <= 2 <= stages:
            experts(nc, env, i, "f1")
        if first <= 3 <= stages:
            retention_block(nc, env, i)
        if first <= 4 <= stages:
            experts(nc, env, i, "f2")
        if first <= 5 <= stages:
            masked_softmax_block(nc, env, i)
        if stages >= 6:
            linear_weights(nc, env, i, main)
        if first <= 6 <= stages:
            linear_block(nc, env, "l1")
        if first <= 7 <= stages:
            rwkv_block(nc, env, i)
        if first <= 8 <= stages:
            linear_block(nc, env, "l2")

        done = main.sem("done")
        with nc.Block() as block:
            @block.sync
            def _(sp):
                for b in range(B):
                    sp.dma_start(x_out[:, b * TILES:(b + 1) * TILES, :],
                                 env.X[:, b * T:(b + 1) * T].rearrange("p (j d) -> p j d", d=D)).then_inc(done, 16)
                sp.wait_ge(done, 16 * B)


def experts(nc, env, i, name):
    PAIRS = B * EXPERTS
    ROWS, HALF = 2 * PAIRS, T // 2
    ROUNDS = (CAPACITY + 7) // 8
    FULL = CAPACITY // P
    REST = CAPACITY - FULL * P
    assert FULL == 2 and REST == 1
    MT = FULL * B
    normed = nc.dram_tensor(f"{name}_normed", [B * T, D], F32, kind="Internal").ap()
    total = nc.dram_tensor(f"{name}_total", [B * T, D], F32, kind="Internal").ap()
    rest_d = nc.dram_tensor(f"{name}_rest", [ROWS, 2], F32, kind="Internal").ap()
    tokens = lambda d, s: d.rearrange("(b j p) d -> b p j d", b=B, p=P)[s]
    with Stage(nc, name) as sw:
        logits = sw.sb("logits", [P, TILES, B, EXPERTS])
        idxT = sw.sb("idxT", [P, EXPERTS, MT], mybir.dt.uint32)
        gateT = sw.sb("gateT", [P, EXPERTS, MT])
        rest_f = sw.sb("rest_f", [B, EXPERTS, 2])
        rest_h = sw.sb("rest_h", [B, 2, EXPERTS, 2])
        rest_i = sw.sb("rest_i", [B, EXPERTS], mybir.dt.uint32)
        saved_total = sw.sem("saved_total")
        with Stage(nc, name + "r") as st:
            nm = Norm(st, env)
            rw = st.sb("rw", [P, EXPERTS])
            psR = st.ps("psR", [P, TILES, EXPERTS])
            got, r_ready, r_taken = st.sem("got"), st.sem("r_ready"), st.sem("r_taken")
            y_saved, y_stored = st.sem("y_saved"), st.sem("y_stored")
            with nc.Block() as block:
                @block.sync
                def _(sp):
                    sp.dma_start(rw[:], i["router_wT"]).then_inc(got, 16)
                    for b in range(B):
                        sp.dma_start(tokens(total, b), batch(env.X, b)).then_inc(saved_total, 16)

                    def body(s, u):
                        wait_alone(sp, nm.y_ready, s + 1)
                        sp.dma_start(normed.rearrange("(b j p) d -> b p j d", b=B, p=P)[ds(s, 1)].rearrange(
                            "o p j d -> (o p) j d"), nm.y[:, u]).then_inc(y_stored, 16)
                        sp.wait_ge(y_stored, s * 16 + 16)
                        sp.sem_inc(y_saved, 1)
                    loop_batches(sp, body)
                    sp.wait_ge(saved_total, 16 * B)

                @block.vector
                def _(dve):
                    nm.credits(dve)
                    dve.sem_inc(y_saved, 2)

                    def body(s, u):
                        dve.wait_ge(r_ready, s + 1)
                        dve.tensor_copy(logits[:, :, ds(s, 1), :].rearrange("p j b e -> p j (b e)"),
                                        psR[:]).then_inc(r_taken, 1)
                    loop_ahead(dve, lambda s, u: nm.vector(dve, s, u, saved=y_saved), body)

                @block.gpsimd
                def _(pool):
                    loop_batches(pool, lambda s, u: nm.gpsimd(pool, s, u))

                @block.tensor
                def _(pe):
                    pe.wait_ge(got, 16)

                    def body(s, u):
                        pe.wait_ge(nm.xt_ready, s + 1)
                        pe.wait_ge(r_taken, s)
                        for j in range(TILES):
                            ins = pe.matmul(psR[:, j, :], nm.xT[:, u, j * P:(j + 1) * P], rw[:], start=True, stop=True)
                        ins.then_inc(r_ready, 1)
                    loop_ahead(pe, lambda s, u: nm.tensor(pe, s, u), body)

                @block.scalar
                def _(act):
                    def body(s, u):
                        act.wait_ge(r_ready, s + 1)
                        act.sem_inc(nm.xt_free, 1)
                    loop_ahead(act, lambda s, u: nm.scalar(act, s, u), body)

        with Stage(nc, name + "k") as st:
            small = st.sb("small", [P, TILES * B])
            work = st.sb("work", [ROWS, HALF])
            best = st.sb("best", [ROWS, ROUNDS * 8])
            where = st.sb("where", [ROWS, ROUNDS * 8], mybir.dt.uint32)
            where_f = st.sb("where_f", [ROWS, ROUNDS * 8])
            halves = st.sb("halves", [P, 2, 2, FULL, PAIRS])
            flipped = st.sb("flipped", [P, 2, FULL, PAIRS])
            flip = st.sb("flip", [P, P])
            first = st.sb("first", [P, FULL, PAIRS])
            first_rest = st.sb("first_rest", [B, EXPERTS])
            rest = st.sb("rest", [ROWS, 2])
            row_base = st.sb("row_base", [ROWS, 1])
            ABREAST = 3
            WIDTH = ABREAST * 8
            assert ROUNDS % ABREAST == 0
            top = st.sb("top", [ROWS, WIDTH])
            idx = st.sb("idx", [ROWS, WIDTH], mybir.dt.uint32)
            psW = st.ps("psW", [PAIRS, T])
            psI = st.ps("psI", [P, 2, 2, FULL, ROWS])
            psF = st.ps("psF", [P, 2, FULL, PAIRS])
            got, own, ex_ready, in_ready, w_ready, t_ready, moved = (
                st.sem(n) for n in ("got", "own", "ex_ready", "in_ready", "w_ready", "t_ready", "moved"))
            rounds_own = st.sem("rounds_own")
            lg = logits[:].rearrange("p j b e -> p (j b) e")
            spread = small[:].unsqueeze(2).broadcast_to([P, TILES * B, EXPERTS])
            with nc.Block() as block:
                @block.vector
                def _(dve):
                    ch = Chain(dve, own)
                    ch(dve.tensor_reduce(small[:], lg, AX.X, ALU.max))
                    dve.tensor_tensor(lg, lg, spread, ALU.subtract).then_inc(in_ready, 1)
                    dve.wait_ge(ex_ready, 1)
                    ch(dve.tensor_reduce(small[:], lg, AX.X, ALU.add))
                    ch(dve.reciprocal(small[:], small[:]))
                    dve.tensor_tensor(lg, lg, spread, ALU.mult).then_inc(in_ready, 1)
                    dve.wait_ge(w_ready, 1)
                    for h in range(2):
                        ins = dve.tensor_copy(work[h * PAIRS:(h + 1) * PAIRS], psW[:, h * HALF:(h + 1) * HALF])
                    ins.then_inc(rounds_own, 1)
                    dve.wait_ge(rounds_own, 1)
                    with dve.Fori(0, ROUNDS // ABREAST) as r:
                        for k in range(ABREAST):
                            n = r * (2 * ABREAST + 2) + 2 * k
                            dve.max(top[:, k * 8:(k + 1) * 8], work[:]).then_inc(rounds_own, 1)
                            wait_alone(dve, rounds_own, n + 2)
                            dve.max_index(idx[:, k * 8:(k + 1) * 8], top[:, k * 8:(k + 1) * 8], work[:])
                            dve.match_replace(work[:], top[:, k * 8:(k + 1) * 8], work[:], TAKEN).then_inc(rounds_own, 1)
                            wait_alone(dve, rounds_own, n + 3)
                        dve.tensor_copy(best[:, ds(r * WIDTH, WIDTH)], top[:]).then_inc(rounds_own, 1)
                        dve.tensor_copy(where[:, ds(r * WIDTH, WIDTH)], idx[:]).then_inc(rounds_own, 1)
                        wait_alone(dve, rounds_own, r * (2 * ABREAST + 2) + 2 * ABREAST + 3)
                    last = CAPACITY - 1
                    ch(dve.tensor_copy(where_f[:], where[:]))
                    dve.wait_ge(got, 32)
                    ch(dve.tensor_scalar(where_f[:], where_f[:], row_base[:, 0:1], None, ALU.add))
                    for rows, rank in ((slice(0, PAIRS), last), (slice(PAIRS, ROWS), 0)):
                        dve.tensor_copy(rest[rows, 0:1], where_f[rows, rank:rank + 1])
                        ins = dve.tensor_copy(rest[rows, 1:2], best[rows, rank:rank + 1])
                    ins.then_inc(in_ready, 1)
                    dve.wait_ge(t_ready, 1)
                    for h in range(2):
                        ins = dve.tensor_copy(halves[:, h], psI[:, h, :, :, h * PAIRS:(h + 1) * PAIRS])
                    ins.then_inc(in_ready, 1)
                    dve.wait_ge(t_ready, 2)
                    ch(dve.tensor_copy(flipped[:], psF[:]))

                    def better(firsts, idx_a, idx_b, gate_a, gate_b, idx_out, gate_out):
                        ch(dve.tensor_tensor(firsts, gate_a, gate_b, ALU.is_ge))
                        ch(dve.tensor_tensor(idx_a, idx_a, idx_b, ALU.subtract))
                        ch(dve.tensor_tensor(idx_a, idx_a, firsts, ALU.mult))
                        ch(dve.tensor_tensor(idx_a, idx_a, idx_b, ALU.add))
                        ch(dve.tensor_tensor(gate_a, gate_a, gate_b, ALU.max))
                        idx_out(idx_a)
                        gate_out(gate_a)

                    a, z = halves[:, 0], flipped
                    form = lambda x: x.rearrange("p f (b e) -> p e f b", b=B)

                    def place(dst):
                        def put(x):
                            for f in range(FULL):
                                ins = dve.tensor_copy(dst[:, :, f * B:(f + 1) * B], form(x)[:, :, f])
                            ch(ins)
                        return put
                    better(first[:], a[:, 0], z[:, 0], a[:, 1], z[:, 1], place(idxT), place(gateT))
                    dve.wait_ge(moved, 32)
                    ha, hz = rest_h[:, 0], rest_h[:, 1]
                    better(first_rest[:], ha[:, :, 0], hz[:, :, 0], ha[:, :, 1], hz[:, :, 1],
                           lambda x: ch(dve.tensor_copy(rest_i[:], x)), lambda x: ch(dve.tensor_copy(rest_f[:, :, 1], x)))

                @block.scalar
                def _(act):
                    act.wait_ge(in_ready, 1)
                    act.activation(lg, lg, ACT.Exp).then_inc(ex_ready, 1)

                @block.tensor
                def _(pe):
                    pe.wait_ge(in_ready, 2)
                    for j in range(TILES):
                        ins = pe.transpose(psW[:, j * P:(j + 1) * P], logits[:, j].rearrange("p b e -> p (b e)"),
                                           env.ident[:])
                    ins.then_inc(w_ready, 1)
                    pe.wait_ge(in_ready, 3)
                    for k, src in enumerate((where_f, best)):
                        for f in range(FULL):
                            for h, at in ((0, f * P), (1, CAPACITY - (f + 1) * P)):
                                ins = pe.transpose(psI[:, h, k, f, :], src[:, at:at + P], env.ident[0:ROWS, 0:ROWS])
                    ins.then_inc(t_ready, 1)
                    pe.wait_ge(in_ready, 4)
                    pe.wait_ge(got, 32)
                    pe.matmul(psF[:].rearrange("p k f r -> p (k f r)"), flip[:], halves[:, 1].rearrange("p k f r -> p (k f r)"),
                              start=True, stop=True).then_inc(t_ready, 1)

                @block.sync
                def _(sp):
                    sp.dma_start(row_base[:], i["row_base"]).then_inc(got, 16)
                    sp.dma_start(flip[:], i["flip"]).then_inc(got, 16)
                    sp.wait_ge(in_ready, 3)
                    sp.dma_start(rest_d, rest[:]).then_inc(moved, 16)
                    sp.wait_ge(moved, 16)
                    sp.dma_start(rest_h[:], rest_d.rearrange("(h b e) k -> b h e k", h=2, b=B)).then_inc(moved, 16)
                    sp.wait_ge(moved, 32)

        with Stage(nc, name + "e") as st:
            w1 = st.sb("w1", [P, 2, HIDDEN])
            w2 = st.sb("w2", [P, 2, HK, D])
            b1 = st.sb("b1", [P, 2, HK])
            b2 = st.sb("b2", [P, 2, D])
            ie = st.sb("ie", [P, 2, MT], mybir.dt.uint32)
            ir = st.sb("ir", [B, 2, 1], mybir.dt.uint32)
            se = st.sb("se", [P, 2, MT], mybir.dt.uint32)
            sr = st.sb("sr", [B, 2, 1], mybir.dt.uint32)
            g = st.sb("g", [P, 2, MT * D])
            gr = st.sb("gr", [B, 2, D])
            WIDE = MT * P + B
            xg = st.sb("xg", [P, 2, WIDE])
            hT = st.sb("hT", [P, 2, HK, WIDE])
            yg = st.sb("yg", [P, 2, MT * D])
            yr = st.sb("yr", [B, 2, D])
            psG = st.ps("psG", [P, MT * P])
            psH = st.ps("psH", [P, 2, 512])
            psY = st.ps("psY", [P, MT * D])
            psL = st.ps("psL", [P, 512])
            psLY = st.ps("psLY", [B, D])
            lx, lh, ly = psL[:, 256:256 + B], psL[:, 384:384 + HK * B], psLY[:]
            w_got = [st.sem("w_got0"), st.sem("w_got1")]
            gathered, scattered = env.gathered, env.scattered
            got0, scattered0 = env.experts_run * 16 * (MT + 1) * EXPERTS // 2, env.experts_run * 16 * (MT + 1) * EXPERTS
            env.experts_run += 1
            names = ("idx_own", "g_taken", "xt_ready", "xg_ready", "h_ready", "h_taken", "lh_ready", "hidden_ready",
                     "y_ready", "y_taken", "own", "yg_ready")
            (idx_own, g_taken, xt_ready, xg_ready, h_ready, h_taken, lh_ready, hidden_ready, y_ready, y_taken,
             own, yg_ready) = (st.sem(n) for n in names)
            rows_own = st.sem("rows_own")
            TURNS = EXPERTS // 2
            CH = MT * P // 512 * HK

            def turns(eng, body):
                body(0, True, False)
                with eng.Fori(1, TURNS - 1) as t:
                    body(t, False, False)
                body(TURNS - 1, False, True)

            with nc.Block() as block:
                @block.sync
                def _(sp):
                    def body(t, first, last):
                        for u in range(2):
                            e = t * 2 + u
                            if not first:
                                wait_alone(sp, y_taken, e - 1)
                            sp.dma_start(w1[:, u, :], i["L0_ffn_w1"][ds(e, 1)].rearrange("o p h -> (o p) h")).then_inc(w_got[u], 16)
                            sp.dma_start(w2[:, u], i["L0_ffn_w2"].rearrange("e (k p) d -> e p k d", p=P)[ds(e, 1)].rearrange(
                                "o p k d -> (o p) k d")).then_inc(w_got[u], 16)
                            sp.dma_start(b1[:, u, :], i["b1_cols"][ds(e, 1)].rearrange(
                                "o p k -> (o p) k")).then_inc(w_got[u], 16)
                            sp.dma_start(b2[:, u, :], i["L0_ffn_b2"][ds(e, 1), :].rearrange(
                                "o d -> (o d)").partition_broadcast(P)).then_inc(w_got[u], 16)
                    turns(sp, body)

                @block.gpsimd
                def _(pool):
                    def take_rows(e, u, main, rest, own):
                        pool.tensor_copy(main[:, u, :], idxT[:, ds(e, 1), :].rearrange("p o m -> p (o m)")).then_inc(own, 1)
                        pool.tensor_copy(rest[:, u, :], rest_i[:, ds(e, 1)]).then_inc(own, 1)
                        wait_alone(pool, own, e * 2 + 2)

                    def gather(e, u, first):
                        if not first:
                            wait_alone(pool, g_taken, e - 1)
                        take_rows(e, u, ie, ir, idx_own)
                        for m in range(MT):
                            pool.indirect_dma_start(g[:, u, m * D:(m + 1) * D], None, normed,
                                                    bass.IndirectOffsetOnAxis(ap=ie[:, u, m:m + 1], axis=0)).then_inc(gathered[u], 16)
                        pool.indirect_dma_start(gr[:, u, :], None, normed,
                                                bass.IndirectOffsetOnAxis(ap=ir[:, u, :], axis=0)).then_inc(gathered[u], 16)

                    gather(0, 0, True)
                    gather(1, 1, True)
                    done = 16 * (MT + 1)

                    def body(t, first, last):
                        for u in range(2):
                            e = t * 2 + u
                            if not last:
                                gather(e + 2, u, False)
                            if not (first and u == 0):
                                wait_alone(pool, scattered, e * done + scattered0)
                            take_rows(e, u, se, sr, rows_own)
                            wait_alone(pool, yg_ready, e + 1)
                            for m in range(MT):
                                pool.indirect_dma_start(total, bass.IndirectOffsetOnAxis(ap=se[:, u, m:m + 1], axis=0),
                                                        yg[:, u, m * D:(m + 1) * D], None, compute_op=ALU.add).then_inc(scattered, 16)
                            pool.indirect_dma_start(total, bass.IndirectOffsetOnAxis(ap=sr[:, u, :], axis=0),
                                                    yr[:, u, :], None, compute_op=ALU.add).then_inc(scattered, 16)
                    turns(pool, body)
                    pool.wait_ge(scattered, done * EXPERTS + scattered0)

                @block.tensor
                def _(pe):
                    def transposes(t, u, first):
                        e = t * 2 + u
                        pe.wait_ge(gathered[u], (t + 1) * 16 * (MT + 1) + got0)
                        if not first:
                            pe.wait_ge(xg_ready, e)
                        for m in range(MT):
                            pe.transpose(psG[:, m * P:(m + 1) * P], g[:, u, m * D:(m + 1) * D], env.ident[:])
                        pe.transpose(lx, gr[:, u, :], env.ident[0:B, 0:B]).then_inc(xt_ready, 1)

                    def hidden(t, u):
                        e = t * 2 + u
                        pe.wait_ge(xg_ready, e + 1)
                        pe.wait_ge(w_got[u], (t + 1) * 64)
                        for k in range(HK):
                            ins = pe.matmul(lh[:, k * B:(k + 1) * B], w1[:, u, k * P:(k + 1) * P],
                                            xg[:, u, MT * P:WIDE], start=True, stop=True)
                        ins.then_inc(lh_ready, 1)
                        for n in range(CH):
                            if not (isinstance(e, int) and e == 0 and n < 2):
                                pe.wait_ge(h_taken, e * CH + n - 1)
                            k, c = n % HK, n // HK
                            pe.matmul(psH[:, n % 2, :], w1[:, u, k * P:(k + 1) * P], xg[:, u, c * 512:(c + 1) * 512],
                                      start=True, stop=True).then_inc(h_ready, 1)

                    def outputs(t, u):
                        e = t * 2 + u
                        pe.wait_ge(hidden_ready, e + 1)
                        pe.wait_ge(y_taken, e)
                        for m in range(MT + 1):
                            o, lo, hi = (ly, MT * P, WIDE) if m == MT else (psY[:, m * D:(m + 1) * D], m * P, (m + 1) * P)
                            for k in range(HK):
                                ins = pe.matmul(o, hT[:, u, k, lo:hi], w2[:, u, k, :], start=(k == 0), stop=(k == HK - 1))
                        ins.then_inc(y_ready, 1)

                    transposes(0, 0, True)

                    def body(t, first, last):
                        for u in range(2):
                            hidden(t, u)
                            if not (last and u == 1):
                                pe.wait_ge(hidden_ready, t * 2 + u + 1)
                                transposes(t + u, 1 - u, False)
                            outputs(t, u)
                    turns(pe, body)

                @block.scalar
                def _(act):
                    def take(t, u):
                        e = t * 2 + u
                        act.wait_ge(xt_ready, e + 1)
                        act.activation(xg[:, u, 0:MT * P], psG[:], ACT.Copy)
                        act.activation(xg[:, u, MT * P:WIDE], lx, ACT.Copy).then_inc(xg_ready, 1)
                        act.sem_inc(g_taken, 1)

                    take(0, 0)

                    def body(t, first, last):
                        for u in range(2):
                            e = t * 2 + u
                            act.wait_ge(w_got[u], (t + 1) * 64)
                            if not first:
                                act.wait_ge(y_ready, e - 1)
                            act.wait_ge(lh_ready, e + 1)
                            for k in range(HK):
                                act.activation(hT[:, u, k, MT * P:WIDE], lh[:, k * B:(k + 1) * B], ACT.Gelu, bias=b1[:, u, k:k + 1])
                            for n in range(CH):
                                k, c = n % HK, n // HK
                                act.wait_ge(h_ready, e * CH + n + 1)
                                ins = act.activation(hT[:, u, k, c * 512:(c + 1) * 512], psH[:, n % 2, :], ACT.Gelu,
                                                     bias=b1[:, u, k:k + 1])
                                ins.then_inc(h_taken, 1)
                            act.wait_ge(h_taken, e * CH + CH)
                            act.sem_inc(hidden_ready, 1)
                            if not (last and u == 1):
                                take(t + u, 1 - u)
                    turns(act, body)

                @block.vector
                def _(dve):
                    def body(t, first, last):
                        for u in range(2):
                            e = t * 2 + u
                            out = yg[:, u, :].rearrange("p (m d) -> p m d", d=D)
                            if not first:
                                dve.wait_ge(scattered, (e - 1) * 16 * (MT + 1) + scattered0)
                            dve.wait_ge(y_ready, e + 1)
                            dve.tensor_tensor(out, psY[:].rearrange("p (m d) -> p m d", d=D),
                                              b2[:, u, :].unsqueeze(1).broadcast_to([P, MT, D]), ALU.add)
                            dve.tensor_tensor(yr[:, u, :], ly, b2[0:B, u, :], ALU.add).then_inc(own, 1)
                            dve.wait_ge(own, e + 1)
                            dve.tensor_tensor(out, out, gateT[:, ds(e, 1), :].rearrange("p o m -> p (o m)").unsqueeze(2)
                                              .broadcast_to([P, MT, D]), ALU.mult)
                            dve.tensor_tensor(yr[:, u, :], yr[:, u, :], rest_f[:, ds(e, 1), 1].broadcast_to([B, D]),
                                              ALU.mult).then_inc(yg_ready, 1)
                            dve.sem_inc(y_taken, 1)
                    turns(dve, body)

            back = st.sem("back")
            with nc.Block() as block:
                @block.sync
                def _(sp):
                    for b in range(B):
                        sp.dma_start(batch(env.X, b), tokens(total, b)).then_inc(back, 16)
                    sp.wait_ge(back, 16 * B)


def retention_inputs(nc, env, st, weights, jobs, mixes=None, pad=0):
    nm = Norm(st, env, pad=pad)
    n_src = 1 if mixes is None else mixes.shape[1]
    psP = st.ps("psP", [P, 2, T])
    p_ready, p_taken = st.sem("p_ready"), st.sem("p_taken")
    src_ready, own = st.sem("src_ready"), st.sem("own")
    if mixes is not None:
        diff = st.sb("diff", [P, T])
        src = st.sb("src", [P, n_src, T])
    J = len(jobs)
    with nc.Block() as block:
        @block.vector
        def _(dve):
            nm.credits(dve)
            ch = Chain(dve, own)
            if mixes is not None:
                dve.memset(nm.xT[:, :, 0:pad], 0.0).then_inc(src_ready, 1)

            def body(s, u):
                if mixes is not None:
                    dve.wait_ge(nm.xt_ready, s + 1)
                    x = nm.xT[:, u, pad:pad + T]
                    ch.start(s)
                    ch(dve.tensor_tensor(diff[:], nm.xT[:, u, 0:T], x, ALU.subtract))
                    dve.wait_ge(p_ready, s * J)
                    for m in range(n_src):
                        ins = dve.scalar_tensor_tensor(src[:, m, :], diff[:], mixes[:, m:m + 1], x, ALU.mult, ALU.add)
                    ins.then_inc(src_ready, 1)
                    dve.wait_ge(src_ready, s + 2)
                    dve.sem_inc(nm.xt_free, 1)
            loop_ahead(dve, lambda s, u: nm.vector(dve, s, u), body)

        @block.gpsimd
        def _(pool):
            loop_batches(pool, lambda s, u: nm.gpsimd(pool, s, u))

        @block.tensor
        def _(pe):
            pe.sem_inc(p_taken, 2)

            def body(s, u):
                if mixes is None:
                    pe.wait_ge(nm.xt_ready, s + 1)
                else:
                    pe.wait_ge(src_ready, s + 2)
                for n, (m, w, form, bias, func, dst) in enumerate(jobs):
                    x = nm.xT[:, u, :] if mixes is None else src[:, m, :]
                    pe.wait_ge(p_taken, s * J + n + 1)
                    o = psP[:, (u * J + n) % 2, :]
                    if form == "channels":
                        for k in range(2):
                            ins = pe.matmul(o[:, k * 512:(k + 1) * 512], w, x[:, k * 512:(k + 1) * 512], start=True, stop=True)
                    else:
                        for k in range(TILES):
                            ins = pe.matmul(o[:, k * P:(k + 1) * P], x[:, k * P:(k + 1) * P], w, start=True, stop=True)
                    ins.then_inc(p_ready, 1)
            loop_ahead(pe, lambda s, u: nm.tensor(pe, s, u), body)

        @block.scalar
        def _(act):
            def body(s, u):
                for n, (m, w, form, bias, func, dst) in enumerate(jobs):
                    wait_alone(act, p_ready, s * J + n + 1)
                    o = psP[:, (u * J + n) % 2, :].rearrange("p (j d) -> p j d", d=D)
                    if bias is not None:
                        act.activation(dst(s), o, ACT.Identity, bias=bias).then_inc(p_taken, 1)
                    else:
                        act.activation(dst(s), o, func).then_inc(p_taken, 1)
                if mixes is None:
                    act.sem_inc(nm.xt_free, 1)
            loop_ahead(act, lambda s, u: nm.scalar(act, s, u), body)


def retention(nc, env, st, QK, KT, V, OUT, mask, key_decay, out_decay, state_decay):
    GROUPS, LOCAL = P // 32, 32 // HD
    qk = st.sb("qk", [P, 2, 2, P])
    qx = st.sb("qx", [P, 2, H, P])
    kd = st.sb("kd", [P, 2, D])
    sm = st.sb("sm", [P, 2, H, P])
    state = st.sb("state", [P, B, D])
    vx = st.sb("vx", [P, 2, LOCAL, P])
    outT = st.sb("outT", [P, 2, P])
    inter = st.sb("inter", [P, 2, D])
    upd = st.sb("upd", [P, 2, D])
    psS = st.ps("psS", [P, GROUPS, LOCAL, P])
    psO = st.ps("psO", [P, 2, 512])
    psM = st.ps("psM", [P, 2, 512])
    inter_at, grow_at = slice(0, D), slice(D, 2 * D)
    vx_ready, outT_ready, turned = st.sem("vx_ready"), st.sem("outT_ready"), st.sem("turned")
    names = ("qk_ready", "kd_ready", "qx_ready", "s_ready", "s_masked", "o_ready", "u_ready", "state_ready",
             "own", "inter_taken")
    (qk_ready, kd_ready, qx_ready, s_ready, s_masked, o_ready, u_ready, state_ready, own,
     inter_taken) = (st.sem(n) for n in names)
    qk_free, kd_free, o_free = (st.sem(n) for n in ("qk_free", "kd_free", "o_free"))
    heads_of_mask = mask.shape[1]

    AT_START = 4
    OUTS = 2

    def step(c, b):
        return c * B + b, c + b * TILES, b

    def around(c, b, delta):
        return step(c + (b + delta) // B, (b + delta) % B)

    def chunks(eng, body):
        for b in range(B):
            body(0, b, True, False)
        with eng.Fori(1, TILES - 1) as c:
            for b in range(B):
                body(c, b, False, False)
        for b in range(B):
            body(TILES - 1, b, False, True)

    with nc.Block() as block:
        @block.scalar
        def _(act):
            act.sem_inc(qk_free, 2)

            def keep(m, n, b):
                act.wait_ge(o_ready, m + OUTS + 1)
                act.activation(outT[:, b % 2, :], psO[:, b % 2, 0:P], ACT.Copy).then_inc(outT_ready, 1)

            def body(c, b, first, last):
                m, n, _ = step(c, b)
                act.wait_ge(qk_free, m + 1)
                act.activation(qk[:, b % 2], QK[:, ds(n, 1)].rearrange("p o a t -> p (o a) t"), ACT.Copy).then_inc(qk_ready, 1)
                if not (first and b < 2):
                    keep(*around(c, b, -2))
            chunks(act, body)
            keep(*step(TILES - 1, B - 2))
            keep(*step(TILES - 1, B - 1))

        @block.gpsimd
        def _(pool):
            pool.sem_inc(kd_free, 2)
            pool.sem_inc(o_ready, OUTS)

            def body(c, b, first, last):
                m, n, _ = step(c, b)
                u = b % 2
                pool.wait_ge(qk_ready, m + 1)
                pool.wait_ge(kd_free, m + 1)
                pool.tensor_tensor(qx[:, u], qk[:, u, 0, :].unsqueeze(1).broadcast_to([P, H, P]),
                                   env.blk[:].unsqueeze(2).broadcast_to([P, H, P]), ALU.mult).then_inc(qx_ready, 1)
                pool.tensor_tensor(kd[:, u, :], KT[:, ds(n, 1), :].rearrange("p o d -> p (o d)"), key_decay,
                                   ALU.mult).then_inc(kd_ready, 1)
                pool.wait_ge(o_ready, m + 1)
                pool.tensor_tensor(vx[:, u], V[:, ds(n, 1), :].broadcast_to([P, LOCAL, P]), env.own_columns[:],
                                   ALU.mult).then_inc(vx_ready, 1)
            chunks(pool, body)

        @block.tensor
        def _(pe):
            pe.wait_ge(own, 1)

            def scores(m, n, b):
                u = b % 2
                pe.wait_ge(qx_ready, m + 1)
                pe.wait_ge(s_masked, (m + 1) * GROUPS)
                for g in range(GROUPS):
                    pe.matmul(psS[:, g].rearrange("p h t -> p (h t)"), qk[:, u, 1, :],
                              qx[:, u, LOCAL * g:LOCAL * (g + 1)].rearrange("p h t -> p (h t)"),
                              start=True, stop=True).then_inc(s_ready, 1)

            def turn(m, n, b):
                pe.wait_ge(outT_ready, m + 1)
                pe.transpose(psO[:, b % 2, P:P + D], outT[:, b % 2, :], env.ident[:]).then_inc(turned, 1)

            def body(c, b, first, last):
                m, n, _ = step(c, b)
                u = b % 2
                v = V[:, ds(n, 1), :].rearrange("p o d -> p (o d)")
                pe.wait_ge(state_ready, m + 1)
                pe.wait_ge(inter_taken, m * 2 + AT_START - 2)
                pe.matmul(psM[:, u, inter_at], qk[:, u, 0, :], state[:, b, :], start=True, stop=True)
                pe.wait_ge(kd_ready, m + 1)
                pe.matmul(psM[:, u, grow_at], kd[:, u, :], v, start=True, stop=True).then_inc(u_ready, 1)
                if not (last and b == B - 1):
                    scores(*around(c, b, 1))
                pe.wait_ge(s_masked, (m + 1) * GROUPS + GROUPS)
                pe.wait_ge(o_free, m + 1)
                pe.wait_ge(vx_ready, m + 1)
                for h in range(LOCAL):
                    for g in range(GROUPS):
                        cols = slice(32 * g, 32 * g + 32)
                        ins = pe.matmul(psO[cols, u, 0:P], vx[:, u, h, cols], sm[:, u, g * LOCAL + h, :],
                                        start=(h == 0), stop=(h == LOCAL - 1))
                ins.then_inc(o_ready, 1)
                if not (first and b == 0):
                    turn(*around(c, b, -1))

            scores(*step(0, 0))
            chunks(pe, body)
            turn(*step(TILES - 1, B - 1))

        @block.vector
        def _(dve):
            dve.sem_inc(s_masked, GROUPS)
            dve.sem_inc(inter_taken, AT_START)
            dve.sem_inc(o_free, OUTS)
            dve.memset(state[:], 0.0).then_inc(own, 1)
            dve.wait_ge(own, 1)
            dve.sem_inc(state_ready, B)

            def add(m, n, b):
                u = b % 2
                dve.wait_ge(turned, m + 1)
                dve.tensor_tensor(OUT[:, ds(n, 1), :].rearrange("p o d -> p (o d)"), psO[:, u, P:P + D], inter[:, u, :],
                                  ALU.add).then_inc(o_free, 1)

            def body(c, b, first, last):
                m, n, _ = step(c, b)
                u = b % 2
                for g in range(GROUPS):
                    dve.wait_ge(s_ready, m * GROUPS + g + 1)
                    mk = mask[:, LOCAL * g:LOCAL * (g + 1), :] if heads_of_mask > 1 else mask.broadcast_to([P, LOCAL, P])
                    dve.tensor_tensor(sm[:, u, LOCAL * g:LOCAL * (g + 1), :], psS[:, g], mk, ALU.mult).then_inc(s_masked, 1)
                if not (first and b < 2):
                    add(*around(c, b, -2))
                dve.wait_ge(o_free, m + 1)
                dve.wait_ge(u_ready, m + 1)
                dve.tensor_tensor(inter[:, u, :], psM[:, u, inter_at], out_decay, ALU.mult).then_inc(inter_taken, 1)
                dve.sem_inc(qk_free, 1)
                dve.sem_inc(kd_free, 1)
                dve.tensor_tensor(upd[:, u, :], psM[:, u, grow_at], env.blk2[:], ALU.mult).then_inc(inter_taken, 1)
                dve.wait_ge(inter_taken, m * 2 + 2 + AT_START)
                dve.scalar_tensor_tensor(state[:, b, :], state[:, b, :], state_decay, upd[:, u, :], ALU.mult,
                                         ALU.add).then_inc(state_ready, 1)
            chunks(dve, body)
            add(*step(TILES - 1, B - 2))
            add(*step(TILES - 1, B - 1))


def retention_block(nc, env, i):
    W = {}
    with Stage(nc, "b") as sw:
        for n in ("Wq", "Wk", "Wv", "Wo"):
            W[n] = sw.sb(n, [P, D])
        cols = sw.sb("cols", [P, 7])
        bk, bv = sw.sb("bk", [P, D]), sw.sb("bv", [P, D])
        mask = sw.sb("mask", [P, 1, P])
        tok_decay = sw.sb("tok_decay", [P, 2])
        dmat = sw.sb("dmat", [P, 2, D])
        QK = sw.sb("QK", [P, B * TILES, 2, P])
        KT = sw.sb("KT", [P, B * TILES, D])
        V = sw.sb("V", [P, B * TILES, D])
        got, own = sw.sem("got"), sw.sem("own")
        with nc.Block() as block:
            @block.sync
            def _(sp):
                n = load(sp, got, [(W[k][:], i[f"L0_attn_b_{k}"]) for k in W]
                         + [(cols[:, k:k + 1], column(i[f"L0_attn_b_{v}"])) for k, v in enumerate(("bq", "bk", "bo", "gamma", "beta"))]
                         + [(bk[:], i["L0_attn_b_bk"].partition_broadcast(P)), (bv[:], i["L0_attn_b_bv"].partition_broadcast(P)),
                            (mask[:, 0, :], i["decay_mask"]), (tok_decay[:], i["decay_cols"])])
                sp.wait_ge(got, n)

            @block.vector
            def _(dve):
                dve.memset(dmat[:], 1.0).then_inc(own, 1)
                dve.memset(cols[:, 6:7], DECAY ** P).then_inc(own, 1)
                dve.wait_ge(own, 2)
                dve.wait_ge(got, 13 * 16)
                for k in range(2):
                    ins = dve.tensor_scalar(dmat[:, k, :], dmat[:, k, :], tok_decay[:, k:k + 1], None, ALU.mult)
                ins.then_inc(own, 1)
        tiles = lambda x, s: x[:, ds(s * TILES, TILES)]
        with Stage(nc, "bi") as st:
            retention_inputs(nc, env, st, None, [
                (0, W["Wq"][:], "channels", cols[:, 0:1], None, lambda s: tiles(QK, s)[:, :, 0, :]),
                (0, W["Wk"][:], "channels", cols[:, 1:2], None, lambda s: tiles(QK, s)[:, :, 1, :]),
                (0, W["Wk"][:], "tokens", None, ACT.Copy, lambda s: tiles(KT, s)),
                (0, W["Wv"][:], "tokens", None, ACT.Copy, lambda s: tiles(V, s)),
            ])
            bias_done = st.sem("bias_done")
            with nc.Block() as block:
                @block.vector
                def _(dve):
                    for x, bias in ((KT, bk), (V, bv)):
                        dve.tensor_tensor(x[:], x[:], bias[:].unsqueeze(1).broadcast_to([P, B * TILES, D]),
                                          ALU.add).then_inc(bias_done, 1)
                    dve.wait_ge(bias_done, 2)
        OUT = sw.sb("OUT", [P, B * TILES, D])
        with Stage(nc, "br") as st:
            retention(nc, env, st, QK, KT, V, OUT, mask[:], dmat[:, 1, :], dmat[:, 0, :], cols[:, 6:7])
        with Stage(nc, "bo") as st:
            group_norm_out(nc, env, st, OUT, W["Wo"], cols)


def group_norm_out(nc, env, st, OUT, wo, cols):
    a = st.sb("a", [P, 2, T])
    aT = st.sb("aT", [P, 2, T])
    yT = st.sb("yT", [P, 2, T])
    stats = st.sb("stats", [P, 2, 2, 6])
    mv = st.sb("mv", [P, 2, 2])
    avg = st.sb("avg", [P, P])
    work = st.sb("work", [P, 2, 8])
    psT = st.ps("psT", [P, T])
    psY = st.ps("psY", [P, T])
    psZ = st.ps("psZ", [P, T])
    psM = st.ps("psM", [P, 2, 512])
    names = ("a_ready", "t1_ready", "aT_ready", "y_ready", "yT_ready", "stats_ready", "mean_ready", "dev_ready",
             "var_ready", "ve_ready", "rstd_ready", "affine_ready", "z_ready", "t2_ready", "added", "own")
    (a_ready, t1_ready, aT_ready, y_ready, yT_ready, stats_ready, mean_ready, dev_ready, var_ready, ve_ready,
     rstd_ready, affine_ready, z_ready, t2_ready, added, own) = (st.sem(n) for n in names)
    made = st.sem("made")
    with nc.Block() as block:
        @block.scalar
        def _(act):
            def project(s, u):
                act.activation(a[:, u, :], OUT[:, ds(s * TILES, TILES), :].rearrange("p j d -> p (j d)"), ACT.Copy).then_inc(a_ready, 1)
                act.wait_ge(t1_ready, s + 1)
                act.activation(aT[:, u, :], psT[:], ACT.Copy).then_inc(aT_ready, 1)
                act.wait_ge(y_ready, s + 1)
                act.activation(yT[:, u, :], psY[:], ACT.Identity, bias=cols[:, 2:3]).then_inc(yT_ready, 1)

            def body(s, u):
                act.wait_ge(affine_ready, s + 1)
                act.activation(yT[:, u, :], yT[:, u, :], ACT.Identity, bias=work[:, u, 5:6], scale=work[:, u, 4:5]).then_inc(z_ready, 1)
            loop_ahead(act, project, body)

        @block.tensor
        def _(pe):
            pe.wait_ge(made, 1)

            def project(s, u):
                pe.wait_ge(a_ready, s + 1)
                pe.wait_ge(aT_ready, s)
                for j in range(TILES):
                    ins = pe.transpose(psT[:, j * P:(j + 1) * P], a[:, u, j * P:(j + 1) * P], env.ident[:])
                ins.then_inc(t1_ready, 1)
                pe.wait_ge(aT_ready, s + 1)
                pe.wait_ge(yT_ready, s)
                for k in range(2):
                    ins = pe.matmul(psY[:, k * 512:(k + 1) * 512], wo[:], aT[:, u, k * 512:(k + 1) * 512], start=True, stop=True)
                ins.then_inc(y_ready, 1)

            def body(s, u):
                pe.wait_ge(stats_ready, s + 1)
                pe.matmul(psM[:, 0, 0:1], avg[:], mv[:, u, 0:1], start=True, stop=True).then_inc(mean_ready, 1)
                pe.wait_ge(dev_ready, s + 1)
                pe.matmul(psM[:, 1, 0:1], avg[:], work[:, u, 2:3], start=True, stop=True).then_inc(var_ready, 1)
                pe.wait_ge(z_ready, s + 1)
                pe.wait_ge(added, s)
                for j in range(TILES):
                    ins = pe.transpose(psZ[:, j * P:(j + 1) * P], yT[:, u, j * P:(j + 1) * P], env.ident[:])
                ins.then_inc(t2_ready, 1)
            loop_ahead(pe, project, body)

        @block.gpsimd
        def _(pool):
            def body(s, u):
                pool.wait_ge(ve_ready, s + 1)
                pool.tensor_tensor(work[:, u, 6:7], work[:, u, 3:4], env.minus_half[:, 0:1], ALU.pow).then_inc(rstd_ready, 1)
            loop_batches(pool, body)

        @block.vector
        def _(dve):
            dve.tensor_scalar(avg[:], env.blk2[:], 1.0 / HD, None, ALU.mult).then_inc(made, 1)
            ch = Chain(dve, own)

            def body(s, u):
                w = lambda k: work[:, u, k:k + 1]
                ch.start(s * 7)
                dve.wait_ge(yT_ready, s + 1)
                for k in range(2):
                    ins = dve.bn_stats(stats[:, u, k, :], yT[:, u, k * 512:(k + 1) * 512])
                ch(ins, alone=True)
                dve.bn_aggr(mv[:, u, :], stats[:, u].rearrange("p k n -> p (k n)")).then_inc(stats_ready, 1)
                dve.wait_ge(mean_ready, s + 1)
                ch(dve.tensor_copy(w(0), psM[:, 0, 0:1]))
                ch(dve.tensor_tensor(w(1), mv[:, u, 0:1], w(0), ALU.subtract))
                ch(dve.tensor_tensor(w(1), w(1), w(1), ALU.mult))
                dve.tensor_tensor(w(2), w(1), mv[:, u, 1:2], ALU.add).then_inc(dev_ready, 1)
                dve.wait_ge(var_ready, s + 1)
                dve.tensor_scalar(w(3), psM[:, 1, 0:1], LN_EPS, None, ALU.add).then_inc(ve_ready, 1)
                dve.wait_ge(rstd_ready, s + 1)
                ch(dve.tensor_tensor(w(4), w(6), cols[:, 3:4], ALU.mult))
                ch(dve.tensor_tensor(w(7), w(0), w(4), ALU.mult))
                ch(dve.tensor_tensor(w(5), cols[:, 4:5], w(7), ALU.subtract))
                dve.sem_inc(affine_ready, 1)
                dve.wait_ge(t2_ready, s + 1)
                xb = batch(env.X, s)
                dve.tensor_tensor(xb, psZ[:].rearrange("p (j d) -> p j d", d=D), xb, ALU.add).then_inc(added, 1)
            loop_batches(dve, body)


def masked_softmax_block(nc, env, i):
    QS = nc.dram_tensor("c_q_parts", [B, H, SPLITS, HD, T], BF16, kind="Internal").ap()
    KS = nc.dram_tensor("c_k_parts", [B, H, SPLITS, HD, T], BF16, kind="Internal").ap()
    LASTD = nc.dram_tensor("c_last", [B, H, T], F32, kind="Internal").ap()
    MASKD = nc.dram_tensor("c_mask", [HEADS, T], BF16, kind="Internal").ap()
    RANKED = T - RECENCY
    TAKE = K_KEEP - RECENCY
    ROUNDS, LEFT = TAKE // 8, TAKE % 8
    ABREAST = 4
    assert LEFT > 0 and ROUNDS % ABREAST == 0
    with Stage(nc, "c") as sw:
        w = sw.sb("w", [P, 3 * D])
        wo = sw.sb("wo", [P, D])
        got = sw.sem("got")
        with nc.Block() as block:
            @block.sync
            def _(sp):
                n = load(sp, got, [(w[:], i["L1_attn_a_W_attn"]), (wo[:], i["L1_attn_a_W_proj"])])
                sp.wait_ge(got, n)
        VTOK = sw.sb("vtok", [P, HEADS, TILES, HD + 1])
        ATT = sw.sb("att", [P, HEADS, TILES, HD])
        with Stage(nc, "cq") as st:
            qkv_stage(nc, env, st, QS, KS, VTOK, w, None, False, None, LASTD)
        with Stage(nc, "ck") as st:
            work = st.sb("work", [HEADS, T])
            top8 = st.sb("top8", [HEADS, 8])
            keep = st.sb("keep", [HEADS, T], BF16)
            loaded, own, stored = st.sem("loaded"), st.sem("own"), st.sem("stored")
            with nc.Block() as block:
                @block.sync
                def _(sp):
                    sp.dma_start(work[:], LASTD.rearrange("b h t -> (b h) t")).then_inc(loaded, 16)
                    sp.wait_ge(own, 2 * ROUNDS + 5)
                    sp.dma_start(MASKD, keep[:]).then_inc(stored, 16)
                    sp.wait_ge(stored, 16)

                @block.vector
                def _(dve):
                    dve.memset(keep[:], 0.0).then_inc(own, 1)
                    dve.wait_ge(loaded, 16)
                    r_work = work[:, 0:RANKED]
                    with dve.Fori(0, ROUNDS // ABREAST) as r:
                        for k in range(ABREAST):
                            n = (r * ABREAST + k) * 2
                            dve.max(top8[:], r_work).then_inc(own, 1)
                            wait_alone(dve, own, n + 2)
                            dve.match_replace(r_work, top8[:], r_work, TAKEN).then_inc(own, 1)
                            wait_alone(dve, own, n + 3)
                    ch = Chain(dve, own)
                    ch.start(2 * ROUNDS + 1)
                    ch(dve.max(top8[:], r_work))
                    ch(dve.memset(top8[:, LEFT:8], TAKEN))
                    ch(dve.match_replace(r_work, top8[:], r_work, TAKEN))
                    ch(dve.tensor_scalar(keep[:, 0:RANKED], r_work, TAKEN, MASKED, ALU.is_gt, ALU.mult))
        with Stage(nc, "ca") as st:
            env.recip_sem["ca"] = st.sem("recip")
            attention(nc, env, st, QS, KS, VTOK, ATT, 96 + 1, None, MASKD)
        with Stage(nc, "co") as st:
            add_projected(nc, env, st, Source(
                lambda s: ATT[:, ds(s * H, H), :, :].rearrange("p h j d -> p j h d"),
                "p (j h d) -> p j h d", j=TILES, h=H), wo, None)


def linear_weights(nc, env, i, main):
    env.lin_w = main.sb("lin_w", [P, D])
    env.lin_b = main.sb("lin_b", [P, D])
    with Stage(nc, "lw") as st:
        k = st.sb("k", [P, D])
        a, b = st.sb("a", [16, D]), st.sb("b", [16, D])
        mx = st.sb("mx", [P, 4])
        ps = st.ps("ps", [P, D])
        got, own, pown, ab_ready, mx_ready, q_ready = (st.sem(n) for n in ("got", "own", "pown", "ab_ready", "mx_ready", "q_ready"))
        with nc.Block() as block:
            @block.sync
            def _(sp):
                n = load(sp, got, [(k[:], i["L1_ffn_kernel"]), (a[:], i["lora_aT"]), (b[:], i["L1_ffn_b"]),
                                   (env.lin_b[:], i["L1_ffn_bias"].partition_broadcast(P))])
                sp.wait_ge(got, n)

            @block.tensor
            def _(pe):
                pe.wait_ge(got, 64)
                pe.matmul(ps[:], a[:], b[:], start=True, stop=True).then_inc(ab_ready, 1)

            @block.gpsimd
            def _(pool):
                pool.wait_ge(mx_ready, 1)
                ch = Chain(pool, pown)
                ch(pool.partition_all_reduce(mx[:, 1:2], mx[:, 0:1], P, bass.bass_isa.ReduceOp.max))
                pool.tensor_scalar(mx[:, 2:3], mx[:, 1:2], 1.0 / 7.0, None, ALU.mult).then_inc(q_ready, 1)

            @block.vector
            def _(dve):
                ch = Chain(dve, own)
                dve.wait_ge(got, 64)
                dve.tensor_reduce(mx[:, 0:1], k[:], AX.X, ALU.max, apply_absolute_value=True).then_inc(mx_ready, 1)
                dve.wait_ge(q_ready, 1)
                ch(dve.reciprocal(mx[:, 3:4], mx[:, 2:3]))
                ch(dve.tensor_scalar(k[:], k[:], mx[:, 3:4], None, ALU.mult))
                ch(dve.tensor_scalar(k[:], k[:], 12582912.0, None, ALU.add))
                ch(dve.tensor_scalar(k[:], k[:], 12582912.0, None, ALU.subtract))
                ch(dve.tensor_scalar(k[:], k[:], -8.0, 7.0, ALU.max, ALU.min))
                ch(dve.tensor_scalar(k[:], k[:], mx[:, 2:3], None, ALU.mult))
                dve.wait_ge(ab_ready, 1)
                ch(dve.tensor_tensor(env.lin_w[:], ps[:], k[:], ALU.add))


def linear_block(nc, env, name):
    with Stage(nc, name) as st:
        nm = Norm(st, env)
        psY = st.ps("psY", [P, T])
        y_ready, added, bias_done = st.sem("y_ready"), st.sem("added"), st.sem("bias_done")
        with nc.Block() as block:
            @block.vector
            def _(dve):
                nm.credits(dve)

                def body(s, u):
                    dve.wait_ge(y_ready, s + 1)
                    dve.wait_ge(bias_done, s + 1)
                    xb = batch(env.X, s)
                    dve.tensor_tensor(xb, psY[:].rearrange("p (j d) -> p j d", d=D), xb, ALU.add).then_inc(added, 1)
                loop_ahead(dve, lambda s, u: nm.vector(dve, s, u), body)

            @block.gpsimd
            def _(pool):
                def body(s, u):
                    nm.gpsimd(pool, s, u)
                    pool.wait_ge(nm.y_ready, s + 1)
                    xb = batch(env.X, s)
                    pool.tensor_tensor(xb, xb, env.lin_b[:].unsqueeze(1).broadcast_to([P, TILES, D]), ALU.add).then_inc(bias_done, 1)
                loop_batches(pool, body)

            @block.tensor
            def _(pe):
                def body(s, u):
                    pe.wait_ge(nm.xt_ready, s + 1)
                    pe.wait_ge(added, s)
                    for j in range(TILES):
                        ins = pe.matmul(psY[:, j * D:(j + 1) * D], nm.xT[:, u, j * P:(j + 1) * P], env.lin_w[:], start=True, stop=True)
                    ins.then_inc(y_ready, 1)
                loop_ahead(pe, lambda s, u: nm.tensor(pe, s, u), body)

            @block.scalar
            def _(act):
                def body(s, u):
                    act.wait_ge(y_ready, s + 1)
                    act.sem_inc(nm.xt_free, 1)
                loop_ahead(act, lambda s, u: nm.scalar(act, s, u), body)


def rwkv_block(nc, env, i):
    with Stage(nc, "r") as sw:
        W = {n: sw.sb(n, [P, D]) for n in ("WrT", "WkT", "WvT", "WgT", "WoT")}
        maa = sw.sb("maa", [P, 4])
        hd = sw.sb("hd", [P, 2, H])
        hc = sw.sb("hc", [P, 2])
        lag, later, steps = sw.sb("lag", [P, P]), sw.sb("later", [P, P]), sw.sb("steps", [P, 2])
        mask = sw.sb("mask", [P, H, P])
        dmat = sw.sb("dmat", [P, 2, H, HD])
        ln_w, ln_b = sw.sb("ln_w", [P, D]), sw.sb("ln_b", [P, D])
        QK = sw.sb("QK", [P, B * TILES, 2, P])
        KT = sw.sb("KT", [P, B * TILES, D])
        V = sw.sb("V", [P, B * TILES, D])
        G = sw.sb("G", [P, B * TILES, D])
        got, own, aown, e_ready, m_ready = (sw.sem(n) for n in ("got", "own", "aown", "e_ready", "m_ready"))
        bonus = sw.sb("bonus", [P, P])
        with nc.Block() as block:
            @block.sync
            def _(sp):
                n = load(sp, got, [(W[k][:], i[k]) for k in W]
                         + [(maa[:, n:n + 1], i[f"L1_attn_b_time_maa_{k}"].rearrange("a b c -> c (a b)"))
                            for n, k in enumerate(("r", "k", "v", "g"))]
                         + [(hd[:, 0, :], i["L1_attn_b_time_decay"].rearrange("h o -> (h o)").partition_broadcast(P)),
                            (hd[:, 1, :], i["L1_attn_b_time_faaaa"].rearrange("h o -> (h o)").partition_broadcast(P)),
                            (lag[:], i["lag"]), (later[:], i["later"]), (steps[:], i["steps"]),
                            (ln_w[:], i["L1_attn_b_ln_w"].partition_broadcast(P)),
                            (ln_b[:], i["L1_attn_b_ln_b"].partition_broadcast(P))])
                for h in range(H):
                    sp.dma_start(hc[h * HD:(h + 1) * HD, 0:1], i["L1_attn_b_time_decay"][h:h + 1, :].rearrange(
                        "a b -> (a b)").partition_broadcast(HD)).then_inc(got, 16)
                sp.wait_ge(got, n + 16 * H)

            ALL = 16 * (5 + 4 + 7 + H)

            @block.scalar
            def _(act):
                act.wait_ge(got, ALL)
                act.activation(hd[:, 0, :], hd[:, 0, :], ACT.Exp)
                act.activation(hc[:, 0:1], hc[:, 0:1], ACT.Exp).then_inc(e_ready, 1)
                act.wait_ge(m_ready, 1)
                act.activation(hc[:, 1:2], hc[:, 0:1], ACT.Exp, scale=float(P)).then_inc(aown, 1)
                for h in range(H):
                    act.activation(mask[:, h, :], lag[:], ACT.Exp, scale=hd[:, 0, h:h + 1]).then_inc(aown, 1)
                for k in range(2):
                    act.activation(dmat[:, k, :, 0], hd[:, 0, :], ACT.Exp, scale=steps[:, k:k + 1]).then_inc(aown, 1)
                act.wait_ge(aown, H + 3)
                for k in range(2):
                    for d in range(1, HD):
                        act.activation(dmat[:, k, :, d], dmat[:, k, :, 0], ACT.Copy).then_inc(aown, 1)

            @block.vector
            def _(dve):
                ch = Chain(dve, own)
                dve.wait_ge(e_ready, 1)
                ch(dve.tensor_scalar(hd[:, 0, :], hd[:, 0, :], 1.0e30, -1.0, ALU.min, ALU.mult))
                dve.tensor_scalar(hc[:, 0:1], hc[:, 0:1], 1.0e30, -1.0, ALU.min, ALU.mult).then_inc(m_ready, 1)
                dve.wait_ge(aown, H + 3)
                ch(dve.tensor_tensor(mask[:], mask[:], later[:].unsqueeze(1).broadcast_to([P, H, P]), ALU.mult))
                for h in range(H):
                    dve.scalar_tensor_tensor(mask[:, h, :], env.ident[:], hd[:, 1, h:h + 1], mask[:, h, :], ALU.mult,
                                             ALU.add).then_inc(own, 1)
                dve.wait_ge(own, H + 2)
        tiles = lambda x, s: x[:, ds(s * TILES, TILES)]
        with Stage(nc, "ri") as st:
            retention_inputs(nc, env, st, None, [
                (0, W["WrT"][:], "channels", None, ACT.Copy, lambda s: tiles(QK, s)[:, :, 0, :]),
                (1, W["WkT"][:], "channels", None, ACT.Copy, lambda s: tiles(QK, s)[:, :, 1, :]),
                (1, W["WkT"][:], "tokens", None, ACT.Copy, lambda s: tiles(KT, s)),
                (2, W["WvT"][:], "tokens", None, ACT.Copy, lambda s: tiles(V, s)),
                (3, W["WgT"][:], "tokens", None, ACT.Gelu, lambda s: tiles(G, s)),
            ], mixes=maa[:], pad=1)
        OUT = sw.sb("OUT", [P, B * TILES, D])
        with Stage(nc, "rr") as st:
            retention(nc, env, st, QK, KT, V, OUT, mask[:], dmat[:, 1].rearrange("p h d -> p (h d)"),
                      dmat[:, 0].rearrange("p h d -> p (h d)"), hc[:, 1:2])
        with Stage(nc, "rn") as st:
            head_norm_gate(nc, env, st, OUT, G, ln_w, ln_b)
        with Stage(nc, "ro") as st:
            add_projected(nc, env, st, Source(lambda s: OUT[:, ds(s * TILES, TILES), :], "p (j d) -> p j d", d=D), W["WoT"], None)


def head_norm_gate(nc, env, st, OUT, G, ln_w, ln_b):
    N = TILES * H
    y = st.sb("y", [P, 2, N, HD])
    sq = st.sb("sq", [P, 2, N, HD])
    s1, s2, root = st.sb("s1", [P, 2, N]), st.sb("s2", [P, 2, N]), st.sb("root", [P, 2, N])
    own, sq_ready, ve_ready, rstd_ready, n_ready, p_own, done = (
        st.sem(n) for n in ("own", "sq_ready", "ve_ready", "rstd_ready", "n_ready", "p_own", "done"))
    y_ready, y_free = st.sem("y_ready"), st.sem("y_free")
    with nc.Block() as block:
        @block.vector
        def _(dve):
            dve.sem_inc(y_free, 2)
            ch = Chain(dve, own)

            def body(s, u):
                ch.start(s * 8)
                o = OUT[:, ds(s * TILES, TILES), :].rearrange("p j (h d) -> p (j h) d", d=HD)
                dve.wait_ge(y_free, s + 1)
                ch(dve.tensor_reduce(s1[:, u, :], o, AX.X, ALU.add))
                ch(dve.tensor_scalar(s1[:, u, :], s1[:, u, :], 1.0 / HD, None, ALU.mult))
                dve.tensor_tensor(y[:, u], o, s1[:, u, :].unsqueeze(2).broadcast_to([P, N, HD]), ALU.subtract).then_inc(y_ready, 1)
                dve.wait_ge(sq_ready, s + 1)
                ch(dve.tensor_reduce(s2[:, u, :], sq[:, u], AX.X, ALU.add))
                dve.tensor_scalar(s2[:, u, :], s2[:, u, :], 1.0 / HD, RWKV_EPS, ALU.mult, ALU.add).then_inc(ve_ready, 1)
                dve.wait_ge(rstd_ready, s + 1)
                ch(dve.reciprocal(s1[:, u, :], root[:, u, :]))
                ch(dve.tensor_tensor(root[:, u, :], s1[:, u, :], s1[:, u, :], ALU.mult))
                ch(dve.tensor_tensor(root[:, u, :], root[:, u, :], s2[:, u, :], ALU.mult))
                ch(dve.tensor_scalar(root[:, u, :], root[:, u, :], -0.5, 1.5, ALU.mult, ALU.add))
                ch(dve.tensor_tensor(s1[:, u, :], s1[:, u, :], root[:, u, :], ALU.mult))
                dve.tensor_tensor(y[:, u], y[:, u], s1[:, u, :].unsqueeze(2).broadcast_to([P, N, HD]), ALU.mult).then_inc(n_ready, 1)
            loop_batches(dve, body)

        @block.scalar
        def _(act):
            def body(s, u):
                act.wait_ge(y_ready, s + 1)
                act.activation(sq[:, u], y[:, u], ACT.Square).then_inc(sq_ready, 1)
                act.wait_ge(ve_ready, s + 1)
                act.activation(root[:, u, :], s2[:, u, :], ACT.Sqrt).then_inc(rstd_ready, 1)
            loop_batches(act, body)

        @block.gpsimd
        def _(pool):
            ch = Chain(pool, p_own)

            def body(s, u):
                ch.start(s * 3)
                pool.wait_ge(n_ready, s + 1)
                v = y[:, u].rearrange("p (j h) d -> p j (h d)", h=H)
                ch(pool.tensor_tensor(v, v, ln_w[:].unsqueeze(1).broadcast_to([P, TILES, D]), ALU.mult))
                ch(pool.tensor_tensor(v, v, ln_b[:].unsqueeze(1).broadcast_to([P, TILES, D]), ALU.add))
                ch(pool.tensor_tensor(OUT[:, ds(s * TILES, TILES), :], v, G[:, ds(s * TILES, TILES), :], ALU.mult))
                pool.sem_inc(y_free, 1)
            loop_batches(pool, body)


def softmax_block_a(nc, env, i):
    QS = nc.dram_tensor("a_q_parts", [B, H, 2 * SPLITS, HD, T], BF16, kind="Internal").ap()
    KS = nc.dram_tensor("a_k_parts", [B, H, SPLITS, HD, T], BF16, kind="Internal").ap()
    KF = nc.dram_tensor("a_key_features", [SPLITS * HD, T], BF16, kind="Internal").ap()
    with Stage(nc, "aw") as sw:
        w = sw.sb("w", [P, 3 * D])
        wo = sw.sb("wo", [P, D])
        cols = sw.sb("cols", [P, 4])
        bv = sw.sb("bv", [P, D])
        bo = sw.sb("bo", [P, D])
        got = sw.sem("got")
        with nc.Block() as block:
            @block.sync
            def _(sp):
                bq = i["L0_attn_a_b_qkv"]
                n = load(sp, got, [(w[:], i["L0_attn_a_w_qkv"]), (wo[:], i["L0_attn_a_w_out"]),
                                   (cols[:, 0:1], column(bq[0:D])), (cols[:, 1:2], column(bq[D:2 * D])),
                                   (cols[:, 2:3], column(i["L0_attn_a_ln_g"])), (cols[:, 3:4], column(i["L0_attn_a_ln_b"])),
                                   (bv[:], bq[2 * D:3 * D].partition_broadcast(P)),
                                   (bo[:], i["L0_attn_a_b_out"].partition_broadcast(P))])
                sp.wait_ge(got, n)
        VTOK = sw.sb("vtok", [P, HEADS, TILES, HD + 1])
        ATT = sw.sb("att", [P, HEADS, TILES, HD])
        with Stage(nc, "ar") as sr:
            stored, n_stored = relative_features(nc, env, sr, i["L0_attn_a_w_rel"], QS, KF)
            with Stage(nc, "aq") as st:
                qkv_stage(nc, env, st, QS[:, :, 0:SPLITS], KS, VTOK, w, (cols[:, 0:1], cols[:, 1:2], bv[:]), True,
                          (cols[:, 2:3], cols[:, 3:4]))
            with nc.Block() as block:
                @block.sync
                def _(sp):
                    sp.wait_ge(stored, n_stored)
        with Stage(nc, "aa") as st:
            env.recip_sem["aa"] = st.sem("recip")
            attention(nc, env, st, QS, KS, VTOK, ATT, 2 * SPLITS * HD, KF)
        with Stage(nc, "ao") as st:
            add_projected(nc, env, st, Source(
                lambda s: ATT[:, ds(s * H, H), :, :].rearrange("p h j d -> p j h d"),
                "p (j h d) -> p j h d", j=TILES, h=H), wo, bo)


def laid_out(inputs):
    out = {name: np.asarray(a) for name, a in inputs.items()}
    out["b1_cols"] = out.pop("L0_ffn_b1").reshape(EXPERTS, HK, P).transpose(0, 2, 1)
    out["router_wT"] = out.pop("L0_ffn_router_w").T
    out["lora_aT"] = out.pop("L1_ffn_a").T
    for n in ("Wr", "Wk", "Wv", "Wg", "Wo"):
        out[f"{n}T"] = out.pop(f"L1_attn_b_{n}").T
    return out




def kernel(**inputs):
    import numpy as _np
    import concourse.bacc as _bacc
    from concourse import mybir as _mybir
    from concourse.bass_utils import run_bass_kernel_spmd as _run

    nc = _bacc.Bacc("TRN2", target_bir_lowering=False, num_devices=1)
    arrays, args = {}, {}
    for name, a in {**laid_out(inputs), **constants()}.items():
        a = _np.ascontiguousarray(a)
        arrays[f"in_{name}"] = a
        args[name] = nc.dram_tensor(f"in_{name}", a.shape, _mybir.dt.from_np(a.dtype), kind="ExternalInput").ap()
    out = nc.dram_tensor("out_0", (B, T, D), _mybir.dt.float32, kind="ExternalOutput").ap()
    build(nc, args, out)
    r = _run(nc, [arrays], core_ids=[0])
    return r.results[0]["out_0"]
```
